# Optimizing a Trainium2 kernel written in Bass

```python
import numpy as np
import jax
import jax.numpy as jnp

def _softmax(x, axis=-1):
    return jax.nn.softmax(x, axis=axis)

def _gelu(x):
    return jax.nn.gelu(x, approximate=True)

def _silu(x):
    return jax.nn.silu(x)

def _sigmoid(x):
    return jax.nn.sigmoid(x)

def _layernorm(x, axis=-1, eps=1e-05):
    m = jnp.mean(x, axis=axis, keepdims=True)
    v = jnp.var(x, axis=axis, keepdims=True)
    return (x - m) / jnp.sqrt(v + eps)

def _scatter_add(tgt, idx, src, axis=0):
    return tgt.at[idx].add(src)

def _segment_sum(src, seg, n):
    return jax.ops.segment_sum(src, seg, n)
kernel_name = 'mk_conv_attn_hybrid_d4_conv_nchw256_r2_570b21'

def setup_inputs(seed: int=0):
    np.random.seed(seed)
    _w = jnp.asarray

    def _rec_inputs():
        import jax
        import jax.numpy as jnp
        _gk = jax.random.key(seed)
        x = -0.0002928 + 1 * jax.random.normal(jax.random.fold_in(_gk, 1), (4, 128, 32, 32), jnp.float32)
        return x
    x = _rec_inputs()

    def _L0_conv_setup():
        import jax, jax.numpy as jnp
        import numpy as np
        B, CIN, COUT, H, W = (4, 128, 128, 32, 32)
        key = jax.random.key(seed)
        ks = jax.random.split(key, 7)
        x = jax.random.normal(ks[0], (B, CIN, H, W), dtype=jnp.float32)
        s = 1.0 / np.sqrt(CIN)
        Wq = jax.random.uniform(ks[1], (COUT, CIN), jnp.float32, -s, s)
        Wk = jax.random.uniform(ks[2], (COUT, CIN), jnp.float32, -s, s)
        Wv = jax.random.uniform(ks[3], (COUT, CIN), jnp.float32, -s, s)
        bq = jax.random.uniform(ks[4], (COUT,), jnp.float32, -s, s)
        bk = jax.random.uniform(ks[5], (COUT,), jnp.float32, -s, s)
        bv = jax.random.uniform(ks[6], (COUT,), jnp.float32, -s, s)
        return {'x': x, 'Wq': Wq, 'Wk': Wk, 'Wv': Wv, 'bq': bq, 'bk': bk, 'bv': bv}
    _L0_conv_all = _L0_conv_setup()
    _L0_conv_in = {k: v for k, v in _L0_conv_all.items() if k in ('Wq', 'Wk', 'Wv', 'bq', 'bk', 'bv')}
    del _L0_conv_all

    def _L1_conv_setup():
        import jax, jax.numpy as jnp
        import numpy as np
        from functools import partial
        DIM = 128
        HEADS = 8
        HEAD_DIM = DIM // HEADS
        SCALES = (1, 2, 4)
        B, H, W = (1, 32, 32)

        def _dwconv3x3(x, w, b):
            y = jax.lax.conv_general_dilated(x, w, window_strides=(1, 1), padding='SAME', feature_group_count=x.shape[1], dimension_numbers=('NCHW', 'OIHW', 'NCHW'))
            return y + b[None, :, None, None]

        def _pwconv(x, w, b):
            return jnp.einsum('bchw,oc->bohw', x, w) + b[None, :, None, None]

        def _avg_pool(x, s):
            Bb, C, Hh, Ww = x.shape
            return x.reshape(Bb, C, Hh // s, s, Ww // s, s).mean(axis=(3, 5))
        key = jax.random.key(seed)
        ks = jax.random.split(key, 9)
        sc = 0.05
        return {'x': jax.random.normal(ks[0], (B, DIM, H, W), dtype=jnp.float32), 'dw_w': jax.random.normal(ks[1], (3, DIM, 1, 3, 3), dtype=jnp.float32) * sc, 'dw_b': jax.random.normal(ks[2], (3, DIM), dtype=jnp.float32) * sc, 'pw_w': jax.random.normal(ks[3], (3, 3 * DIM, DIM), dtype=jnp.float32) * sc, 'pw_b': jax.random.normal(ks[4], (3, 3 * DIM), dtype=jnp.float32) * sc, 'pos_w': jax.random.normal(ks[5], (3, DIM, 1, 3, 3), dtype=jnp.float32) * sc, 'pos_b': jax.random.normal(ks[6], (3, DIM), dtype=jnp.float32) * sc, 'fusion_w': jax.random.normal(ks[7], (DIM, 3 * DIM), dtype=jnp.float32) * sc, 'fusion_b': jax.random.normal(ks[8], (DIM,), dtype=jnp.float32) * sc}
    _L1_conv_all = _L1_conv_setup()
    _L1_conv_in = {k: v for k, v in _L1_conv_all.items() if k in ('dw_w', 'dw_b', 'pw_w', 'pw_b', 'pos_w', 'pos_b', 'fusion_w', 'fusion_b')}
    del _L1_conv_all

    def _L2_attn_setup():
        import jax, jax.numpy as jnp
        import numpy as np
        EPS = 1e-09
        key = jax.random.key(seed)
        kE, kQ, kK, kV = jax.random.split(key, 4)
        B, S, D = (8, 1024, 128)
        return {'E': jax.random.normal(kE, (B, S, D), dtype=jnp.float32), 'WQ': jax.random.normal(kQ, (D, D), dtype=jnp.float32) * (1.0 / np.sqrt(D)), 'WK': jax.random.normal(kK, (D, D), dtype=jnp.float32) * (1.0 / np.sqrt(D)), 'WV': jax.random.normal(kV, (D, D), dtype=jnp.float32) * (1.0 / np.sqrt(D))}
    _L2_attn_all = _L2_attn_setup()
    _L2_attn_in = {k: v for k, v in _L2_attn_all.items() if k in ('WQ', 'WK', 'WV')}
    del _L2_attn_all

    def _L2_ffn_setup():
        import jax, jax.numpy as jnp
        import numpy as np
        D_MODEL = 128
        N_EXPERTS = 16
        HIDDEN = 256
        SCALE = 0.02
        key = jax.random.key(seed)
        ks = jax.random.split(key, 5)
        x = jax.random.normal(ks[0], (4, 4096, D_MODEL), dtype=jnp.float32)
        gate_w = jax.random.normal(ks[1], (D_MODEL, N_EXPERTS), dtype=jnp.float32) * SCALE
        gate_b = jnp.zeros((N_EXPERTS,), dtype=jnp.float32)
        w1 = jax.random.normal(ks[2], (N_EXPERTS, D_MODEL, HIDDEN), dtype=jnp.float32) * SCALE
        w2 = jax.random.normal(ks[3], (N_EXPERTS, D_MODEL, HIDDEN), dtype=jnp.float32) * SCALE
        w3 = jax.random.normal(ks[4], (N_EXPERTS, HIDDEN, D_MODEL), dtype=jnp.float32) * SCALE
        return {'x': x, 'gate_w': gate_w, 'gate_b': gate_b, 'w1': w1, 'w2': w2, 'w3': w3}
    _L2_ffn_all = _L2_ffn_setup()
    _L2_ffn_in = {k: v for k, v in _L2_ffn_all.items() if k in ('gate_w', 'gate_b', 'w1', 'w2', 'w3')}
    del _L2_ffn_all

    def _L3_attn_setup():
        import jax, jax.numpy as jnp
        import numpy as np
        H = 8
        key = jax.random.key(seed)
        ks = jax.random.split(key, 10)
        B, N, D, E = (1, 2048, 128, 32768)
        s = 0.02
        return {'x': jax.random.normal(ks[0], (B, N, D), jnp.float32), 'edge_index': jax.random.randint(ks[1], (2, E), 0, N, jnp.int32), 'edge_attr': jax.random.normal(ks[2], (E, 3), jnp.float32), 'Wq': jax.random.normal(ks[3], (D, D), jnp.float32) * s, 'bq': jnp.zeros((D,), jnp.float32), 'Wk': jax.random.normal(ks[4], (D, D), jnp.float32) * s, 'bk': jnp.zeros((D,), jnp.float32), 'Wv': jax.random.normal(ks[5], (D, D), jnp.float32) * s, 'bv': jnp.zeros((D,), jnp.float32), 'Wo': jax.random.normal(ks[6], (D, D), jnp.float32) * s, 'bo': jnp.zeros((D,), jnp.float32), 'We': jax.random.normal(ks[7], (3, H), jnp.float32) * s, 'be': jnp.zeros((H,), jnp.float32)}
    _L3_attn_all = _L3_attn_setup()
    _L3_attn_in = {k: v for k, v in _L3_attn_all.items() if k in ('edge_index', 'edge_attr', 'Wq', 'bq', 'Wk', 'bk', 'Wv', 'bv', 'Wo', 'bo', 'We', 'be')}
    del _L3_attn_all

    def _L3_ffn_setup():
        import jax, jax.numpy as jnp
        import numpy as np
        NUM_EXPERTS = 8
        TOP_K = 2
        B, S, D = (8, 4096, 128)

        def _moe(tokens, router_w, w1, b1, w2, b2):
            N = tokens.shape[0]
            E = router_w.shape[0]
            logits = tokens.astype(jnp.float32) @ router_w.astype(jnp.float32).T
            probs = jax.nn.softmax(logits, axis=-1)
            rw, re = jax.lax.top_k(probs, TOP_K)
            if TOP_K > 1:
                rw = rw / jnp.maximum(rw.sum(-1, keepdims=True), 1e-12)
            rw = rw.astype(tokens.dtype)
            combine = jnp.zeros((N, E), tokens.dtype).at[jnp.arange(N)[:, None], re].set(rw)
            out = tokens
            for e in range(E):
                h = jax.nn.gelu(tokens @ w1[e] + b1[e], approximate=False)
                y = h @ w2[e] + b2[e]
                out = out + combine[:, e:e + 1] * y
            return out
        key = jax.random.key(seed)
        ks = jax.random.split(key, 4)
        scale = 1.0 / np.sqrt(D).astype(np.float32)
        return {'input_embeddings': jax.random.normal(ks[0], (B, S, D), jnp.float32), 'router_w': jax.random.normal(ks[1], (NUM_EXPERTS, D), jnp.float32) * scale, 'w1': jax.random.normal(ks[2], (NUM_EXPERTS, D, D), jnp.float32) * scale, 'b1': jnp.zeros((NUM_EXPERTS, D), jnp.float32), 'w2': jax.random.normal(ks[3], (NUM_EXPERTS, D, D), jnp.float32) * scale, 'b2': jnp.zeros((NUM_EXPERTS, D), jnp.float32)}
    _L3_ffn_all = _L3_ffn_setup()
    _L3_ffn_in = {k: v for k, v in _L3_ffn_all.items() if k in ('router_w', 'w1', 'b1', 'w2', 'b2')}
    del _L3_ffn_all
    return {'x': x, 'L0_conv_Wq': _L0_conv_in['Wq'], 'L0_conv_Wk': _L0_conv_in['Wk'], 'L0_conv_Wv': _L0_conv_in['Wv'], 'L0_conv_bq': _L0_conv_in['bq'], 'L0_conv_bk': _L0_conv_in['bk'], 'L0_conv_bv': _L0_conv_in['bv'], 'L1_conv_dw_w': _L1_conv_in['dw_w'], 'L1_conv_dw_b': _L1_conv_in['dw_b'], 'L1_conv_pw_w': _L1_conv_in['pw_w'], 'L1_conv_pw_b': _L1_conv_in['pw_b'], 'L1_conv_pos_w': _L1_conv_in['pos_w'], 'L1_conv_pos_b': _L1_conv_in['pos_b'], 'L1_conv_fusion_w': _L1_conv_in['fusion_w'], 'L1_conv_fusion_b': _L1_conv_in['fusion_b'], 'L2_attn_WQ': _L2_attn_in['WQ'], 'L2_attn_WK': _L2_attn_in['WK'], 'L2_attn_WV': _L2_attn_in['WV'], 'L2_ffn_gate_w': _L2_ffn_in['gate_w'], 'L2_ffn_gate_b': _L2_ffn_in['gate_b'], 'L2_ffn_w1': _L2_ffn_in['w1'], 'L2_ffn_w2': _L2_ffn_in['w2'], 'L2_ffn_w3': _L2_ffn_in['w3'], 'L3_attn_edge_index': _L3_attn_in['edge_index'], 'L3_attn_edge_attr': _L3_attn_in['edge_attr'], 'L3_attn_Wq': _L3_attn_in['Wq'], 'L3_attn_bq': _L3_attn_in['bq'], 'L3_attn_Wk': _L3_attn_in['Wk'], 'L3_attn_bk': _L3_attn_in['bk'], 'L3_attn_Wv': _L3_attn_in['Wv'], 'L3_attn_bv': _L3_attn_in['bv'], 'L3_attn_Wo': _L3_attn_in['Wo'], 'L3_attn_bo': _L3_attn_in['bo'], 'L3_attn_We': _L3_attn_in['We'], 'L3_attn_be': _L3_attn_in['be'], 'L3_ffn_router_w': _L3_ffn_in['router_w'], 'L3_ffn_w1': _L3_ffn_in['w1'], 'L3_ffn_b1': _L3_ffn_in['b1'], 'L3_ffn_w2': _L3_ffn_in['w2'], 'L3_ffn_b2': _L3_ffn_in['b2']}

def reference(x, L0_conv_Wq, L0_conv_Wk, L0_conv_Wv, L0_conv_bq, L0_conv_bk, L0_conv_bv, L1_conv_dw_w, L1_conv_dw_b, L1_conv_pw_w, L1_conv_pw_b, L1_conv_pos_w, L1_conv_pos_b, L1_conv_fusion_w, L1_conv_fusion_b, L2_attn_WQ, L2_attn_WK, L2_attn_WV, L2_ffn_gate_w, L2_ffn_gate_b, L2_ffn_w1, L2_ffn_w2, L2_ffn_w3, L3_attn_edge_index, L3_attn_edge_attr, L3_attn_Wq, L3_attn_bq, L3_attn_Wk, L3_attn_bk, L3_attn_Wv, L3_attn_bv, L3_attn_Wo, L3_attn_bo, L3_attn_We, L3_attn_be, L3_ffn_router_w, L3_ffn_w1, L3_ffn_b1, L3_ffn_w2, L3_ffn_b2):
    import jax
    import jax.numpy as jnp

    def _L0_conv_ref(x, Wq, Wk, Wv, bq, bk, bv):
        import jax, jax.numpy as jnp
        import numpy as np
        B, CIN, COUT, H, W = (4, 128, 128, 32, 32)
        b, cin, h, w = x.shape
        xf = x.reshape(b, cin, h * w)
        q = jnp.einsum('oc,bcn->bon', Wq, xf) + bq[None, :, None]
        k = jnp.einsum('oc,bcn->bon', Wk, xf) + bk[None, :, None]
        v = jnp.einsum('oc,bcn->bon', Wv, xf) + bv[None, :, None]
        scores = jnp.einsum('bcn,bcm->bnm', q, k)
        attn = jax.nn.softmax(scores, axis=-1)
        out = jnp.einsum('bnm,bcm->bcn', attn, v)
        return out.reshape(b, q.shape[1], h, w)

    def _L1_conv_ref(x, dw_w, dw_b, pw_w, pw_b, pos_w, pos_b, fusion_w, fusion_b):
        import jax, jax.numpy as jnp
        import numpy as np
        from functools import partial
        DIM = 128
        HEADS = 8
        HEAD_DIM = DIM // HEADS
        SCALES = (1, 2, 4)
        B, H, W = (1, 32, 32)

        def _dwconv3x3(x, w, b):
            y = jax.lax.conv_general_dilated(x, w, window_strides=(1, 1), padding='SAME', feature_group_count=x.shape[1], dimension_numbers=('NCHW', 'OIHW', 'NCHW'))
            return y + b[None, :, None, None]

        def _pwconv(x, w, b):
            return jnp.einsum('bchw,oc->bohw', x, w) + b[None, :, None, None]

        def _avg_pool(x, s):
            Bb, C, Hh, Ww = x.shape
            return x.reshape(Bb, C, Hh // s, s, Ww // s, s).mean(axis=(3, 5))
        Bb, C, Hh, Ww = x.shape
        outputs = []
        for i, scale in enumerate(SCALES):
            xs = _avg_pool(x, scale) if scale > 1 else x
            x_dw = _dwconv3x3(xs, dw_w[i], dw_b[i])
            qkv = _pwconv(x_dw, pw_w[i], pw_b[i])
            q, k, v = jnp.split(qkv, 3, axis=1)
            pos = _dwconv3x3(xs, pos_w[i], pos_b[i])
            q = q + pos
            k = k + pos
            Hs, Ws = (xs.shape[2], xs.shape[3])
            Ns = Hs * Ws
            q = q.reshape(Bb, HEADS, HEAD_DIM, Ns)
            k = k.reshape(Bb, HEADS, HEAD_DIM, Ns)
            v = v.reshape(Bb, HEADS, HEAD_DIM, Ns)
            attn = jnp.einsum('bhdn,bhdm->bhnm', q, k) / HEAD_DIM ** 0.5
            attn = jax.nn.softmax(attn, axis=-1)
            out = jnp.einsum('bhnm,bhdm->bhdn', attn, v)
            out = out.reshape(Bb, C, Hs, Ws)
            if scale > 1:
                out = jax.image.resize(out, (Bb, C, Hh, Ww), method='bilinear')
            outputs.append(out)
        cat = jnp.concatenate(outputs, axis=1)
        return jnp.einsum('bchw,oc->bohw', cat, fusion_w) + fusion_b[None, :, None, None]

    def _L2_attn_ref(E, WQ, WK, WV):
        import jax, jax.numpy as jnp
        import numpy as np
        EPS = 1e-09
        D = E.shape[-1]
        scale = jnp.asarray(np.sqrt(D), dtype=E.dtype)
        Q = jnp.einsum('bsd,ed->bse', E, WQ)
        K = jnp.einsum('bsd,ed->bse', E, WK)
        V = jnp.einsum('bsd,ed->bse', E, WV)
        W = jnp.einsum('bqd,bkd->bqk', Q, K) / scale
        S_len = W.shape[-1]
        tril = jnp.tril(jnp.ones((S_len, S_len), dtype=W.dtype))
        M = jnp.where(W == 0, jnp.zeros_like(W), tril[None, :, :])
        x_max = jnp.max(W, axis=-1, keepdims=True)
        x_exp = jnp.exp(W - x_max) * M
        A = x_exp / (jnp.sum(x_exp, axis=-1, keepdims=True) + EPS)
        return jnp.einsum('bqk,bkd->bqd', A, V)

    def _L2_ffn_ref(x, gate_w, gate_b, w1, w2, w3):
        import jax, jax.numpy as jnp
        import numpy as np
        D_MODEL = 128
        N_EXPERTS = 16
        HIDDEN = 256
        SCALE = 0.02
        n_experts = w1.shape[0]
        logits = jnp.einsum('bsd,de->bse', x, gate_w) + gate_b
        probs = jax.nn.softmax(logits, axis=-1)
        top_probs, top_idx = jax.lax.top_k(probs, 2)
        top_probs = top_probs / jnp.sum(top_probs, axis=-1, keepdims=True)
        dispatch = jnp.sum(jax.nn.one_hot(top_idx, n_experts, dtype=x.dtype) * top_probs[..., None], axis=-2)
        h1 = jnp.einsum('bsd,edh->bseh', x, w1)
        h2 = jnp.einsum('bsd,edh->bseh', x, w2)
        hidden = jax.nn.silu(h1) * h2
        expert_out = jnp.einsum('bseh,eho->bseo', hidden, w3)
        return jnp.einsum('bseo,bse->bso', expert_out, dispatch)

    def _L3_attn_ref(x, edge_index, edge_attr, Wq, bq, Wk, bk, Wv, bv, Wo, bo, We, be):
        import jax, jax.numpy as jnp
        import numpy as np
        H = 8
        B, N, D = x.shape
        hd = D // H
        q = (x @ Wq + bq).reshape(B, N, H, hd)
        k = (x @ Wk + bk).reshape(B, N, H, hd)
        v = (x @ Wv + bv).reshape(B, N, H, hd)
        scores = jnp.einsum('bihd,bjhd->bhij', q, k) / jnp.sqrt(jnp.asarray(hd, x.dtype))
        eb = edge_attr @ We + be
        edge_tgt = edge_index[1]
        col_bias = jnp.zeros((H, N), x.dtype).at[:, edge_tgt].set(eb.T)
        scores = scores + col_bias[None, :, None, :]
        attn = jax.nn.softmax(scores, axis=-1)
        out = jnp.einsum('bhij,bjhd->bihd', attn, v).reshape(B, N, D)
        return out @ Wo + bo

    def _L3_ffn_ref(input_embeddings, router_w, w1, b1, w2, b2):
        import jax, jax.numpy as jnp
        import numpy as np
        NUM_EXPERTS = 8
        TOP_K = 2
        B, S, D = (8, 4096, 128)

        def _moe(tokens, router_w, w1, b1, w2, b2):
            N = tokens.shape[0]
            E = router_w.shape[0]
            logits = tokens.astype(jnp.float32) @ router_w.astype(jnp.float32).T
            probs = jax.nn.softmax(logits, axis=-1)
            rw, re = jax.lax.top_k(probs, TOP_K)
            if TOP_K > 1:
                rw = rw / jnp.maximum(rw.sum(-1, keepdims=True), 1e-12)
            rw = rw.astype(tokens.dtype)
            combine = jnp.zeros((N, E), tokens.dtype).at[jnp.arange(N)[:, None], re].set(rw)
            out = tokens
            for e in range(E):
                h = jax.nn.gelu(tokens @ w1[e] + b1[e], approximate=False)
                y = h @ w2[e] + b2[e]
                out = out + combine[:, e:e + 1] * y
            return out
        b, s, d = input_embeddings.shape
        tokens = input_embeddings.reshape(b * s, d)
        return _moe(tokens, router_w, w1, b1, w2, b2).reshape(b, s, d)

    def _gn(v, G=32, eps=1e-05):
        B_, C_, H_, W_ = v.shape
        g = v.reshape(B_, G, C_ // G, H_, W_)
        m = jnp.mean(g, axis=(2, 3, 4), keepdims=True)
        s = jnp.var(g, axis=(2, 3, 4), keepdims=True)
        return ((g - m) / jnp.sqrt(s + eps)).reshape(v.shape)

    def _ln_c(v, eps=1e-06):
        m = jnp.mean(v, axis=1, keepdims=True)
        s = jnp.var(v, axis=1, keepdims=True)
        return (v - m) / jnp.sqrt(s + eps)

    def _ln_t(v, eps=1e-05):
        m = jnp.mean(v, axis=-1, keepdims=True)
        s = jnp.var(v, axis=-1, keepdims=True)
        return (v - m) / jnp.sqrt(s + eps)

    def _to_tokens(v):
        B_, C_, H_, W_ = v.shape
        return v.reshape(B_, C_, H_ * W_).transpose(0, 2, 1)

    def _from_tokens(t, like):
        B_, C_, H_, W_ = like.shape
        return t.transpose(0, 2, 1).reshape(B_, C_, H_, W_)
    x = x + _L0_conv_ref(_gn(x), L0_conv_Wq, L0_conv_Wk, L0_conv_Wv, L0_conv_bq, L0_conv_bk, L0_conv_bv)
    x = x + _L1_conv_ref(_gn(x), L1_conv_dw_w, L1_conv_dw_b, L1_conv_pw_w, L1_conv_pw_b, L1_conv_pos_w, L1_conv_pos_b, L1_conv_fusion_w, L1_conv_fusion_b)
    t = _to_tokens(x)
    t = t + _L2_attn_ref(_ln_t(t), L2_attn_WQ, L2_attn_WK, L2_attn_WV)
    t = t + _L2_ffn_ref(_ln_t(t), L2_ffn_gate_w, L2_ffn_gate_b, L2_ffn_w1, L2_ffn_w2, L2_ffn_w3)
    t = t + _L3_attn_ref(_ln_t(t), L3_attn_edge_index, L3_attn_edge_attr, L3_attn_Wq, L3_attn_bq, L3_attn_Wk, L3_attn_bk, L3_attn_Wv, L3_attn_bv, L3_attn_Wo, L3_attn_bo, L3_attn_We, L3_attn_be)
    t = t + _L3_ffn_ref(_ln_t(t), L3_ffn_router_w, L3_ffn_w1, L3_ffn_b1, L3_ffn_w2, L3_ffn_b2)
    x = _from_tokens(t, x)
    return x

_drawn_inputs = setup_inputs


def setup_inputs(seed=0):
    import zlib

    import numpy as np

    out = dict(_drawn_inputs(seed))
    spreads = {'L2_ffn_gate_b': (0.0, 0.653),
     'L3_attn_bq': (0.0, 0.8),
     'L3_attn_bk': (0.0, 0.8),
     'L3_attn_bv': (0.0, 0.299),
     'L3_attn_bo': (0.0, 0.1),
     'L3_attn_be': (0.0, 0.8),
     'L3_ffn_b1': (0.0, 0.346),
     'L3_ffn_b2': (0.0, 0.1)}
    factors = {'L0_conv_bk': 8.0,
     'L1_conv_dw_w': 4.069,
     'L1_conv_pos_w': 8.0,
     'L1_conv_pos_b': 8.0,
     'L2_ffn_gate_w': 4.756,
     'L2_ffn_w1': 4.257,
     'L2_ffn_w2': 4.137,
     'L2_ffn_w3': 4.182,
     'L3_attn_edge_attr': 8.0,
     'L3_attn_Wq': 8.0,
     'L3_attn_Wk': 8.0,
     'L3_attn_Wv': 3.55,
     'L3_attn_We': 8.0}
    for name, (base, spread) in spreads.items():
        noise = np.random.default_rng([zlib.crc32(name.encode()), seed]).standard_normal(out[name].shape)
        drawn = base * np.exp(spread * noise) if base else spread * noise
        out[name] = jnp.asarray(drawn.astype(out[name].dtype))
    for name, factor in factors.items():
        out[name] = (out[name] * factor).astype(out[name].dtype)
    return out
```

```python
import struct
from contextlib import ExitStack

import concourse.bass as bass
from concourse import mybir

F32 = mybir.dt.float32
BF16 = mybir.dt.bfloat16
U16 = mybir.dt.uint16
U32 = mybir.dt.uint32
I32 = mybir.dt.int32
ALU = mybir.AluOpType
ACT = mybir.ActivationFunctionType
AX = mybir.AxisListType

P = 128
B, C, H, W = 4, 128, 32, 32
N = H * W
TILES = B * N // P
HEADS, HD = 8, 16
SLOT = 32
Q_PART = (0, 0, 1, 1, 0, 2)
K_PART = (0, 1, 0, 1, 2, 0)
STACK = len(Q_PART) * HD
TWO_ONES = struct.unpack("<f", struct.pack("<I", 0x3F803F80))[0]


class Stage(ExitStack):

    def __init__(self, nc):
        super().__init__()
        self.nc, self.sems = nc, []

    def semaphore(self, name):
        self.sems.append(self.nc.alloc_semaphore(name))
        return self.sems[-1]

    def __exit__(self, *what):
        done = super().__exit__(*what)
        for sem in self.sems:
            self.nc.gpsimd.sem_clear(sem)
            self.nc.release_semaphore(sem)
        return done


class Chain:

    def __init__(self, eng, sem, base=0):
        self.eng, self.sem, self.base, self.n = eng, sem, base, 0

    def __call__(self, ins):
        self.n += 1
        ins.then_inc(self.sem, 1)
        self.eng.wait_ge(self.sem, self.base + self.n)


def hold(eng, sem, value, held):
    eng.wait_ge(sem, value)
    eng.sem_inc(held, 1)


def flat(ap):
    return ap.rearrange("p a b -> p (a b)")


def at(t, i):
    if len(t.shape) == 3:
        return t[:, bass.ds(i, 1), :].rearrange("p o n -> p (o n)")
    return t[:, bass.ds(i, 1), :, :].rearrange("p o a n -> p (o a) n")


class Machine:

    def __init__(self, nc, ctx, ins):
        self.nc, self.ctx, self.ins = nc, ctx, ins
        self.xc = self.sb("x_channels", [P, B, N], F32)
        self.tt = self.xc[:].rearrange("p b (t c) -> p (b t) c", c=C)
        self.xnT = self.sb("normalised_channels", [P, B, N], F32)
        self.ident = self.sb("ident", [P, P], F32)
        self.identb = self.sb("identb", [P, P], BF16)
        self.sums_out, self.sums_in, self.inverse_out, self.inverse_in, self.gathered = (
            nc.alloc_semaphore(x) for x in ("sums_out", "sums_in", "inverse_out", "inverse_in", "gathered"))
        self.rounds = 0

    def sb(self, name, shape, dt, ctx=None):
        return (ctx or self.ctx).enter_context(self.nc.sbuf_tensor(name, shape, dt))

    def psum(self, name, shape, ctx):
        return ctx.enter_context(self.nc.psum_tensor(f"{name}_bank", shape, F32))

    def sem(self, name, ctx):
        return ctx.semaphore(name)


def make_identities(m):
    nc = m.nc
    with Stage(nc) as ctx:
        zeroed, made, loaded = (m.sem(f"i_{x}", ctx) for x in ("zeroed", "made", "loaded"))
        block = ctx.enter_context(nc.Block())

        @block.sync
        def _(sp):
            sp.dma_start(m.xc[:], m.ins["x"].rearrange("b c h w -> c b (h w)")).then_inc(loaded, 16)
            sp.wait_ge(loaded, 16)

        @block.gpsimd
        def _(pool):
            pool.memset(m.ident[:], 0.0).then_inc(zeroed, 1)
            pool.memset(m.identb[:], 0.0).then_inc(zeroed, 1)
            pool.wait_ge(zeroed, 2)
            for one in (m.ident, m.identb):
                pool.affine_select(out=one[:], in_=one[:], compare_op=ALU.not_equal, fill=1.0, base=0,
                                   pattern=[[-1, P]], channel_multiplier=1).then_inc(made, 1)
            pool.wait_ge(made, 2)


def group_norm(m, name, out_of, eps=1e-5):
    nc = m.nc
    with Stage(nc) as ctx:
        sb = lambda n, s, dt=F32: m.sb(f"{name}_{n}", s, dt, ctx)
        group, stats, mv, moments = sb("group", [P, P]), sb("stats", [P, B * 2, 6]), sb("mv", [P, B, 2]), sb("moments", [P, 2, B])
        gm, rstd, tmp, epsb = sb("gm", [P, 2, B]), sb("rstd", [P, B]), sb("tmp", [P, B]), sb("eps", [P, 1])
        ps = m.psum(f"{name}_ps", [P, 2 * B], ctx)
        loaded, ready, summed, rooted, dve_step = (m.sem(f"{name}_{x}", ctx) for x in ("loaded", "ready", "summed", "rooted", "dve"))
        block = ctx.enter_context(nc.Block())

        @block.sync
        def _(sp):
            sp.dma_start(group[:], m.ins["c_group"]).then_inc(loaded, 16)

        @block.tensor
        def _(pe):
            pe.wait_ge(loaded, 16)
            pe.wait_ge(ready, 1)
            pe.matmul(ps[:], group[:], flat(moments[:]), start=True, stop=True).then_inc(summed, 1)

        @block.scalar
        def _(act):
            act.wait_ge(ready, 2)
            act.activation(tmp[:], rstd[:], ACT.Sqrt, bias=epsb[:]).then_inc(rooted, 1)

        @block.vector
        def _(dve):
            step = Chain(dve, dve_step)
            step(dve.memset(epsb[:], eps))
            for b in range(B):
                for h in range(2):
                    last = dve.bn_stats(stats[:, 2 * b + h, :], m.xc[:, b, h * 512:(h + 1) * 512])
            step(last)
            for b in range(B):
                last = dve.bn_aggr(mv[:, b, :], stats[:, 2 * b:2 * b + 2, :])
            step(last)
            step(dve.tensor_tensor(tmp[:], mv[:, :, 0], mv[:, :, 0], ALU.mult))
            step(dve.tensor_copy(moments[:, 0, :], mv[:, :, 0]))
            dve.tensor_tensor(moments[:, 1, :], mv[:, :, 1], tmp[:], ALU.add).then_inc(ready, 1)
            dve.wait_ge(summed, 1)
            step(dve.tensor_copy(flat(gm[:]), ps[:]))
            step(dve.tensor_tensor(tmp[:], gm[:, 0, :], gm[:, 0, :], ALU.mult))
            dve.tensor_tensor(rstd[:], gm[:, 1, :], tmp[:], ALU.subtract).then_inc(ready, 1)
            dve.wait_ge(rooted, 1)
            step(dve.reciprocal(rstd[:], tmp[:]))
            for b in range(B):
                src, dst = out_of(b)
                last = dve.tensor_scalar(dst, src, gm[:, 0, b:b + 1], rstd[:, b:b + 1], ALU.subtract, ALU.mult)
            step(last)


def token_norm(m, name, keep=None, eps=1e-5):
    nc = m.nc
    G = 4
    with Stage(nc) as ctx:
        sb = lambda n, s, dt=F32: m.sb(f"{name}_{n}", s, dt, ctx)
        xn = keep if keep is not None else sb("xn", [P, TILES, C])
        stats, mv = sb("stats", [P, TILES, 6]), sb("mv", [P, TILES, 2])
        root, rstd, epsb = sb("root", [P, TILES]), sb("rstd", [P, TILES]), sb("eps", [P, 1])
        ps = [m.psum(f"{name}_ps{i}", [P, G * P], ctx) for i in range(2)]
        ready, rooted, turned, taken, dve_step = (m.sem(f"{name}_{x}", ctx) for x in ("ready", "rooted", "turned", "taken", "dve"))
        block = ctx.enter_context(nc.Block())

        @block.vector
        def _(dve):
            step = Chain(dve, dve_step)
            step(dve.memset(epsb[:], eps))
            for t in range(TILES):
                last = dve.bn_stats(stats[:, t, :], m.tt[:, t, :])
            step(last)
            for t in range(TILES):
                last = dve.bn_aggr(mv[:, t, :], stats[:, t, :])
            last.then_inc(ready, 1)
            dve.wait_ge(rooted, 1)
            step(dve.reciprocal(rstd[:], root[:]))
            for t in range(TILES):
                dve.tensor_scalar(xn[:, t, :], m.tt[:, t, :], mv[:, t, 0:1], rstd[:, t:t + 1], ALU.subtract, ALU.mult).then_inc(ready, 1)

        @block.scalar
        def _(act):
            act.wait_ge(ready, 1)
            act.activation(root[:], mv[:, :, 1], ACT.Sqrt, bias=epsb[:]).then_inc(rooted, 1)
            for g in range(TILES // G):
                act.wait_ge(turned, g + 1)
                act.activation(m.xnT[:].rearrange("p b n -> p (b n)")[:, g * G * P:(g + 1) * G * P], ps[g % 2][:], ACT.Copy).then_inc(taken, 1)
            act.wait_ge(taken, TILES // G)

        @block.tensor
        def _(pe):
            for g in range(TILES // G):
                if g >= 2:
                    pe.wait_ge(taken, g - 1)
                pe.wait_ge(ready, 1 + G * (g + 1))
                for t in range(G):
                    last = pe.transpose(ps[g % 2][:, t * P:(t + 1) * P], xn[:, g * G + t, :], m.ident[:])
                last.then_inc(turned, 1)


def one_head_attention(m, name, wq, wk, wv, bq, bk, bv, scale, causal):
    nc = m.nc
    T = N // P
    with Stage(nc) as ctx:
        sb = lambda n, s, dt=F32: m.sb(f"{name}_{n}", s, dt, ctx)
        w = sb("w", [P, 3, C])
        bqk, bvb = sb("bqk", [P, 2]), sb("bvb", [P, C])
        xs, q, k, v = sb("xs", [P, N]), sb("q", [P, N]), sb("k", [P, N]), sb("v", [P, T, C])
        neg, rows, inv = sb("neg", [P, T]), sb("rows", [P, T]), sb("inv", [P, T])
        prob, probT = [sb(f"prob{i}", [P, N]) for i in range(2)], [sb(f"probT{i}", [P, T, P]) for i in range(2)]
        out = [sb(f"out{i}", [P, C]) for i in range(2)]
        tril = sb("tril", [P, P]) if causal else None
        s_ps = [m.psum(f"{name}_s{i}", [P, N], ctx) for i in range(2)]
        t_ps = m.psum(f"{name}_t", [P, T, P], ctx)
        o_ps = m.psum(f"{name}_o", [P, 512], ctx)
        r_ps = m.psum(f"{name}_r", [P, 512], ctx)
        names = ("loaded", "staged", "qk_made", "v_made", "qk_kept", "v_kept", "scored", "maxed", "exped", "masked", "turned", "turn_kept",
                 "mixed", "inverted", "scaled", "out_turned", "added", "dve", "tri")
        S = {x: m.sem(f"{name}_{x}", ctx) for x in names}
        n_loads = (5 if causal else 8)
        block = ctx.enter_context(nc.Block())
        width = lambda t: (t + 1) * P if causal else N

        @block.sync
        def _(sp):
            for i, x in enumerate((wq, wk, wv)):
                sp.dma_start(w[:, i, :], x).then_inc(S["loaded"], 16)
            if not causal:
                sp.dma_start(bqk[:, 0:1], bq.rearrange("(c o) -> c o", o=1)).then_inc(S["loaded"], 16)
                sp.dma_start(bqk[:, 1:2], bk.rearrange("(c o) -> c o", o=1)).then_inc(S["loaded"], 16)
                sp.dma_start(bvb[:], bv.rearrange("(o c) -> o c", o=1).broadcast_to((P, C))).then_inc(S["loaded"], 16)
            else:
                sp.dma_start(tril[:], m.ins["c_tril"]).then_inc(S["loaded"], 16)
            sp.wait_ge(S["loaded"], 16 * (4 if causal else 6))

        @block.tensor
        def _(pe):
            pe.wait_ge(S["loaded"], 16 * (4 if causal else 6))
            with pe.Fori(0, B) as b:
                pe.wait_ge(S["staged"], b + 1)
                for i in range(2):
                    for h in range(2):
                        last = pe.matmul(s_ps[i][:, h * 512:(h + 1) * 512], w[:, i, :], xs[:, h * 512:(h + 1) * 512], start=True, stop=True)
                last.then_inc(S["qk_made"], 1)
                for t in range(T):
                    last = pe.matmul(t_ps[:, t, :], xs[:, t * P:(t + 1) * P], w[:, 2, :], start=True, stop=True)
                last.then_inc(S["v_made"], 1)
                pe.wait_ge(S["qk_kept"], 2 * b + 2)

                def scores(t):
                    if t >= 2:
                        pe.wait_ge(S["exped"], b * T + t - 1)
                        if causal:
                            pe.wait_ge(S["masked"], b * T + t - 1)
                    for h in range(2):
                        last = pe.matmul(s_ps[t % 2][:, h * 512:(h + 1) * 512], q[:, t * P:(t + 1) * P], k[:, h * 512:(h + 1) * 512], start=True, stop=True)
                    last.then_inc(S["scored"], 1)

                def out_turn(t):
                    pe.wait_ge(S["scaled"], b * T + t + 1)
                    if t >= 1:
                        pe.wait_ge(S["added"], b * T + t)
                    pe.transpose(r_ps[:, 0:P], out[t % 2][:], m.ident[:]).then_inc(S["out_turned"], 1)

                scores(0)
                pe.wait_ge(S["v_kept"], b + 1)
                for t in range(T):
                    if t + 1 < T:
                        scores(t + 1)
                    pe.wait_ge(S["masked" if causal else "exped"], b * T + t + 1)
                    if t >= 1:
                        pe.wait_ge(S["turn_kept"], b * T + t)
                    n = width(t) // P
                    for j in range(n):
                        last = pe.transpose(t_ps[:, j, :], prob[t % 2][:, j * P:(j + 1) * P], m.ident[:])
                    last.then_inc(S["turned"], 1)
                    if not causal and t >= 1:
                        out_turn(t - 1)
                    pe.wait_ge(S["turn_kept"], b * T + t + 1)
                    if t >= 1:
                        pe.wait_ge(S["added" if causal else "scaled"], b * T + t)
                    for j in range(n):
                        last = pe.matmul(o_ps[:, 0:C], probT[t % 2][:, j, :], v[:, j, :], start=(j == 0), stop=(j == n - 1))
                    last.then_inc(S["mixed"], 1)
                if not causal:
                    out_turn(T - 1)

        @block.scalar
        def _(act):
            act.wait_ge(S["loaded"], 16 * (4 if causal else 6))
            def scale_out(b, t):
                act.wait_ge(S["mixed"], b * T + t + 1)
                act.wait_ge(S["inverted"], b * T + t + 1)
                if t >= 2:
                    act.wait_ge(S["out_turned"], b * T + t - 1)
                act.activation(out[t % 2][:], o_ps[:, 0:C], ACT.Copy, scale=inv[:, t:t + 1]).then_inc(S["scaled"], 1)

            with act.Fori(0, B) as b:
                act.wait_ge(S["qk_made"], b + 1)
                for i, to in enumerate((q, k)):
                    if causal:
                        act.activation(to[:], s_ps[i][:], ACT.Copy).then_inc(S["qk_kept"], 1)
                    else:
                        act.activation(to[:], s_ps[i][:], ACT.Identity, bias=bqk[:, i:i + 1]).then_inc(S["qk_kept"], 1)
                for t in range(T):
                    act.wait_ge(S["maxed"], b * T + t + 1)
                    if t >= 2:
                        act.wait_ge(S["turned"], b * T + t - 1)
                    if causal:
                        act.activation(prob[t % 2][:, 0:width(t)], s_ps[t % 2][:, 0:width(t)], ACT.Exp, bias=neg[:, t:t + 1], scale=scale).then_inc(S["exped"], 1)
                    else:
                        act.activation(prob[t % 2][:], s_ps[t % 2][:], ACT.Exp, bias=neg[:, t:t + 1], accum_out=rows[:, t:t + 1]).then_inc(S["exped"], 1)
                        if t >= 1:
                            scale_out(b, t - 1)
                if not causal:
                    scale_out(b, T - 1)

        @block.vector
        def _(dve):
            dve.wait_ge(S["loaded"], 16 * (4 if causal else 6))
            def add_turned(b, t):
                dve.wait_ge(S["out_turned"], b * T + t + 1)
                tile = at(m.xc, b)[:, t * P:(t + 1) * P]
                dve.tensor_tensor(tile, r_ps[:, 0:P], tile, ALU.add).then_inc(S["added"], 1)

            PER = T * 4 if causal else 0
            with dve.Fori(0, B) as b:
                step = Chain(dve, S["dve"], b * PER)
                dve.tensor_copy(xs[:], at(m.xnT, b)).then_inc(S["staged"], 1)
                dve.wait_ge(S["v_made"], b + 1)
                if causal:
                    dve.tensor_copy(v[:], t_ps[:]).then_inc(S["v_kept"], 1)
                else:
                    dve.tensor_tensor(v[:], t_ps[:], bvb[:].rearrange("p (o c) -> p o c", o=1).broadcast_to((P, T, C)), ALU.add).then_inc(S["v_kept"], 1)

                def maximum(t):
                    dve.wait_ge(S["scored"], b * T + t + 1)
                    if causal:
                        step(dve.tensor_reduce(neg[:, t:t + 1], s_ps[t % 2][:], AX.X, ALU.max))
                        dve.tensor_scalar(neg[:, t:t + 1], neg[:, t:t + 1], -scale, None, ALU.mult).then_inc(S["maxed"], 1)
                    else:
                        dve.tensor_reduce(neg[:, t:t + 1], s_ps[t % 2][:], AX.X, ALU.max, negate=True).then_inc(S["maxed"], 1)

                maximum(0)
                for t in range(T):
                    if causal:
                        dve.wait_ge(S["exped"], b * T + t + 1)
                        pr, n = prob[t % 2], width(t)
                        step(dve.tensor_tensor(pr[:, n - P:n], pr[:, n - P:n], tril[:], ALU.mult))
                        dve.scalar_tensor_tensor(out=pr[:, 0:n], in0=s_ps[t % 2][:, 0:n], scalar=0.0, in1=pr[:, 0:n], op0=ALU.not_equal,
                                                 op1=ALU.mult, accum_out=rows[:, t:t + 1]).then_inc(S["masked"], 1)
                    if t + 1 < T:
                        maximum(t + 1)
                    dve.wait_ge(S["turned"], b * T + t + 1)
                    n = width(t) // P
                    if t >= 2:
                        dve.wait_ge(S["mixed"], b * T + t - 1)
                    dve.tensor_copy(probT[t % 2][:, 0:n, :], t_ps[:, 0:n, :]).then_inc(S["turn_kept"], 1)
                    if causal:
                        dve.wait_ge(S["masked"], b * T + t + 1)
                        step(dve.tensor_scalar(inv[:, t:t + 1], rows[:, t:t + 1], 1e-9, None, ALU.add))
                        step(dve.reciprocal(inv[:, t:t + 1], inv[:, t:t + 1]))
                        dve.wait_ge(S["mixed"], b * T + t + 1)
                        tile = at(m.xc, b)[:, t * C:(t + 1) * C]
                        dve.scalar_tensor_tensor(out=tile, in0=o_ps[:, 0:C], scalar=inv[:, t:t + 1], in1=tile, op0=ALU.mult,
                                                 op1=ALU.add).then_inc(S["added"], 1)
                    else:
                        dve.reciprocal(inv[:, t:t + 1], rows[:, t:t + 1]).then_inc(S["inverted"], 1)
                        if t >= 1:
                            add_turned(b, t - 1)
                if not causal:
                    add_turned(b, T - 1)
                assert step.n == PER, step.n



def turn_activations(m, name, out=None):
    nc = m.nc
    G = 4
    with Stage(nc) as ctx:
        ps = [m.psum(f"{name}_ps{i}", [P, G * P], ctx) for i in range(4)]
        turned, taken, stored = (m.sem(f"{name}_{x}", ctx) for x in ("turned", "taken", "stored"))
        block = ctx.enter_context(nc.Block())
        flat_x = m.xc[:].rearrange("p b n -> p (b n)")
        GROUPS = TILES // G

        @block.tensor
        def _(pe):
            for g in range(GROUPS):
                if g >= 4:
                    pe.wait_ge(taken, g - 3)
                for t in range(G):
                    last = pe.transpose(ps[g % 4][:, t * P:(t + 1) * P], m.tt[:, g * G + t, :], m.ident[:])
                last.then_inc(turned, 1)

        @block.vector
        def _(dve):
            for g in range(GROUPS):
                dve.wait_ge(turned, g + 1)
                dve.tensor_copy(flat_x[:, g * G * P:(g + 1) * G * P], ps[g % 4][:]).then_inc(taken, 1)

        if out is not None:
            @block.sync
            def _(sp):
                for b in range(B):
                    sp.wait_ge(taken, (b + 1) * GROUPS // B)
                    sp.dma_start(out[b].rearrange("c h w -> c (h w)"), m.xc[:, b, :]).then_inc(stored, 16)
                sp.wait_ge(stored, B * 16)


class HeadScratch:

    def __init__(self, nc, name, n):
        self.q = nc.dram_tensor(f"{name}_q_parts", [B, 3, P, n], BF16, kind="Internal").ap()
        self.k = nc.dram_tensor(f"{name}_k_parts", [B, 3, P, n], BF16, kind="Internal").ap()
        self.v = nc.dram_tensor(f"{name}_v", [B, min(P, n), n // min(P, n), HEADS * SLOT], F32, kind="Internal").ap()


def split_in_three(eng, step, parts, x, rest):
    step(eng.tensor_copy(parts[:, 0], x))
    step(eng.tensor_tensor(rest, x, parts[:, 0], ALU.subtract))
    step(eng.tensor_copy(parts[:, 1], rest))
    return eng.tensor_tensor(parts[:, 2], rest, parts[:, 1], ALU.subtract)


def many_heads_attention(m, name, n, scratch, out, scale, bias_parts=None):
    nc = m.nc
    TN, CH = min(P, n), min(512, n)
    T, NH, NC = n // TN, n // CH, n // CH
    KB = STACK + (3 if bias_parts is not None else 0)
    KM = KB + 3
    GH = NH * T
    NU = 4 * T
    R = NU // GH
    LAG = GH + (4 if GH >= 16 else 1)
    GU, UU, PN = 4 * GH, 16 * GH, 4 * NH
    NUSES = 4 * (NU + 1)
    LOADS = 2 * len(Q_PART) * 16
    SUMS = 4 * n // P
    with Stage(nc) as ctx:
        sb = lambda nm, s, dt=F32: m.sb(f"{name}_{nm}", s, dt, ctx)
        qs = [sb(f"qs{s}", [P, 4, n], BF16) for s in range(4)]
        ks = [sb(f"ks{s}", [P, 4, n], BF16) for s in range(4)]
        vs = [sb(f"vs{i}", [TN, T, 8 * SLOT]) for i in range(2)]
        prob = [sb(f"prob{i}", [TN, CH]) for i in range(8)]
        mx = [sb(f"mx{s}", [TN, NU]) for s in range(4)]
        mrest, mparts = sb("mrest", [TN, NU]), sb("mparts", [TN, 3, NU], BF16)
        mrows = [sb(f"mrows{s}", [NU, 3, TN], BF16) for s in range(4)]
        spread, inverse, wide = sb("spread", [P, SUMS]), sb("inverse", [P, SUMS]), [sb(f"wide{i}", [P, n]) for i in range(2)]
        sums_dram = nc.dram_tensor(f"{name}_sums_d", [4, n], F32, kind="Internal").ap()
        inverse_dram = nc.dram_tensor(f"{name}_inverse_d", [4, n], F32, kind="Internal").ap()
        n_ps = [m.psum(f"{name}_n{i}", [P, 1024], ctx) for i in range(2)]
        t_ps = [m.psum(f"{name}_t{i}", [P, 512], ctx) for i in range(3)]
        o_ps = m.psum(f"{name}_o", [P, 512], ctx)
        cleared = m.sem(f"{name}_cleared", ctx)
        biased = m.sem(f"{name}_biased", ctx)
        qk_loaded = [m.sem(f"{name}_qk_loaded{s}", ctx) for s in range(4)]
        v_loaded = [m.sem(f"{name}_v_loaded{i}", ctx) for i in range(2)]
        row_loaded = [m.sem(f"{name}_row_loaded{s}", ctx) for s in range(4)]
        first_made, first_used, rows_ready, rows_made = (m.sem(f"{name}_{x}", ctx) for x in ("first_made", "first_used", "rows_ready", "rows_made"))
        scored, exped, mixed, kept, dve_step = (m.sem(f"{name}_{x}", ctx) for x in ("scored", "exped", "mixed", "kept", "dve"))
        held, held_pe = m.sem(f"{name}_held", ctx), m.sem(f"{name}_held_pe", ctx)
        inverted, divided = m.sem(f"{name}_inverted", ctx), m.sem(f"{name}_divided", ctx)
        sums_out, sums_in, inverse_out, inverse_in, rounds = m.sums_out, m.sums_in, m.inverse_out, m.inverse_in, m.rounds
        m.rounds += 2 * B
        block = ctx.enter_context(nc.Block())
        heads_of = lambda dram, half: dram.rearrange("(g h r) n -> g r h n", g=2, h=4, r=HD)[half]

        @block.sync
        def _(sp):
            sp.wait_ge(cleared, 8)
            if bias_parts is not None:
                for s in range(4):
                    sp.dma_start(ks[s][STACK:KB, :, :], bias_parts[:, 4 * (s % 2):4 * (s % 2) + 4, :]).then_inc(biased, 16)
            with sp.Fori(0, B // 2) as i:
                for s in range(4):
                    b, half = 2 * i + s // 2, s % 2
                    sp.wait_ge(kept, i * PN + (s + 1) * NH)
                    for parts, dram, slots in ((qs[s], scratch.q, Q_PART), (ks[s], scratch.k, K_PART)):
                        for slot, level in enumerate(slots):
                            src = dram[bass.ds(b, 1), level, :, :].rearrange("o p n -> (o p) n")
                            sp.dma_start(parts[slot * HD:(slot + 1) * HD, :, :], heads_of(src, half)).then_inc(qk_loaded[s], 16)
                    if half == 1:
                        sp.dma_start(vs[s // 2][:], scratch.v[bass.ds(b, 1), :, :, :].rearrange("o p t c -> (o p) t c")).then_inc(v_loaded[s // 2], 16)
                for s in range(4):
                    sp.wait_ge(rows_made, i * 4 + s + 1)
                    for part in range(3):
                        sp.dma_start(qs[s][KB + part:KB + part + 1, :, :].rearrange("o h (t q) -> o (h t) q", q=TN),
                                     mrows[s][:, part, :]).then_inc(row_loaded[s], 16)

        @block.tensor
        def _(pe):
            if bias_parts is not None:
                pe.wait_ge(biased, 64)
            pe.sem_inc(mixed, 2)

            def wait(sem, value):
                if TN < P:
                    hold(pe, sem, value, held_pe)
                else:
                    pe.wait_ge(sem, value)

            with pe.Fori(0, B // 2) as i:
                uses = [0]

                def bank():
                    wait(first_used, i * NUSES + uses[0] + 1)
                    uses[0] += 1
                    return n_ps[(uses[0] - 1) % 2]

                def first_pass(u):
                    s, j, t = u // NU, u % NU // T, u % T
                    if u % NU == 0:
                        wait(qk_loaded[s], (i + 1) * LOADS)
                    ps = bank()
                    for c in range(NC):
                        last = pe.matmul(ps[0:TN, c * CH:(c + 1) * CH], qs[s][0:KB, j, t * TN:(t + 1) * TN], ks[s][0:KB, j, c * CH:(c + 1) * CH], start=True, stop=True)
                    last.then_inc(first_made, 1)

                def turn_maxima(s):
                    wait(rows_ready, i * 4 + s + 1)
                    ps = bank()[:].bitcast(BF16)
                    for part in range(3):
                        last = pe.transpose(ps[0:NU, part * TN:(part + 1) * TN], mparts[:, part, :], m.identb[0:TN, 0:TN])
                    last.then_inc(first_made, 1)

                def second_pass(g, heads):
                    s, h, t = g // GH, g % GH // T, g % T
                    if g % GH == 0:
                        wait(row_loaded[s], (i + 1) * 48)
                    for j in heads:
                        q = 4 * g + j
                        if q >= 3:
                            wait(exped, i * UU + q - 2)
                        pe.matmul(t_ps[q % 3][0:TN, 0:CH], ks[s][0:KM, j, t * TN:(t + 1) * TN], qs[s][0:KM, j, h * CH:(h + 1) * CH], start=True, stop=True).then_inc(scored, 1)

                def mix(g):
                    s, t = g // GH, g % T
                    if g % GH == 0 and s % 2 == 0:
                        wait(v_loaded[s // 2], (i + 1) * 16)
                    if t == 0:
                        wait(kept, PN + i * PN + g // T)
                    wait(exped, i * UU + 4 * (g + 1))
                    for j in range(4):
                        head = 4 * (s % 2) + j
                        last = pe.matmul(o_ps[SLOT * j:SLOT * (j + 1), 0:CH], vs[s // 2][:, t, head * SLOT:(head + 1) * SLOT], prob[(4 * g + j) % 8][:], start=(t == 0), stop=(t == T - 1))
                    last.then_inc(mixed, 1)

                for slot in range(GU + LAG + 1):
                    units = range(R * slot, R * (slot + 1)) if slot < GU else ()
                    for u in units[:R // 2]:
                        first_pass(u)
                    if slot >= LAG and slot - LAG < GU:
                        second_pass(slot - LAG, (0, 1))
                    for u in units[R // 2:]:
                        first_pass(u)
                    if slot % GH == 0 and 1 <= slot // GH <= 4:
                        turn_maxima(slot // GH - 1)
                    if slot >= LAG and slot - LAG < GU:
                        second_pass(slot - LAG, (2, 3))
                    if slot > LAG:
                        mix(slot - LAG - 1)
                assert uses[0] == NUSES

        @block.gpsimd
        def _(pool):
            for s in range(4):
                for rows in (qs[s], ks[s]):
                    pool.memset(rows[STACK:KM, :, :].rearrange("p h n -> p (h n)").bitcast(F32), TWO_ONES).then_inc(cleared, 1)
            with pool.Fori(0, B // 2) as i:
                for s in range(4):
                    b = 2 * i + s // 2
                    done = i * 4 + s + 1
                    half = out[:, s % 2, bass.ds(b, 1), :].rearrange("p o n -> p (o n)")
                    hold(pool, kept, PN + i * PN + (s + 1) * NH, held)
                    pool.dma_start(sums_dram, out[HD:P:SLOT, s % 2, bass.ds(b, 1), :].rearrange("p o n -> p (o n)")).then_inc(sums_out, 16)
                    hold(pool, sums_out, (rounds + done) * 16, held)
                    pool.dma_start(spread[:], sums_dram.rearrange("h (c q) -> (h c) q", q=SUMS)).then_inc(sums_in, 16)
                    hold(pool, inverted, done, held)
                    pool.dma_start(inverse_dram.rearrange("h (c q) -> (h c) q", q=SUMS), inverse[:]).then_inc(inverse_out, 16)
                    hold(pool, inverse_out, (rounds + done) * 16, held)
                    pool.dma_start(wide[s % 2][:], inverse_dram.rearrange("h (o n) -> h o n", o=1).broadcast_to((4, SLOT, n))).then_inc(inverse_in, 16)
                    hold(pool, inverse_in, (rounds + done) * 16, held)
                    pool.tensor_tensor(half, half, wide[s % 2][:], ALU.mult).then_inc(divided, 1)
                    hold(pool, divided, done, held)

        @block.scalar
        def _(act):
            with act.Fori(0, B // 2) as i:
                for q in range(UU):
                    if q % 4 == 0:
                        act.wait_ge(mixed, i * GU + q // 4 + 1)
                    act.wait_ge(scored, i * UU + q + 1)
                    act.activation(prob[q % 8][:], t_ps[q % 3][0:TN, 0:CH], ACT.Exp, scale=scale).then_inc(exped, 1)

        @block.vector
        def _(dve):
            dve.sem_inc(first_used, 2)
            dve.sem_inc(kept, PN)
            PER = 4 * 3
            with dve.Fori(0, B // 2) as i:
                step = Chain(dve, dve_step, i * PER)
                uses = [0]

                def bank():
                    dve.wait_ge(first_made, i * NUSES + uses[0] + 1)
                    uses[0] += 1
                    return n_ps[(uses[0] - 1) % 2]

                def maximum(u):
                    s = u // NU
                    dve.tensor_reduce(mx[s][:, u % NU:u % NU + 1], bank()[0:TN, 0:n], AX.X, ALU.max, negate=True).then_inc(first_used, 1)

                def rows_of(s):
                    dve.wait_ge(first_used, 2 + i * NUSES + uses[0])
                    split_in_three(dve, step, mparts[:], mx[s][:], mrest[:]).then_inc(rows_ready, 1)
                    dve.wait_ge(rows_ready, i * 4 + s + 1)

                def keep_rows(s):
                    ps = bank()[:].bitcast(BF16)
                    dve.tensor_copy(mrows[s][:].rearrange("a b c -> a (b c)"), ps[0:NU, 0:3 * TN]).then_inc(first_used, 1)
                    dve.wait_ge(first_used, 2 + i * NUSES + uses[0])
                    dve.sem_inc(rows_made, 1)

                def keep_output(p):
                    s, h = p // NH, p % NH
                    dve.wait_ge(mixed, 2 + i * GU + (p + 1) * T)
                    b = 2 * i + s // 2
                    to = out[:, s % 2, bass.ds(b, 1), h * CH:(h + 1) * CH].rearrange("p o n -> p (o n)")
                    dve.tensor_copy(to, o_ps[:, 0:CH]).then_inc(kept, 1)

                def invert(s):
                    dve.wait_ge(sums_in, (rounds + i * 4 + s + 1) * 16)
                    dve.reciprocal(inverse[:], spread[:]).then_inc(inverted, 1)

                for slot in range(GU + LAG + 1):
                    if slot < GU:
                        for u in range(R * slot, R * (slot + 1)):
                            maximum(u)
                    if slot % GH == 0 and 1 <= slot // GH <= 4:
                        keep_rows(slot // GH - 1)
                    if slot < GU and slot % GH == GH - 1:
                        rows_of(slot // GH)
                    g = slot - LAG - 1
                    if g >= 0 and g % T == T - 1:
                        keep_output(g // T)
                    for s in range(4):
                        if slot == min(LAG + GH * (s + 1) + 3, GU + LAG):
                            invert(s)
                assert step.n == PER and uses[0] == NUSES


def head_inputs(m, name, n, scratch, wq, wk, wv, bq, bk, bv, stage, k_scale=1.0, with_pos=None):
    nc = m.nc
    TN, CH = min(P, n), min(512, n)
    T, NC = n // TN, n // CH
    with Stage(nc) as ctx:
        sb = lambda nm, s, dt=F32: m.sb(f"{name}_{nm}", s, dt, ctx)
        src, wqk, wvp, bqk, bvp = sb("src", [P, n]), sb("wqk", [P, 2, C]), sb("wvp", [P, 8, SLOT]), sb("bqk", [P, 2]), sb("bvp", [P, 8, SLOT])
        v = sb("values", [TN, T, HEADS * SLOT])
        x, rest, parts = [sb(f"x{i}", [P, n]) for i in range(2)], [sb(f"rest{i}", [P, n]) for i in range(2)], [sb(f"parts{i}", [P, 3, n], BF16) for i in range(2)]
        qk_ps = [m.psum(f"{name}_p{i}", [P, 1024], ctx) for i in range(2)]
        v_ps = m.psum(f"{name}_v", [P, 2048], ctx)
        zeroed, loaded, staged, qk_made, v_made, qk_kept, taken, cast, split, stored, dve_step = (
            m.sem(f"{name}_{z}", ctx) for z in ("zeroed", "loaded", "staged", "qk_made", "v_made", "qk_kept", "taken", "cast", "split", "stored", "dve"))
        block = ctx.enter_context(nc.Block())
        column = lambda a: a.rearrange("(c o) -> c o", o=1)

        @block.sync
        def _(sp):
            sp.dma_start(wqk[:, 0, :], wq).then_inc(loaded, 16)
            sp.dma_start(wqk[:, 1, :], wk).then_inc(loaded, 16)
            sp.dma_start(bqk[:, 0:1], column(bq)).then_inc(loaded, 16)
            sp.dma_start(bqk[:, 1:2], column(bk)).then_inc(loaded, 16)
            sp.wait_ge(zeroed, 2)
            sp.dma_start(wvp[:, :, 0:HD], wv.rearrange("c (h d) -> c h d", d=HD)).then_inc(loaded, 16)
            sp.dma_start(bvp[:, :, 0:HD], bv.rearrange("(o h d) -> o h d", o=1, d=HD).broadcast_to((P, HEADS, HD))).then_inc(loaded, 16)
            with sp.Fori(0, B) as b:
                for i, dram in enumerate((scratch.q, scratch.k)):
                    sp.wait_ge(split, 2 * b + i + 1)
                    sp.dma_start(dram[bass.ds(b, 1), :, :, :].rearrange("o l p n -> p (o l) n"), parts[i][:]).then_inc(stored, 16)
                sp.wait_ge(taken, b + 2)
                sp.dma_start(scratch.v[bass.ds(b, 1), :, :, :].rearrange("o p t c -> (o p) t c"), v[:]).then_inc(stored, 16)
            sp.wait_ge(stored, (B + 1) * 48)

        @block.gpsimd
        def _(pool):
            pool.memset(wvp[:], 0.0).then_inc(zeroed, 1)
            pool.memset(bvp[:], 1.0).then_inc(zeroed, 1)

        @block.tensor
        def _(pe):
            pe.wait_ge(loaded, 96)
            with pe.Fori(0, B) as b:
                pe.wait_ge(staged, b + 1)
                pe.wait_ge(qk_kept, 2 * b + 2)
                for i in range(2):
                    for c in range(NC):
                        pe.matmul(qk_ps[i][:, c * CH:(c + 1) * CH], wqk[:, i, :], src[:, c * CH:(c + 1) * CH], start=True, stop=True).then_inc(qk_made, 1)
                pe.wait_ge(taken, b + 1)
                for t in range(T):
                    last = pe.matmul(v_ps[0:TN, t * 256:(t + 1) * 256], src[:, t * TN:(t + 1) * TN], wvp[:].rearrange("p h d -> p (h d)"), start=True, stop=True)
                last.then_inc(v_made, 1)

        @block.vector
        def _(dve):
            dve.wait_ge(loaded, 96)
            dve.sem_inc(qk_kept, 2)
            dve.sem_inc(taken, 1)
            dve.sem_inc(stored, 48)
            with dve.Fori(0, B) as b:
                step = Chain(dve, dve_step, b * stage.steps)
                stage(dve, step, b, src, staged)
                assert step.n == stage.steps, step.n
                for i in range(2):
                    dve.wait_ge(qk_made, 2 * NC * b + NC * (i + 1))
                    if with_pos is not None:
                        dve.scalar_tensor_tensor(out=x[i][:], in0=qk_ps[i][:, 0:n], scalar=bqk[:, i:i + 1], in1=with_pos, op0=ALU.add, op1=ALU.add).then_inc(qk_kept, 1)
                    else:
                        dve.tensor_scalar(x[i][:], qk_ps[i][:, 0:n], bqk[:, i:i + 1], (1.0, k_scale)[i], ALU.add, ALU.mult).then_inc(qk_kept, 1)
                dve.wait_ge(qk_kept, 2 * b + 4)
                dve.wait_ge(stored, b * 48 + 48)
                for i in range(2):
                    dve.tensor_copy(parts[i][:, 0], x[i][:]).then_inc(cast, 1)
                dve.wait_ge(cast, 6 * b + 2)
                for i in range(2):
                    dve.tensor_tensor(rest[i][:], x[i][:], parts[i][:, 0], ALU.subtract).then_inc(cast, 1)
                dve.wait_ge(cast, 6 * b + 4)
                for i in range(2):
                    dve.tensor_copy(parts[i][:, 1], rest[i][:]).then_inc(cast, 1)
                dve.wait_ge(cast, 6 * b + 6)
                for i in range(2):
                    dve.tensor_tensor(parts[i][:, 2], rest[i][:], parts[i][:, 1], ALU.subtract).then_inc(split, 1)
                dve.wait_ge(v_made, b + 1)
                flat_bias = bvp[0:TN].rearrange("p h d -> p (h d)").rearrange("p (o c) -> p o c", o=1).broadcast_to((TN, T, 8 * SLOT))
                dve.tensor_tensor(v[:], v_ps[0:TN, 0:T * 256].rearrange("p (t c) -> p t c", c=256), flat_bias, ALU.add).then_inc(taken, 1)


def route(m, name, n_experts, gate, gate_bias, combine, combineT=None):
    nc = m.nc
    E = n_experts
    with Stage(nc) as ctx:
        sb = lambda nm, s, dt=F32: m.sb(f"{name}_{nm}", s, dt, ctx)
        gw, gb, logits, iota = sb("gw", [P, E]), sb("gb", [P, E]), sb("logits", [P, TILES, E]), sb("iota", [P, E])
        top, index, indexf = sb("top", [P, TILES, 8]), sb("index", [P, TILES, 8], U32), sb("indexf", [P, TILES, 2])
        gap, odds, weight, second = sb("gap", [P, TILES]), sb("odds", [P, TILES]), sb("weight", [P, TILES, 2]), sb("second", [P, TILES, E])
        ps = m.psum(f"{name}_ps", [P, TILES, E], ctx)
        dT_ps = [m.psum(f"{name}_d{i}", [P, 512], ctx) for i in range(2)] if combineT is not None else None
        loaded, made, counted, compared, exped, combined, turned, taken, dve_step = (
            m.sem(f"{name}_{x}", ctx) for x in ("loaded", "made", "counted", "compared", "exped", "combined", "turned", "taken", "dve"))
        block = ctx.enter_context(nc.Block())
        n_loads = 2 if gate_bias is not None else 1

        @block.sync
        def _(sp):
            sp.dma_start(gw[:], gate).then_inc(loaded, 16)
            if gate_bias is not None:
                sp.dma_start(gb[:], gate_bias.rearrange("(o e) -> o e", o=1).broadcast_to((P, E))).then_inc(loaded, 16)

        @block.gpsimd
        def _(pool):
            pool.iota(iota[:], pattern=[[1, E]], base=0, channel_multiplier=0, allow_small_or_imprecise_dtypes=True).then_inc(counted, 1)

        @block.tensor
        def _(pe):
            pe.wait_ge(loaded, 16 * n_loads)
            for t in range(TILES):
                last = pe.matmul(ps[:, t, :], m.xnT[:].rearrange("p b n -> p (b n)")[:, t * P:(t + 1) * P], gw[:], start=True, stop=True)
            last.then_inc(made, 1)
            if combineT is not None:
                pe.wait_ge(combined, 1)
                for g in range(TILES // 4):
                    if g >= 2:
                        pe.wait_ge(taken, g - 1)
                    for t in range(4):
                        last = pe.transpose(dT_ps[g % 2][0:E, t * P:(t + 1) * P], combine[:, 4 * g + t, :], m.ident[:])
                    last.then_inc(turned, 1)

        @block.scalar
        def _(act):
            act.wait_ge(compared, 1)
            act.activation(odds[:], gap[:], ACT.Exp).then_inc(exped, 1)

        @block.vector
        def _(dve):
            step = Chain(dve, dve_step)
            dve.wait_ge(made, 1)
            if gate_bias is not None:
                step(dve.tensor_tensor(logits[:], ps[:], gb[:].rearrange("p (o e) -> p o e", o=1).broadcast_to((P, TILES, E)), ALU.add))
            else:
                step(dve.tensor_copy(logits[:], ps[:]))
            for t in range(TILES):
                last = dve.max(top[:, t, :], logits[:, t, :])
            step(last)
            for t in range(TILES):
                last = dve.max_index(index[:, t, :], top[:, t, :], logits[:, t, :])
            dve.tensor_tensor(gap[:], top[:, :, 1], top[:, :, 0], ALU.subtract).then_inc(compared, 1)
            step(last)
            step(dve.tensor_copy(indexf[:], index[:, :, 0:2]))
            dve.wait_ge(exped, 1)
            step(dve.tensor_scalar(weight[:, :, 1], odds[:], 1.0, None, ALU.add))
            step(dve.reciprocal(weight[:, :, 0], weight[:, :, 1]))
            step(dve.tensor_tensor(weight[:, :, 1], weight[:, :, 0], odds[:], ALU.mult))
            dve.wait_ge(counted, 1)
            numbers = iota[:].rearrange("p (o e) -> p o e", o=1).broadcast_to((P, TILES, E))
            for i, to in enumerate((combine, second)):
                step(dve.tensor_tensor(to[:], numbers, indexf[:, :, i:i + 1].broadcast_to((P, TILES, E)), ALU.is_equal))
                step(dve.tensor_tensor(to[:], to[:], weight[:, :, i:i + 1].broadcast_to((P, TILES, E)), ALU.mult))
            dve.tensor_tensor(combine[:], combine[:], second[:], ALU.add).then_inc(combined, 1)
            if combineT is not None:
                for g in range(TILES // 4):
                    dve.wait_ge(turned, g + 1)
                    dve.tensor_copy(combineT[:, g, :], dT_ps[g % 2][0:E, :]).then_inc(taken, 1)
                dve.wait_ge(taken, TILES // 4)


def gated_experts(m, name, n_experts, hidden, w1, w2, w3, combine):
    nc = m.nc
    E, HC, TG = n_experts, hidden // P, 4
    GROUPS = TILES // TG
    UNITS = E * HC
    with Stage(nc) as ctx:
        sb = lambda nm, s, dt=F32: m.sb(f"{name}_{nm}", s, dt, ctx)
        w1s, w2s, w3s = sb("w1", [P, E, hidden]), sb("w2", [P, E, hidden]), sb("w3", [P, E, HC, C])
        gate, hid = [sb(f"gate{i}", [P, 512]) for i in range(2)], [sb(f"hid{i}", [P, HC, 512]) for i in range(2)]
        g_ps, u_ps, o_ps = ([m.psum(f"{name}_{x}{i}", [P, 512], ctx) for i in range(2)] for x in "guo")
        loaded, opened, gated, made, mixed, added = (m.sem(f"{name}_{x}", ctx) for x in ("loaded", "opened", "gated", "made", "mixed", "added"))
        block = ctx.enter_context(nc.Block())

        @block.sync
        def _(sp):
            sp.dma_start(w1s[:], w1.rearrange("e c h -> c e h")).then_inc(loaded, 16)
            sp.dma_start(w2s[:], w2.rearrange("e c h -> c e h")).then_inc(loaded, 16)
            sp.dma_start(w3s[:], w3.rearrange("e (k h) c -> h e k c", k=HC)).then_inc(loaded, 16)

        @block.tensor
        def _(pe):
            pe.wait_ge(loaded, 48)
            with pe.Fori(0, GROUPS) as g:
                x = m.xnT[:].rearrange("p b n -> p (b n)")[:, bass.ds(g * 512, 512)]

                def opening(u):
                    e, k = u // HC, u % HC
                    pe.wait_ge(made, 2 + g * UNITS + u - 1)
                    pe.matmul(g_ps[u % 2][:], w1s[:, e, k * P:(k + 1) * P], x, start=True, stop=True)
                    pe.matmul(u_ps[u % 2][:], w2s[:, e, k * P:(k + 1) * P], x, start=True, stop=True).then_inc(opened, 1)

                def closing(e):
                    pe.wait_ge(made, 2 + g * UNITS + (e + 1) * HC)
                    pe.wait_ge(added, 2 + g * E + e - 1)
                    for t in range(TG):
                        for k in range(HC):
                            last = pe.matmul(o_ps[e % 2][:, t * P:(t + 1) * P], hid[e % 2][:, k, t * P:(t + 1) * P], w3s[:, e, k, :], start=(k == 0), stop=(k == HC - 1))
                    last.then_inc(mixed, 1)

                for e in range(E):
                    for k in range(HC):
                        opening(e * HC + k)
                    if e >= 1:
                        closing(e - 1)
                closing(E - 1)

        @block.scalar
        def _(act):
            with act.Fori(0, GROUPS) as g:
                for u in range(UNITS):
                    act.wait_ge(opened, g * UNITS + u + 1)
                    act.wait_ge(made, 2 + g * UNITS + u - 1)
                    act.activation(gate[u % 2][:], g_ps[u % 2][:], ACT.Silu).then_inc(gated, 1)

        @block.vector
        def _(dve):
            dve.sem_inc(made, 2)
            dve.sem_inc(added, 2)
            with dve.Fori(0, GROUPS) as g:

                def make(u):
                    e, k = u // HC, u % HC
                    dve.wait_ge(gated, g * UNITS + u + 1)
                    if k == 0 and e >= 2:
                        dve.wait_ge(mixed, g * E + e - 1)
                    dve.tensor_tensor(hid[e % 2][:, k, :], gate[u % 2][:], u_ps[u % 2][:], ALU.mult).then_inc(made, 1)

                def add(e):
                    dve.wait_ge(mixed, g * E + e + 1)
                    dve.wait_ge(added, 2 + g * E + e)
                    for t in range(TG):
                        tile = m.tt[:, bass.ds(g * TG + t, 1), :].rearrange("p o c -> p (o c)")
                        weight = combine[:, bass.ds(g * TG + t, 1), e:e + 1].rearrange("p o e -> p (o e)")
                        last = dve.scalar_tensor_tensor(out=tile, in0=o_ps[e % 2][:, t * P:(t + 1) * P], scalar=weight, in1=tile, op0=ALU.mult, op1=ALU.add)
                    last.then_inc(added, 1)

                for e in range(E):
                    for k in range(HC):
                        make(e * HC + k)
                    if e >= 1:
                        add(e - 1)
                add(E - 1)


def gelu_experts(m, name, n_experts, w1, b1, w2, b2, combine, combineT, xn):
    nc = m.nc
    E, TG = n_experts, 4
    GROUPS = TILES // TG
    with Stage(nc) as ctx:
        sb = lambda nm, s, dt=F32: m.sb(f"{name}_{nm}", s, dt, ctx)
        w1s, w2s, b1s, b2s = sb("w1", [P, E, C]), sb("w2", [P, E, C]), sb("b1", [P, E]), sb("b2", [E, C])
        share, hid = sb("share", [E, 512]), [sb(f"hid{i}", [P, 512]) for i in range(2)]
        h_ps = [m.psum(f"{name}_h{i}", [P, 512], ctx) for i in range(2)]
        o_ps = [m.psum(f"{name}_o{i}", [P, 512], ctx) for i in range(2)]
        b_ps = m.psum(f"{name}_b", [P, 512], ctx)
        loaded, staged, opened, made, mixed, biased, bias_added, added = (
            m.sem(f"{name}_{x}", ctx) for x in ("loaded", "staged", "opened", "made", "mixed", "biased", "bias_added", "added"))
        block = ctx.enter_context(nc.Block())

        @block.sync
        def _(sp):
            sp.dma_start(w1s[:], w1.rearrange("e c h -> c e h")).then_inc(loaded, 16)
            sp.dma_start(w2s[:], w2.rearrange("e h c -> h e c")).then_inc(loaded, 16)
            sp.dma_start(b1s[:], b1).then_inc(loaded, 16)
            sp.dma_start(b2s[:], b2).then_inc(loaded, 16)

        @block.tensor
        def _(pe):
            pe.wait_ge(loaded, 64)
            with pe.Fori(0, GROUPS) as g:
                x = m.xnT[:].rearrange("p b n -> p (b n)")[:, bass.ds(g * 512, 512)]
                pe.wait_ge(staged, g + 1)
                for t in range(TG):
                    last = pe.matmul(b_ps[:, t * P:(t + 1) * P], share[:, t * P:(t + 1) * P], b2s[:], start=True, stop=True)
                last.then_inc(biased, 1)

                def closing(e):
                    pe.wait_ge(made, g * E + e + 1)
                    pe.wait_ge(added, 2 + g * E + e - 1)
                    for t in range(TG):
                        last = pe.matmul(o_ps[e % 2][:, t * P:(t + 1) * P], hid[e % 2][:, t * P:(t + 1) * P], w2s[:, e, :], start=True, stop=True)
                    last.then_inc(mixed, 1)

                for e in range(E):
                    if e >= 2:
                        pe.wait_ge(made, g * E + e - 1)
                    pe.matmul(h_ps[e % 2][:], w1s[:, e, :], x, start=True, stop=True).then_inc(opened, 1)
                    if e >= 1:
                        closing(e - 1)
                closing(E - 1)

        @block.scalar
        def _(act):
            act.wait_ge(loaded, 64)
            with act.Fori(0, GROUPS) as g:
                for e in range(E):
                    act.wait_ge(opened, g * E + e + 1)
                    if e >= 2:
                        act.wait_ge(mixed, g * E + e - 1)
                    act.activation(hid[e % 2][:], h_ps[e % 2][:], ACT.Gelu, bias=b1s[:, e:e + 1]).then_inc(made, 1)

        @block.vector
        def _(dve):
            dve.sem_inc(added, 2)
            with dve.Fori(0, GROUPS) as g:
                group = m.tt[:, bass.ds(g * TG, TG), :]
                dve.tensor_copy(share[:], combineT[:, bass.ds(g, 1), :].rearrange("p o n -> p (o n)")).then_inc(staged, 1)
                dve.wait_ge(biased, g + 1)
                dve.tensor_tensor(group, group, b_ps[:].rearrange("p (t c) -> p t c", c=C), ALU.add).then_inc(bias_added, 1)
                dve.wait_ge(bias_added, 2 * g + 1)
                dve.tensor_tensor(group, group, xn[:, bass.ds(g * TG, TG), :], ALU.add).then_inc(bias_added, 1)
                dve.wait_ge(bias_added, 2 * g + 2)
                for e in range(E):
                    dve.wait_ge(mixed, g * E + e + 1)
                    dve.wait_ge(added, 2 + g * E + e)
                    for t in range(TG):
                        tile = m.tt[:, bass.ds(g * TG + t, 1), :].rearrange("p o c -> p (o c)")
                        weight = combine[:, bass.ds(g * TG + t, 1), e:e + 1].rearrange("p o e -> p (o e)")
                        last = dve.scalar_tensor_tensor(out=tile, in0=o_ps[e % 2][:, t * P:(t + 1) * P], scalar=weight, in1=tile, op0=ALU.mult, op1=ALU.add)
                    last.then_inc(added, 1)


def load_padded(eng, to, rows, loaded):
    for half in range(2):
        for j in range(4):
            first = half * 64 + j * HD
            eng.dma_start(to[j * SLOT:j * SLOT + HD, half, :], rows[first:first + HD, :]).then_inc(loaded, 16)
    return 8 * 16


def output_projection(m, name, heads_out, wo, bo):
    nc = m.nc
    T = N // P
    with Stage(nc) as ctx:
        sb = lambda nm, s, dt=F32: m.sb(f"{name}_{nm}", s, dt, ctx)
        wp, bob, src, total = sb("wp", [P, 2, C]), sb("bob", [P, C]), sb("src", [P, 2, N]), sb("total", [P, T, C])
        ps = m.psum(f"{name}_ps", [P, T, C], ctx)
        zeroed, loaded, staged, made, taken, added = (m.sem(f"{name}_{x}", ctx) for x in ("zeroed", "loaded", "staged", "made", "taken", "added"))
        block = ctx.enter_context(nc.Block())

        @block.gpsimd
        def _(pool):
            pool.memset(wp[:], 0.0).then_inc(zeroed, 1)

        @block.sync
        def _(sp):
            sp.dma_start(bob[:], bo.rearrange("(o c) -> o c", o=1).broadcast_to((P, C))).then_inc(loaded, 16)
            sp.wait_ge(zeroed, 1)
            load_padded(sp, wp, wo, loaded)

        @block.tensor
        def _(pe):
            pe.wait_ge(loaded, 9 * 16)
            with pe.Fori(0, B) as b:
                pe.wait_ge(staged, b + 1)
                pe.wait_ge(taken, b + 1)
                for t in range(T):
                    for half in range(2):
                        last = pe.matmul(ps[:, t, :], src[:, half, t * P:(t + 1) * P], wp[:, half, :], start=(half == 0), stop=(half == 1))
                last.then_inc(made, 1)

        @block.vector
        def _(dve):
            dve.wait_ge(loaded, 9 * 16)
            dve.sem_inc(taken, 1)
            with dve.Fori(0, B) as b:
                dve.tensor_copy(src[:], heads_out[:, :, bass.ds(b, 1), :].rearrange("p h o n -> p (h o) n")).then_inc(staged, 1)
                dve.wait_ge(made, b + 1)
                dve.tensor_tensor(total[:], ps[:], bob[:].rearrange("p (o c) -> p o c", o=1).broadcast_to((P, T, C)), ALU.add).then_inc(taken, 1)
                dve.wait_ge(taken, b + 2)
                tokens = at(m.xc, b)
                dve.tensor_tensor(tokens, tokens, total[:].rearrange("p t c -> p (t c)"), ALU.add).then_inc(added, 1)


def edge_bias(m, name, targets, attributes, we, be, bias_parts):
    nc = m.nc
    EDGES = targets.shape[0]
    CHUNK, KEYS = 8192, N // P
    CHUNKS = EDGES // CHUNK
    with Stage(nc) as ctx:
        sb = lambda nm, s, dt=F32: m.sb(f"{name}_{nm}", s, dt, ctx)
        raw, a, c_, short = sb("raw", [P, EDGES // P], I32), sb("a", [P, EDGES // P]), sb("c", [P, EDGES // P]), sb("short", [P, EDGES // P], U16)
        text = [sb(f"text{i}", [P, CHUNK + KEYS], U16) for i in range(2)]
        keys, where = sb("keys", [P, KEYS], I32), sb("where", [P, CHUNKS, KEYS], U32)
        place, miss, best, found, index = sb("place", [P, CHUNKS, KEYS]), sb("miss", [P, CHUNKS, KEYS]), sb("best", [P, KEYS]), sb("found", [P, KEYS]), sb("index", [P, KEYS], U32)
        rows, rowsT, wb = sb("rows", [P, KEYS, 4]), sb("rowsT", [4, N]), sb("wb", [4, HEADS])
        bias, rest, parts = sb("bias", [HEADS, N]), sb("rest", [HEADS, N]), sb("parts", [HEADS, 3, N], BF16)
        ps, b_ps = m.psum(f"{name}_ps", [P, N], ctx), m.psum(f"{name}_b", [P, N], ctx)
        dram = nc.dram_tensor(f"{name}_targets", [EDGES], U16, kind="Internal").ap()
        loaded, packed, sent, keyed, keys_set, chunk_in, searched, indexed, ones, masked, turned, kept, summed, split, stored, dve_step = (
            m.sem(f"{name}_{x}", ctx) for x in ("loaded", "packed", "sent", "keyed", "keys_set", "chunk_in", "searched", "indexed",
                                                "ones", "masked", "turned", "kept_", "summed", "split", "stored", "dve"))
        block = ctx.enter_context(nc.Block())

        @block.sync
        def _(sp):
            sp.dma_start(raw[:], targets.rearrange("(p e) -> p e", p=P)).then_inc(loaded, 16)
            sp.dma_start(wb[0:3, :], we).then_inc(loaded, 16)
            sp.dma_start(wb[3:4, :], be.rearrange("(o h) -> o h", o=1)).then_inc(loaded, 16)
            sp.wait_ge(packed, 1)
            sp.dma_start(dram.rearrange("(p e) -> p e", p=P), short[:]).then_inc(sent, 16)
            sp.wait_ge(sent, 16)
            for i in range(CHUNKS):
                if i >= 2:
                    sp.wait_ge(searched, i - 1)
                sp.dma_start(text[i % 2][:, 0:CHUNK], dram[i * CHUNK:(i + 1) * CHUNK].rearrange("(o e) -> o e", o=1).broadcast_to((P, CHUNK))).then_inc(chunk_in, 16)
                sp.wait_ge(chunk_in, 16 * (i + 1))
            sp.wait_ge(split, 1)
            sp.dma_start(bias_parts.rearrange("l h n -> h l n"), parts[:]).then_inc(stored, 16)
            sp.wait_ge(stored, 16)

        @block.gpsimd
        def _(pool):
            pool.memset(rows[:, :, 3:4], 1.0).then_inc(ones, 1)
            pool.iota(keys[:], pattern=[[P, KEYS]], base=0, channel_multiplier=1).then_inc(keyed, 1)
            pool.wait_ge(indexed, 1)
            for r in range(KEYS):
                pool.indirect_dma_start(out=rows[:, r, 0:3], out_offset=None, in_=attributes,
                                        in_offset=bass.IndirectOffsetOnAxis(ap=index[:, r:r + 1], axis=0)).then_inc(m.gathered, 16)
            pool.wait_ge(m.gathered, 16 * KEYS)

        @block.vector
        def _(dve):
            step = Chain(dve, dve_step)
            dve.wait_ge(loaded, 48)
            step(dve.tensor_copy(a[:], raw[:]))
            step(dve.tensor_scalar(c_[:], a[:], 0.0, float(N), ALU.is_lt, ALU.mult))
            step(dve.tensor_tensor(a[:], a[:], c_[:], ALU.add))
            step(dve.tensor_scalar(c_[:], a[:], 0.0, float(2 * N), ALU.is_lt, ALU.mult))
            step(dve.tensor_scalar(a[:], a[:], 0.0, float(N), ALU.max, ALU.min))
            step(dve.tensor_tensor(a[:], a[:], c_[:], ALU.max))
            dve.tensor_copy(short[:], a[:]).then_inc(packed, 1)
            dve.wait_ge(keyed, 1)
            for i in range(2):
                dve.tensor_copy(text[i][:, CHUNK:CHUNK + KEYS], keys[:]).then_inc(keys_set, 1)
            dve.wait_ge(keys_set, 2)
            for i in range(CHUNKS):
                dve.wait_ge(chunk_in, 16 * (i + 1))
                dve.max_index(where[:, i, :], text[i % 2][:, CHUNK:CHUNK + KEYS], text[i % 2][:]).then_inc(searched, 1)
            dve.wait_ge(searched, CHUNKS)
            step(dve.tensor_copy(place[:], where[:]))
            step(dve.tensor_scalar(miss[:], place[:], float(CHUNK), float(2 * EDGES), ALU.is_ge, ALU.mult))
            for i in range(CHUNKS):
                last = dve.scalar_tensor_tensor(out=place[:, i, :], in0=place[:, i, :], scalar=float(i * CHUNK), in1=miss[:, i, :], op0=ALU.add, op1=ALU.add)
            step(last)
            step(dve.tensor_reduce(best[:], place[:].rearrange("p c k -> p k c"), AX.X, ALU.min))
            step(dve.tensor_scalar(found[:], best[:], float(EDGES), None, ALU.is_lt))
            step(dve.tensor_scalar(best[:], best[:], float(EDGES - 1), None, ALU.min))
            dve.tensor_copy(index[:], best[:]).then_inc(indexed, 1)
            dve.wait_ge(m.gathered, 16 * KEYS)
            dve.wait_ge(ones, 1)
            dve.tensor_tensor(rows[:], rows[:], found[:].rearrange("p (k o) -> p k o", o=1).broadcast_to((P, KEYS, 4)), ALU.mult).then_inc(masked, 1)
            dve.wait_ge(turned, 1)
            dve.tensor_copy(rowsT[:], ps[0:4, :]).then_inc(kept, 1)
            dve.wait_ge(summed, 1)
            step(dve.tensor_copy(bias[:], b_ps[0:HEADS, :]))
            split_in_three(dve, step, parts[:], bias[:], rest[:]).then_inc(split, 1)

        @block.tensor
        def _(pe):
            pe.wait_ge(masked, 1)
            for r in range(KEYS):
                last = pe.transpose(ps[0:4, r * P:(r + 1) * P], rows[:, r, :], m.ident[:])
            last.then_inc(turned, 1)
            pe.wait_ge(kept, 1)
            for h in range(2):
                last = pe.matmul(b_ps[0:HEADS, h * 512:(h + 1) * 512], wb[:], rowsT[:, h * 512:(h + 1) * 512], start=True, stop=True)
            last.then_inc(summed, 1)


def pool_by_two(m, name, src, size, dst):
    nc = m.nc
    half = size // 2
    with Stage(nc) as ctx:
        pair = m.sb(f"{name}_pair", [P, B, size, half], F32, ctx)
        four = m.sb(f"{name}_four", [P, B, half, half], F32, ctx)
        step_sem = m.sem(f"{name}_step", ctx)
        block = ctx.enter_context(nc.Block())

        @block.vector
        def _(dve):
            step = Chain(dve, step_sem)
            step(dve.memset(dst[:], 0.0))
            for b in range(B):
                last = dve.tensor_tensor(pair[:, b], src[:, b, 1:size + 1, 1:size + 1:2], src[:, b, 1:size + 1, 2:size + 2:2], ALU.add)
            step(last)
            for b in range(B):
                last = dve.tensor_tensor(four[:, b], pair[:, b, 0:size:2, :], pair[:, b, 1:size:2, :], ALU.add)
            step(last)
            for b in range(B):
                last = dve.tensor_scalar(dst[:, b, 1:half + 1, 1:half + 1], four[:, b], 0.25, None, ALU.mult)
            step(last)


def convolutions(m, name, size, padded, taps, pos, tapped):

    def stage(dve, step, b, src, staged):
        batch = padded[:, bass.ds(b, 1), :, :].rearrange("p o y x -> p (o y) x")
        views = [t[:].rearrange("p (y x) -> p y x", x=size) for t in (src, pos)]
        for tap in range(9):
            y, x = tap // 3, tap % 3
            window = batch[:, y:y + size, x:x + size]
            for i, to in enumerate(views):
                weight = taps[:, i, tap:tap + 1]
                if tap == 0:
                    ins = dve.tensor_scalar(to, window, weight, taps[:, i, 9:10], ALU.mult, ALU.add)
                else:
                    dve.wait_ge(tapped, b * 17 + 2 * tap - 1 + i)
                    ins = dve.scalar_tensor_tensor(out=to, in0=window, scalar=weight, in1=to, op0=ALU.mult, op1=ALU.add)
                ins.then_inc(staged if (tap, i) == (8, 1) else tapped, 1)
        dve.wait_ge(staged, b + 1)

    stage.steps = 0
    return stage


def fuse_scales(m, name, outs, fusion_w, fusion_b):
    nc = m.nc
    with Stage(nc) as ctx:
        sb = lambda nm, s, dt=F32: m.sb(f"{name}_{nm}", s, dt, ctx)
        wp = [sb(f"wp{i}", [P, 2, C]) for i in range(3)]
        up2, up4, fb = sb("up2", [P, 2, N]), sb("up4", [64, N]), sb("fb", [P, 1])
        s2, s4, f = sb("s2", [P, 2, 256]), sb("s4", [P, 2, 64]), sb("f", [P, 3, C])
        f_ps, ps = m.psum(f"{name}_f", [P, 4, C], ctx), m.psum(f"{name}_ps", [P, N], ctx)
        zeroed, loaded, staged, projected, kept, fused, added = (
            m.sem(f"{name}_{x}", ctx) for x in ("zeroed", "loaded", "staged", "projected", "kept_", "fused", "added"))
        block = ctx.enter_context(nc.Block())
        LOADED = 3 * 8 * 16 + 3 * 16

        @block.gpsimd
        def _(pool):
            for w in wp:
                pool.memset(w[:], 0.0).then_inc(zeroed, 1)

        @block.sync
        def _(sp):
            sp.dma_start(up2[:], m.ins["c_up2"].rearrange("(k p) n -> p k n", p=P)).then_inc(loaded, 16)
            sp.dma_start(up4[:], m.ins["c_up4"]).then_inc(loaded, 16)
            sp.dma_start(fb[:], fusion_b.rearrange("(c o) -> c o", o=1)).then_inc(loaded, 16)
            sp.wait_ge(zeroed, 3)
            for i in range(3):
                load_padded(sp, wp[i], fusion_w[i * C:(i + 1) * C, :], loaded)

        @block.tensor
        def _(pe):
            pe.wait_ge(loaded, LOADED)
            with pe.Fori(0, B) as b:
                pe.wait_ge(staged, 2 * b + 2)
                for k in range(2):
                    for half in range(2):
                        pe.matmul(f_ps[:, k, :], s2[:, half, k * P:(k + 1) * P], wp[1][:, half, :], start=(half == 0), stop=(half == 1))
                for half in range(2):
                    last = pe.matmul(f_ps[0:64, 2, :], s4[:, half, :], wp[2][:, half, :], start=(half == 0), stop=(half == 1))
                last.then_inc(projected, 1)
                pe.wait_ge(kept, 2 * b + 2)
                for c in range(2):
                    to, cols = ps[:, c * 512:(c + 1) * 512], slice(c * 512, (c + 1) * 512)
                    for half in range(2):
                        pe.matmul(to, wp[0][:, half, :], outs[0][:, half, bass.ds(b, 1), cols].rearrange("p o n -> p (o n)"), start=(half == 0), stop=False)
                    for k in range(2):
                        pe.matmul(to, f[:, k, :], up2[:, k, cols], start=False, stop=False)
                    last = pe.matmul(to, f[0:64, 2, :], up4[:, cols], start=False, stop=True)
                last.then_inc(fused, 1)

        @block.vector
        def _(dve):
            dve.wait_ge(loaded, LOADED)
            with dve.Fori(0, B) as b:
                for to, src in ((s2, outs[1]), (s4, outs[2])):
                    dve.tensor_copy(to[:], src[:, :, bass.ds(b, 1), :].rearrange("p h o n -> p (h o) n")).then_inc(staged, 1)
                dve.wait_ge(projected, b + 1)
                dve.tensor_copy(f[:, 0:2, :], f_ps[:, 0:2, :]).then_inc(kept, 1)
                dve.tensor_copy(f[0:64, 2, :], f_ps[0:64, 2, :]).then_inc(kept, 1)
                dve.wait_ge(fused, b + 1)
                batch = at(m.xc, b)
                dve.scalar_tensor_tensor(out=batch, in0=ps[:], scalar=fb[:, 0:1], in1=batch, op0=ALU.add, op1=ALU.add).then_inc(added, 1)


def scaled_attention_block(m, ins):
    nc = m.nc
    sizes = (H, H // 2, H // 4)
    with ExitStack() as outer:
        outs = [m.sb(f"scale{i}_out", [P, 2, B, s * s], F32, outer) for i, s in enumerate(sizes)]
        scratch = [HeadScratch(nc, f"scale{i}", s * s) for i, s in enumerate(sizes)]
        with Stage(nc) as ctx:
            padded = [m.sb(f"padded{i}", [P, B, s + 2, s + 2], F32, ctx) for i, s in enumerate(sizes)]
            taps = [m.sb(f"taps{i}", [P, 2, 10], F32, ctx) for i in range(3)]
            tap_loaded = m.sem("tap_loaded", ctx)
            bordered = m.sem("bordered", ctx)
            with nc.Block() as block:
                @block.sync
                def _(sp):
                    for i in range(3):
                        for j, kind in enumerate(("dw", "pos")):
                            sp.dma_start(taps[i][:, j, 0:9], ins[f"L1_conv_{kind}_w"][i].rearrange("c o y x -> c (o y x)")).then_inc(tap_loaded, 16)
                            sp.dma_start(taps[i][:, j, 9:10], ins[f"L1_conv_{kind}_b"][i].rearrange("(c o) -> c o", o=1)).then_inc(tap_loaded, 16)
                    sp.wait_ge(tap_loaded, 12 * 16)

                @block.gpsimd
                def _(pool):
                    pool.memset(padded[0][:], 0.0).then_inc(bordered, 1)
                    pool.wait_ge(bordered, 1)

            inside = lambda b: padded[0][:, b, 1:H + 1, 1:W + 1]
            group_norm(m, "gn1", lambda b: (m.xc[:, b, :].rearrange("p (y x) -> p y x", x=W), inside(b)))
            pool_by_two(m, "pool2", padded[0], H, padded[1])
            pool_by_two(m, "pool4", padded[1], H // 2, padded[2])
            for i, s in enumerate(sizes):
                with Stage(nc) as inner:
                    pos = m.sb(f"pos{i}", [P, s * s], F32, inner)
                    tapped = m.sem(f"tapped{i}", inner)
                    pw, pb = ins["L1_conv_pw_w"], ins["L1_conv_pw_b"]
                    head_inputs(m, f"in{i}", s * s, scratch[i], *(pw[i, :, j * C:(j + 1) * C] for j in range(3)),
                                *(pb[i, j * C:(j + 1) * C] for j in range(3)), convolutions(m, f"conv{i}", s, padded[i], taps[i], pos, tapped), with_pos=pos[:])
        for i, s in enumerate(sizes):
            many_heads_attention(m, f"heads{i}", s * s, scratch[i], outs[i], HD ** -0.5)
        fuse_scales(m, "fuse", outs, ins["L1_conv_fusion_w"], ins["L1_conv_fusion_b"])


def hybrid_kernel(nc, ins, out):
    with ExitStack() as ctx:
        m = Machine(nc, ctx, ins)
        make_identities(m)
        group_norm(m, "gn0", lambda b: (m.xc[:, b, :], m.xnT[:, b, :]))
        one_head_attention(m, "attn0", *(ins[f"L0_conv_{x}"] for x in ("Wq", "Wk", "Wv", "bq", "bk", "bv")), 1.0, False)
        scaled_attention_block(m, ins)
        turn_activations(m, "to_tokens")
        token_norm(m, "ln2")
        one_head_attention(m, "attn2", ins["L2_attn_WQ"], ins["L2_attn_WK"], ins["L2_attn_WV"], None, None, None, C ** -0.5, True)
        with ExitStack() as layer:
            combine = m.sb("combine2", [P, TILES, 16], F32, layer)
            token_norm(m, "ln3")
            route(m, "route2", 16, ins["L2_ffn_gate_w"], ins["L2_ffn_gate_b"], combine)
            gated_experts(m, "experts2", 16, 2 * C, ins["L2_ffn_w1"], ins["L2_ffn_w2"], ins["L2_ffn_w3"], combine)
        with ExitStack() as layer:
            bias_parts = nc.dram_tensor("bias_parts", [3, HEADS, N], BF16, kind="Internal").ap()
            edge_bias(m, "edges", ins["targets"], ins["attributes"], ins["L3_attn_We"], ins["L3_attn_be"], bias_parts)
            heads_out = m.sb("heads_out", [P, 2, B, N], F32, layer)
            scratch = HeadScratch(nc, "edge", N)
            token_norm(m, "ln4")

            def stage(dve, step, b, src, staged):
                dve.tensor_copy(src[:], at(m.xnT, b)).then_inc(staged, 1)
            stage.steps = 0
            head_inputs(m, "in3", N, scratch, *(ins[f"L3_attn_{x}"] for x in ("Wq", "Wk", "Wv", "bq", "bk", "bv")), stage, k_scale=HD ** -0.5)
            many_heads_attention(m, "heads3", N, scratch, heads_out, 1.0, bias_parts)
            output_projection(m, "project", heads_out, ins["L3_attn_Wo"], ins["L3_attn_bo"])
        with ExitStack() as layer:
            combine, combineT = m.sb("combine3", [P, TILES, 8], F32, layer), m.sb("combineT3", [8, TILES // 4, 512], F32, layer)
            xn = m.sb("xn5", [P, TILES, C], F32, layer)
            token_norm(m, "ln5", keep=xn)
            route(m, "route3", 8, ins["L3_ffn_router_w"], None, combine, combineT)
            gelu_experts(m, "experts3", 8, ins["L3_ffn_w1"], ins["L3_ffn_b1"], ins["L3_ffn_w2"], ins["L3_ffn_b2"], combine, combineT, xn)
        turn_activations(m, "to_channels", out)


def spreading_matrix(factor):
    import numpy as np

    def line(fine):
        at_ = (np.arange(fine) + 0.5) / factor - 0.5
        weight = np.maximum(0.0, 1.0 - np.abs(at_[None, :] - np.arange(fine // factor)[:, None]))
        return weight / weight.sum(0, keepdims=True)
    return np.kron(line(H), line(W)).astype(np.float32)


def kernel(**inputs):
    import numpy as np
    from concourse import bacc
    from concourse.bass_utils import run_bass_kernel_spmd

    arrays = {name: np.asarray(a) for name, a in inputs.items()}
    for name in ("L0_conv_Wq", "L0_conv_Wk", "L0_conv_Wv", "L2_attn_WQ", "L2_attn_WK", "L2_attn_WV", "L1_conv_fusion_w", "L3_ffn_router_w", "L3_ffn_b1"):
        arrays[name] = arrays[name].T
    arrays["L1_conv_pw_w"] = arrays["L1_conv_pw_w"].transpose(0, 2, 1)
    arrays["targets"] = arrays.pop("L3_attn_edge_index")[1, ::-1]
    arrays["attributes"] = arrays.pop("L3_attn_edge_attr")[::-1]
    arrays["c_group"] = np.kron(np.eye(C // 4), np.full((4, 4), 0.25)).astype(np.float32)
    arrays["c_tril"] = np.tril(np.ones((P, P), np.float32))
    arrays["c_up2"], arrays["c_up4"] = spreading_matrix(2), spreading_matrix(4)

    nc = bacc.Bacc("TRN2", target_bir_lowering=False, num_devices=1)
    ins = {}
    for name in arrays:
        arrays[name] = np.ascontiguousarray(arrays[name])
        ins[name] = nc.dram_tensor(name, arrays[name].shape, mybir.dt.from_np(arrays[name].dtype), kind="ExternalInput").ap()
    out = nc.dram_tensor("out", (B, C, H, W), F32, kind="ExternalOutput").ap()
    hybrid_kernel(nc, ins, out)
    return run_bass_kernel_spmd(nc, [arrays], core_ids=[0]).results[0]["out"]
```

```python
import struct
from contextlib import ExitStack

import concourse.bass as bass
from concourse import mybir

F32 = mybir.dt.float32
BF16 = mybir.dt.bfloat16
U16 = mybir.dt.uint16
U32 = mybir.dt.uint32
I32 = mybir.dt.int32
ALU = mybir.AluOpType
ACT = mybir.ActivationFunctionType
AX = mybir.AxisListType

P = 128
B, C, H, W = 4, 128, 32, 32
N = H * W
TILES = B * N // P
HEADS, HD = 8, 16
SLOT = 32
Q_PART = (0, 0, 1, 1, 0, 2)
K_PART = (0, 1, 0, 1, 2, 0)
STACK = len(Q_PART) * HD
TWO_ONES = struct.unpack("<f", struct.pack("<I", 0x3F803F80))[0]


class Stage(ExitStack):

    def __init__(self, nc):
        super().__init__()
        self.nc, self.sems = nc, []

    def semaphore(self, name):
        self.sems.append(self.nc.alloc_semaphore(name))
        return self.sems[-1]

    def __exit__(self, *what):
        done = super().__exit__(*what)
        for sem in self.sems:
            self.nc.gpsimd.sem_clear(sem)
            self.nc.release_semaphore(sem)
        return done


class Chain:

    def __init__(self, eng, sem, base=0):
        self.eng, self.sem, self.base, self.n = eng, sem, base, 0

    def __call__(self, ins):
        self.n += 1
        ins.then_inc(self.sem, 1)
        self.eng.wait_ge(self.sem, self.base + self.n)


def hold(eng, sem, value, held):
    eng.wait_ge(sem, value)
    eng.sem_inc(held, 1)


def flat(ap):
    return ap.rearrange("p a b -> p (a b)")


def at(t, i):
    if len(t.shape) == 3:
        return t[:, bass.ds(i, 1), :].rearrange("p o n -> p (o n)")
    return t[:, bass.ds(i, 1), :, :].rearrange("p o a n -> p (o a) n")


class Machine:

    def __init__(self, nc, ctx, ins):
        self.nc, self.ctx, self.ins = nc, ctx, ins
        self.xc = self.sb("x_channels", [P, B, N], F32)
        self.tt = self.xc[:].rearrange("p b (t c) -> p (b t) c", c=C)
        self.xnT = self.sb("normalised_channels", [P, B, N], F32)
        self.ident = self.sb("ident", [P, P], F32)
        self.identb = self.sb("identb", [P, P], BF16)
        self.sums_out, self.sums_in, self.inverse_out, self.inverse_in, self.gathered = (
            nc.alloc_semaphore(x) for x in ("sums_out", "sums_in", "inverse_out", "inverse_in", "gathered"))
        self.rounds = 0
        self.scattered, self.fetched = nc.alloc_semaphore("scattered"), [nc.alloc_semaphore(f"fetched{i}") for i in range(8)]

    def sb(self, name, shape, dt, ctx=None):
        return (ctx or self.ctx).enter_context(self.nc.sbuf_tensor(name, shape, dt))

    def psum(self, name, shape, ctx):
        return ctx.enter_context(self.nc.psum_tensor(f"{name}_bank", shape, F32))

    def sem(self, name, ctx):
        return ctx.semaphore(name)


def make_identities(m):
    nc = m.nc
    with Stage(nc) as ctx:
        zeroed, made, loaded = (m.sem(f"i_{x}", ctx) for x in ("zeroed", "made", "loaded"))
        block = ctx.enter_context(nc.Block())

        @block.sync
        def _(sp):
            sp.dma_start(m.xc[:], m.ins["x"].rearrange("b c h w -> c b (h w)")).then_inc(loaded, 16)
            sp.wait_ge(loaded, 16)

        @block.gpsimd
        def _(pool):
            pool.memset(m.ident[:], 0.0).then_inc(zeroed, 1)
            pool.memset(m.identb[:], 0.0).then_inc(zeroed, 1)
            pool.wait_ge(zeroed, 2)
            for one in (m.ident, m.identb):
                pool.affine_select(out=one[:], in_=one[:], compare_op=ALU.not_equal, fill=1.0, base=0,
                                   pattern=[[-1, P]], channel_multiplier=1).then_inc(made, 1)
            pool.wait_ge(made, 2)


def group_norm(m, name, out_of, eps=1e-5):
    nc = m.nc
    with Stage(nc) as ctx:
        sb = lambda n, s, dt=F32: m.sb(f"{name}_{n}", s, dt, ctx)
        group, stats, mv, moments = sb("group", [P, P]), sb("stats", [P, B * 2, 6]), sb("mv", [P, B, 2]), sb("moments", [P, 2, B])
        gm, rstd, tmp, epsb = sb("gm", [P, 2, B]), sb("rstd", [P, B]), sb("tmp", [P, B]), sb("eps", [P, 1])
        ps = m.psum(f"{name}_ps", [P, 2 * B], ctx)
        loaded, ready, summed, rooted, dve_step = (m.sem(f"{name}_{x}", ctx) for x in ("loaded", "ready", "summed", "rooted", "dve"))
        block = ctx.enter_context(nc.Block())

        @block.sync
        def _(sp):
            sp.dma_start(group[:], m.ins["c_group"]).then_inc(loaded, 16)

        @block.tensor
        def _(pe):
            pe.wait_ge(loaded, 16)
            pe.wait_ge(ready, 1)
            pe.matmul(ps[:], group[:], flat(moments[:]), start=True, stop=True).then_inc(summed, 1)

        @block.scalar
        def _(act):
            act.wait_ge(ready, 2)
            act.activation(tmp[:], rstd[:], ACT.Sqrt, bias=epsb[:]).then_inc(rooted, 1)

        @block.vector
        def _(dve):
            step = Chain(dve, dve_step)
            step(dve.memset(epsb[:], eps))
            for b in range(B):
                for h in range(2):
                    last = dve.bn_stats(stats[:, 2 * b + h, :], m.xc[:, b, h * 512:(h + 1) * 512])
            step(last)
            for b in range(B):
                last = dve.bn_aggr(mv[:, b, :], stats[:, 2 * b:2 * b + 2, :])
            step(last)
            step(dve.tensor_tensor(tmp[:], mv[:, :, 0], mv[:, :, 0], ALU.mult))
            step(dve.tensor_copy(moments[:, 0, :], mv[:, :, 0]))
            dve.tensor_tensor(moments[:, 1, :], mv[:, :, 1], tmp[:], ALU.add).then_inc(ready, 1)
            dve.wait_ge(summed, 1)
            step(dve.tensor_copy(flat(gm[:]), ps[:]))
            step(dve.tensor_tensor(tmp[:], gm[:, 0, :], gm[:, 0, :], ALU.mult))
            dve.tensor_tensor(rstd[:], gm[:, 1, :], tmp[:], ALU.subtract).then_inc(ready, 1)
            dve.wait_ge(rooted, 1)
            step(dve.reciprocal(rstd[:], tmp[:]))
            for b in range(B):
                src, dst = out_of(b)
                last = dve.tensor_scalar(dst, src, gm[:, 0, b:b + 1], rstd[:, b:b + 1], ALU.subtract, ALU.mult)
            step(last)


def token_norm(m, name, keep=None, collected=None, eps=1e-5):
    nc = m.nc
    G = 4
    GROUPS = TILES // G
    with Stage(nc) as ctx:
        sb = lambda n, s, dt=F32: m.sb(f"{name}_{n}", s, dt, ctx)
        xn = keep if keep is not None else sb("xn", [P, TILES, C])
        stats, mv = sb("stats", [P, TILES, 6]), sb("mv", [P, TILES, 2])
        root, rstd, epsb = sb("root", [P, TILES]), sb("rstd", [P, TILES]), sb("eps", [P, 1])
        got = sb("got", [P, TILES, 2, C]) if collected is not None else None
        ps = [m.psum(f"{name}_ps{i}", [P, G * P], ctx) for i in range(2)]
        added, spread, ready, rooted, normed, turned, taken, dve_step = (
            m.sem(f"{name}_{x}", ctx) for x in ("added", "spread", "ready", "rooted", "normed", "turned", "taken", "dve"))
        block = ctx.enter_context(nc.Block())

        @block.gpsimd
        def _(pool):
            if collected is not None:
                picks, routed = collected
                for t in range(TILES):
                    for i, slots in enumerate(picks.slots):
                        pool.indirect_dma_start(out=got[:, t, i, :], out_offset=None, in_=routed.y,
                                                in_offset=bass.IndirectOffsetOnAxis(ap=slots[:, t:t + 1], axis=0)).then_inc(m.fetched[t // G], 16)

        @block.vector
        def _(dve):
            step = Chain(dve, dve_step)
            step(dve.memset(epsb[:], eps))

            def add_experts(g):
                dve.wait_ge(m.fetched[g], 2 * G * 16)
                for i in range(2):
                    if i == 1:
                        dve.wait_ge(added, (2 * g + 1) * G)
                    for t in range(g * G, (g + 1) * G):
                        dve.scalar_tensor_tensor(out=m.tt[:, t, :], in0=got[:, t, i, :], scalar=collected[0].weight[:, t, i:i + 1], in1=m.tt[:, t, :],
                                                 op0=ALU.mult, op1=ALU.add).then_inc(added, 1)
                dve.wait_ge(added, (2 * g + 2) * G)

            for g in range(GROUPS + 1):
                if g < GROUPS:
                    if collected is not None:
                        add_experts(g)
                    tiles = range(g * G, (g + 1) * G)
                    for t in tiles:
                        dve.bn_stats(stats[:, t, :], m.tt[:, t, :]).then_inc(spread, 1)
                    dve.wait_ge(spread, G * (g + 1))
                    for t in tiles:
                        last = dve.bn_aggr(mv[:, t, :], stats[:, t, :])
                    last.then_inc(ready, 1)
                if g >= 1:
                    before = slice((g - 1) * G, g * G)
                    dve.wait_ge(rooted, g)
                    dve.wait_ge(ready, g)
                    step(dve.reciprocal(rstd[:, before], root[:, before]))
                    for t in range(before.start, before.stop):
                        dve.tensor_scalar(xn[:, t, :], m.tt[:, t, :], mv[:, t, 0:1], rstd[:, t:t + 1], ALU.subtract, ALU.mult).then_inc(normed, 1)

        @block.scalar
        def _(act):
            for g in range(GROUPS + 1):
                if g < GROUPS:
                    act.wait_ge(ready, g + 1)
                    act.activation(root[:, g * G:(g + 1) * G], mv[:, g * G:(g + 1) * G, 1], ACT.Sqrt, bias=epsb[:]).then_inc(rooted, 1)
                if g >= 1:
                    act.wait_ge(turned, g)
                    act.activation(m.xnT[:].rearrange("p b n -> p (b n)")[:, (g - 1) * G * P:g * G * P], ps[(g - 1) % 2][:], ACT.Copy).then_inc(taken, 1)
            act.wait_ge(taken, GROUPS)

        @block.tensor
        def _(pe):
            for g in range(GROUPS):
                if g >= 2:
                    pe.wait_ge(taken, g - 1)
                pe.wait_ge(normed, G * (g + 1))
                for t in range(G):
                    last = pe.transpose(ps[g % 2][:, t * P:(t + 1) * P], xn[:, g * G + t, :], m.ident[:])
                last.then_inc(turned, 1)


def one_head_attention(m, name, wq, wk, wv, bq, bk, bv, scale, causal, routed=None):
    nc = m.nc
    T = N // P
    with Stage(nc) as ctx:
        sb = lambda n, s, dt=F32: m.sb(f"{name}_{n}", s, dt, ctx)
        w = sb("w", [P, 3, C])
        bqk, bvb = sb("bqk", [P, 2]), sb("bvb", [P, C])
        xs, q, k, v = sb("xs", [P, N]), sb("q", [P, N]), sb("k", [P, N]), sb("v", [P, T, C])
        neg, rows, inv = sb("neg", [P, T]), sb("rows", [P, T]), sb("inv", [P, T])
        prob, probT = [sb(f"prob{i}", [P, N]) for i in range(2)], [sb(f"probT{i}", [P, T, P]) for i in range(2)]
        out = [sb(f"out{i}", [P, C]) for i in range(2)]
        tril = sb("tril", [P, P]) if causal else None
        s_ps = [m.psum(f"{name}_s{i}", [P, N], ctx) for i in range(2)]
        t_ps = m.psum(f"{name}_t", [P, T, P], ctx)
        o_ps = m.psum(f"{name}_o", [P, 512], ctx)
        r_ps = m.psum(f"{name}_r", [P, 512], ctx)
        names = ("loaded", "staged", "qk_made", "v_made", "qk_kept", "v_kept", "scored", "maxed", "exped", "masked", "turned", "turn_kept",
                 "mixed", "inverted", "scaled", "out_turned", "added", "dve", "held")
        S = {x: m.sem(f"{name}_{x}", ctx) for x in names}
        zeros = sb("zeros", [P, STEP_TILES * C]) if routed else None
        zeroed, cleared = m.sem(f"{name}_zeroed", ctx), m.sem(f"{name}_cleared", ctx)
        block = ctx.enter_context(nc.Block())
        width = lambda t: (t + 1) * P if causal else N

        @block.sync
        def _(sp):
            for i, x in enumerate((wq, wk, wv)):
                sp.dma_start(w[:, i, :], x).then_inc(S["loaded"], 16)
            if not causal:
                sp.dma_start(bqk[:, 0:1], bq.rearrange("(c o) -> c o", o=1)).then_inc(S["loaded"], 16)
                sp.dma_start(bqk[:, 1:2], bk.rearrange("(c o) -> c o", o=1)).then_inc(S["loaded"], 16)
                sp.dma_start(bvb[:], bv.rearrange("(o c) -> o c", o=1).broadcast_to((P, C))).then_inc(S["loaded"], 16)
            else:
                sp.dma_start(tril[:], m.ins["c_tril"]).then_inc(S["loaded"], 16)
            sp.wait_ge(S["loaded"], 16 * (4 if causal else 6))
            if routed:
                clear_routed(sp, None, routed, zeros, zeroed, cleared)

        @block.gpsimd
        def _(pool):
            if routed:
                clear_routed(None, pool, routed, zeros, zeroed, cleared)
            pool.tensor_copy(xs[:], m.xnT[:, 0, :]).then_inc(S["staged"], 1)
            with pool.Fori(0, B - 1) as b:
                hold(pool, S["v_made"], b + 1, S["held"])
                pool.tensor_copy(xs[:], at(m.xnT, b + 1)).then_inc(S["staged"], 1)

        @block.tensor
        def _(pe):
            pe.wait_ge(S["loaded"], 16 * (4 if causal else 6))
            def project(b, i):
                pe.wait_ge(S["staged"], b + 1)
                if not isinstance(b, int) or b > 0:
                    pe.wait_ge(S["exped"], b * T - 1 + i)
                    if causal:
                        pe.wait_ge(S["masked"], b * T - 1 + i)
                for h in range(2):
                    last = pe.matmul(s_ps[i][:, h * 512:(h + 1) * 512], w[:, i, :], xs[:, h * 512:(h + 1) * 512], start=True, stop=True)
                last.then_inc(S["qk_made"], 1)

            def values(b):
                if not isinstance(b, int) or b > 0:
                    pe.wait_ge(S["turn_kept"], b * T)
                for t in range(T):
                    last = pe.matmul(t_ps[:, t, :], xs[:, t * P:(t + 1) * P], w[:, 2, :], start=True, stop=True)
                last.then_inc(S["v_made"], 1)

            def attend(b, further):
                pe.wait_ge(S["qk_kept"], 2 * b + 2)

                def scores(t):
                    if t >= 2:
                        pe.wait_ge(S["exped"], b * T + t - 1)
                        if causal:
                            pe.wait_ge(S["masked"], b * T + t - 1)
                    for h in range(2):
                        last = pe.matmul(s_ps[t % 2][:, h * 512:(h + 1) * 512], q[:, t * P:(t + 1) * P], k[:, h * 512:(h + 1) * 512], start=True, stop=True)
                    last.then_inc(S["scored"], 1)

                def out_turn(t):
                    pe.wait_ge(S["scaled"], b * T + t + 1)
                    if t >= 1:
                        pe.wait_ge(S["added"], b * T + t)
                    pe.transpose(r_ps[:, 0:P], out[t % 2][:], m.ident[:]).then_inc(S["out_turned"], 1)

                def mix(t):
                    pe.wait_ge(S["turn_kept"], b * T + t + 1)
                    if t >= 1:
                        pe.wait_ge(S["added" if causal else "scaled"], b * T + t)
                    n = width(t) // P
                    for j in range(n):
                        last = pe.matmul(o_ps[:, 0:C], probT[t % 2][:, j, :], v[:, j, :], start=(j == 0), stop=(j == n - 1))
                    last.then_inc(S["mixed"], 1)

                scores(0)
                scores(1)
                pe.wait_ge(S["v_kept"], b + 1)
                for t in range(T):
                    pe.wait_ge(S["masked" if causal else "exped"], b * T + t + 1)
                    if t >= 1:
                        pe.wait_ge(S["turn_kept"], b * T + t)
                    for j in range(width(t) // P):
                        last = pe.transpose(t_ps[:, j, :], prob[t % 2][:, j * P:(j + 1) * P], m.ident[:])
                    last.then_inc(S["turned"], 1)
                    if t + 2 < T:
                        scores(t + 2)
                    elif further:
                        project(b + 1, t + 2 - T)
                    mix(t)
                    if not causal and t >= 1:
                        out_turn(t - 1)
                if not causal:
                    out_turn(T - 1)
                if further:
                    values(b + 1)

            project(0, 0)
            project(0, 1)
            values(0)
            with pe.Fori(0, B - 1) as b:
                attend(b, True)
            attend(B - 1, False)

        @block.scalar
        def _(act):
            act.wait_ge(S["loaded"], 16 * (4 if causal else 6))
            def scale_out(b, t):
                act.wait_ge(S["mixed"], b * T + t + 1)
                act.wait_ge(S["inverted"], b * T + t + 1)
                if t >= 2:
                    act.wait_ge(S["out_turned"], b * T + t - 1)
                act.activation(out[t % 2][:], o_ps[:, 0:C], ACT.Copy, scale=inv[:, t:t + 1]).then_inc(S["scaled"], 1)

            def keep_turned(b, t):
                act.wait_ge(S["turned"], b * T + t + 1)
                if t >= 2:
                    act.wait_ge(S["mixed"], b * T + t - 1)
                act.activation(probT[t % 2][:, 0:width(t) // P, :], t_ps[:, 0:width(t) // P, :], ACT.Copy).then_inc(S["turn_kept"], 1)

            def keep_projection(b, i):
                to = (q, k)[i]
                act.wait_ge(S["qk_made"], 2 * b + 1 + i)
                if causal:
                    act.activation(to[:], s_ps[i][:], ACT.Copy).then_inc(S["qk_kept"], 1)
                else:
                    act.activation(to[:], s_ps[i][:], ACT.Identity, bias=bqk[:, i:i + 1]).then_inc(S["qk_kept"], 1)

            def attend(b, further):
                def exponentials(t):
                    act.wait_ge(S["maxed"], b * T + t + 1)
                    if t >= 2:
                        act.wait_ge(S["turned"], b * T + t - 1)
                    if causal:
                        act.activation(prob[t % 2][:, 0:width(t)], s_ps[t % 2][:, 0:width(t)], ACT.Exp, bias=neg[:, t:t + 1], scale=scale).then_inc(S["exped"], 1)
                    else:
                        act.activation(prob[t % 2][:], s_ps[t % 2][:], ACT.Exp, bias=neg[:, t:t + 1], accum_out=rows[:, t:t + 1]).then_inc(S["exped"], 1)

                exponentials(0)
                exponentials(1)
                for t in range(T):
                    if causal:
                        keep_turned(b, t)
                    if t + 2 < T:
                        exponentials(t + 2)
                    elif further:
                        keep_projection(b + 1, t + 2 - T)
                    if not causal:
                        scale_out(b, t)

            keep_projection(0, 0)
            keep_projection(0, 1)
            with act.Fori(0, B - 1) as b:
                attend(b, True)
            attend(B - 1, False)

        @block.vector
        def _(dve):
            dve.wait_ge(S["loaded"], 16 * (4 if causal else 6))
            def add_turned(b, t):
                dve.wait_ge(S["out_turned"], b * T + t + 1)
                tile = at(m.xc, b)[:, t * P:(t + 1) * P]
                dve.tensor_tensor(tile, r_ps[:, 0:P], tile, ALU.add).then_inc(S["added"], 1)

            PER = T * 4 if causal else 0
            with dve.Fori(0, B) as b:
                step = Chain(dve, S["dve"], b * PER)
                dve.wait_ge(S["v_made"], b + 1)
                if causal:
                    dve.tensor_copy(v[:], t_ps[:]).then_inc(S["v_kept"], 1)
                else:
                    dve.tensor_tensor(v[:], t_ps[:], bvb[:].rearrange("p (o c) -> p o c", o=1).broadcast_to((P, T, C)), ALU.add).then_inc(S["v_kept"], 1)

                def maximum(t):
                    dve.wait_ge(S["scored"], b * T + t + 1)
                    if causal:
                        step(dve.tensor_reduce(neg[:, t:t + 1], s_ps[t % 2][:], AX.X, ALU.max))
                        dve.tensor_scalar(neg[:, t:t + 1], neg[:, t:t + 1], -scale, None, ALU.mult).then_inc(S["maxed"], 1)
                    else:
                        dve.tensor_reduce(neg[:, t:t + 1], s_ps[t % 2][:], AX.X, ALU.max, negate=True).then_inc(S["maxed"], 1)

                def add_output(t):
                    dve.wait_ge(S["mixed"], b * T + t + 1)
                    tile = at(m.xc, b)[:, t * C:(t + 1) * C]
                    dve.scalar_tensor_tensor(out=tile, in0=o_ps[:, 0:C], scalar=inv[:, t:t + 1], in1=tile, op0=ALU.mult,
                                             op1=ALU.add).then_inc(S["added"], 1)

                def mask(t):
                    dve.wait_ge(S["exped"], b * T + t + 1)
                    pr, n = prob[t % 2], width(t)
                    step(dve.tensor_tensor(pr[:, n - P:n], pr[:, n - P:n], tril[:], ALU.mult))
                    dve.scalar_tensor_tensor(out=pr[:, 0:n], in0=s_ps[t % 2][:, 0:n], scalar=0.0, in1=pr[:, 0:n], op0=ALU.not_equal,
                                             op1=ALU.mult, accum_out=rows[:, t:t + 1]).then_inc(S["masked"], 1)

                def invert(t):
                    if causal:
                        dve.wait_ge(S["masked"], b * T + t + 1)
                        step(dve.tensor_scalar(inv[:, t:t + 1], rows[:, t:t + 1], 1e-9, None, ALU.add))
                        step(dve.reciprocal(inv[:, t:t + 1], inv[:, t:t + 1]))
                    else:
                        dve.reciprocal(inv[:, t:t + 1], rows[:, t:t + 1]).then_inc(S["inverted"], 1)

                maximum(0)
                maximum(1)
                if causal:
                    mask(0)
                for t in range(T):
                    if causal and t + 1 < T:
                        mask(t + 1)
                    if not causal:
                        dve.wait_ge(S["turned"], b * T + t + 1)
                        if t >= 2:
                            dve.wait_ge(S["mixed"], b * T + t - 1)
                        dve.tensor_copy(probT[t % 2][:], t_ps[:]).then_inc(S["turn_kept"], 1)
                    if t + 2 < T:
                        maximum(t + 2)
                    invert(t)
                    if causal:
                        add_output(t)
                    elif t >= 2:
                        add_turned(b, t - 2)
                if not causal:
                    for t in range(T - 2, T):
                        add_turned(b, t)
                assert step.n == PER, step.n



def turn_activations(m, name, out=None):
    nc = m.nc
    G = 4
    with Stage(nc) as ctx:
        ps = [m.psum(f"{name}_ps{i}", [P, G * P], ctx) for i in range(4)]
        turned, taken, stored = (m.sem(f"{name}_{x}", ctx) for x in ("turned", "taken", "stored"))
        block = ctx.enter_context(nc.Block())
        flat_x = m.xc[:].rearrange("p b n -> p (b n)")
        GROUPS = TILES // G

        @block.tensor
        def _(pe):
            for g in range(GROUPS):
                if g >= 4:
                    pe.wait_ge(taken, g - 3)
                for t in range(G):
                    last = pe.transpose(ps[g % 4][:, t * P:(t + 1) * P], m.tt[:, g * G + t, :], m.ident[:])
                last.then_inc(turned, 1)

        @block.vector
        def _(dve):
            for g in range(GROUPS):
                dve.wait_ge(turned, g + 1)
                dve.tensor_copy(flat_x[:, g * G * P:(g + 1) * G * P], ps[g % 4][:]).then_inc(taken, 1)

        if out is not None:
            @block.sync
            def _(sp):
                for b in range(B):
                    sp.wait_ge(taken, (b + 1) * GROUPS // B)
                    sp.dma_start(out[b].rearrange("c h w -> c (h w)"), m.xc[:, b, :]).then_inc(stored, 16)
                sp.wait_ge(stored, B * 16)


class HeadScratch:

    def __init__(self, nc, name, n):
        self.together = n <= 256
        shape = [3, P, B, n] if self.together else [B, 3, P, n]
        self.q, self.k = (nc.dram_tensor(f"{name}_{x}_parts", shape, BF16, kind="Internal").ap() for x in "qk")
        self.v = nc.dram_tensor(f"{name}_v", [B, min(P, n), n // min(P, n), HEADS * SLOT], F32, kind="Internal").ap()

    def batch(self, dram, b):
        return dram.rearrange("l c b n -> l c (b n)") if self.together else dram[b]


def split_in_three(eng, step, parts, x, rest):
    step(eng.tensor_copy(parts[:, 0], x))
    step(eng.tensor_tensor(rest, x, parts[:, 0], ALU.subtract))
    step(eng.tensor_copy(parts[:, 1], rest))
    return eng.tensor_tensor(parts[:, 2], rest, parts[:, 1], ALU.subtract)


def many_heads_attention(m, name, n, scratch, out, scale, bias_parts=None, ahead=None):
    nc = m.nc
    TN, CH = min(P, n), min(512, n)
    T, NH, NC = n // TN, n // CH, n // CH
    KB = STACK + (3 if bias_parts is not None else 0)
    KM = KB + 3
    whole = scratch.together
    NBUF = B if whole else 1
    LB = min(B, 512 // n) if whole else 1
    CPB, TQ = 2 * NH, CH // TN
    UC = 4 * TQ
    R, SLOTS = UC // T, CPB * T
    LAG = T + (6 if whole else 2)
    NUSES = CPB * (UC + 1)
    LOADS = 2 * len(Q_PART) * 16
    assert NUSES % 2 == 0 and SLOTS * 4 % 8 == 0
    NROW = B * CPB if whole else CPB
    SUMS = 4 * n // P
    with Stage(nc) as ctx:
        sb = lambda nm, s, dt=F32: m.sb(f"{name}_{nm}", s, dt, ctx)
        qs, ks = (sb(x, [P, 8 * NBUF * n], BF16) for x in ("qs", "ks"))
        vs = sb("vs", [TN, B if whole else 1, T, 8 * SLOT])
        prob = [sb(f"prob{i}", [TN, CH]) for i in range(8)]
        mx, mrest, mparts = sb("mx", [TN, UC]), sb("mrest", [TN, UC]), sb("mparts", [TN, 3, UC], BF16)
        mrows = [sb(f"mrows{c}", [UC, 3, TN], BF16) for c in range(NROW)]
        if whole:
            wide = [sb("wide", [P, 2 * n])]
        else:
            spread, inverse, wide = sb("spread", [P, SUMS]), sb("inverse", [P, SUMS]), [sb(f"wide{i}", [P, n]) for i in range(2)]
            sums_dram = nc.dram_tensor(f"{name}_sums_d", [4, n], F32, kind="Internal").ap()
            inverse_dram = nc.dram_tensor(f"{name}_inverse_d", [4, n], F32, kind="Internal").ap()
        n_ps = [m.psum(f"{name}_n{i}", [P, 1024], ctx) for i in range(2)]
        t_ps = [m.psum(f"{name}_t{i}", [P, 512], ctx) for i in range(3)]
        o_ps = m.psum(f"{name}_o", [P, 512], ctx)
        cleared, biased = m.sem(f"{name}_cleared", ctx), m.sem(f"{name}_biased", ctx)
        qk_loaded = [m.sem(f"{name}_qk_loaded{s}", ctx) for s in range(B // LB if whole else 2)]
        v_loaded = [m.sem(f"{name}_v_loaded{i}", ctx) for i in range(B // LB if whole else 2)]
        row_loaded = [m.sem(f"{name}_row_loaded{c}", ctx) for c in range(NROW)]
        first_made, first_used, rows_ready, rows_made = (m.sem(f"{name}_{x}", ctx) for x in ("first_made", "first_used", "rows_ready", "rows_made"))
        scored, exped, mixed, kept, dve_step = (m.sem(f"{name}_{x}", ctx) for x in ("scored", "exped", "mixed", "kept", "dve"))
        held, held_pe, held_dve, norm_step = (m.sem(f"{name}_{x}", ctx) for x in ("held", "held_pe", "held_dve", "norm"))
        inverted, divided = m.sem(f"{name}_inverted", ctx), m.sem(f"{name}_divided", ctx)
        sums_out, sums_in, inverse_out, inverse_in, rounds = m.sums_out, m.sums_in, m.inverse_out, m.inverse_in, m.rounds
        zeroed, ahead_loaded = m.sem(f"{name}_zeroed", ctx), m.sem(f"{name}_ahead_loaded", ctx)
        if not whole:
            m.rounds += 2 * B - 1
        block = ctx.enter_context(nc.Block())

        def query(b, rows, s, h, j, start, size):
            off = (((s * NH + h) * 4 + j) * NBUF + (b if whole else 0)) * CH + start
            return qs[rows, off:off + size]

        def key(b, rows, s, j, start, size):
            off = ((4 * s + j) * NBUF + (b if whole else 0)) * n + start
            return ks[rows, off:off + size]

        def behind(b, k, lag):
            back, place = divmod(k - lag, SLOTS)
            if isinstance(b, int) and not 0 <= b + back < B:
                return None, place
            return b + back, place

        def over(b):
            return isinstance(b, int) and b == B

        def first_use(b):
            return (0, 0) if isinstance(b, int) and b == 0 else (b * NUSES - 1, 1)

        def over_batches(eng, emit):
            emit(0, SLOTS)
            if whole:
                for b in range(1, B):
                    emit(b, SLOTS)
            else:
                with eng.Fori(1, B) as b:
                    emit(b, SLOTS)
            emit(B, LAG + (1 if whole else 4))

        def score_bank(b, place, j):
            if whole:
                return (4 * (b * SLOTS + place) + j) % 3, 3
            q, per = 4 * place + j, 4 * SLOTS
            return q % 3, (3 if q >= 3 else per + q - max(x for x in range(per) if x % 3 == q % 3))

        @block.sync
        def _(sp):
            def load_qk(b, s, loaded):
                for parts, dram, slots in ((qs, scratch.q, Q_PART), (ks, scratch.k, K_PART)):
                    for slot, level in enumerate(slots):
                        rows = slice(slot * HD, (slot + 1) * HD)
                        if whole:
                            to = parts[rows, :].rearrange("r (g n) -> r g n", g=8)[:, :, b * n:(b + LB) * n]
                            src = dram[level].rearrange("(g r) b n -> r g (b n)", r=HD)[:, :, b * n:(b + LB) * n]
                        else:
                            to, src = parts[rows, 4 * s * n:4 * (s + 1) * n], dram[b, level].rearrange("(g r) n -> r g n", r=HD)[:, 4 * s:4 * (s + 1), :]
                            if parts is qs:
                                to, src = to.rearrange("r (c j n) -> r c j n", c=NH, j=4), src.rearrange("r j (c n) -> r c j n", c=NH)
                            else:
                                to = to.rearrange("r (j n) -> r j n", j=4)
                        sp.dma_start(to, src).then_inc(loaded, 16)

            def load_v(b, s):
                if whole:
                    sp.dma_start(vs[:, b:b + LB], scratch.v[b:b + LB].rearrange("b p t c -> p b t c")).then_inc(v_loaded[b // LB], 16)
                else:
                    cols = slice(s * 4 * SLOT, (s + 1) * 4 * SLOT)
                    sp.dma_start(vs[:, 0, :, cols], scratch.v[b, :, :, cols]).then_inc(v_loaded[s], 16)

            def rows(b, c):
                sp.wait_ge(rows_made, b * CPB + c + 1)
                r = (b * CPB + c) % NROW
                for part in range(3):
                    if whole:
                        to = qs[KB + part:KB + part + 1, :].rearrange("o (g n) -> o g n", g=8)[:, 4 * c:4 * c + 4, b * n:(b + 1) * n]
                        for t in range(TQ):
                            sp.dma_start(to[:, :, t * TN:(t + 1) * TN], mrows[r][t:UC:TQ, part, :]).then_inc(row_loaded[r], 16)
                    else:
                        sp.dma_start(qs[KB + part:KB + part + 1, c * 4 * CH:(c + 1) * 4 * CH].rearrange("o (u q) -> o u q", q=TN),
                                     mrows[r][:, part, :]).then_inc(row_loaded[r], 16)

            if whole:
                for b in range(0, B, LB):
                    load_qk(b, None, qk_loaded[b // LB])
                    load_v(b, None)
                sp.wait_ge(cleared, 2)
                for b in range(B):
                    for c in range(CPB):
                        rows(b, c)
            else:
                for s in range(2):
                    load_qk(0, s, qk_loaded[s])
                    if s == 0:
                        sp.wait_ge(cleared, 2)
                        if bias_parts is not None:
                            sp.dma_start(ks[STACK:KB, :], bias_parts.rearrange("l h n -> l (h n)")).then_inc(biased, 16)
                    load_v(0, s)
                for g in range(2 * B):
                    b, s = g // 2, g % 2
                    rows(b, s * NH)
                    if 1 <= g < 2 * B - 1:
                        sp.wait_ge(scored, 4 * g * NH * T)
                        load_qk((g + 1) // 2, (g + 1) % 2, qk_loaded[(g + 1) % 2])
                    for h in range(1, NH):
                        rows(b, s * NH + h)
                    if 1 <= g < 2 * B - 1:
                        sp.wait_ge(kept, g * NH)
                        load_v((g + 1) // 2, (g + 1) % 2)
            if ahead is not None:
                ahead.load(sp, zeroed, ahead_loaded)

        @block.tensor
        def _(pe):
            if bias_parts is not None:
                pe.wait_ge(biased, 16)

            def wait(sem, value):
                if isinstance(value, int) and value <= 0:
                    return
                if TN < P:
                    hold(pe, sem, value, held_pe)
                else:
                    pe.wait_ge(sem, value)

            def emit(b, slots):
                done = first_use(b)
                uses = [0]

                def bank():
                    wait(first_used, done[0] + uses[0] - 1)
                    uses[0] += 1
                    return n_ps[(done[1] + uses[0] - 1) % 2]

                def first_pass(u):
                    c, j, t = u // UC, u % UC // TQ, u % TQ
                    s, h = c // NH, c % NH
                    if whole and u == 0:
                        wait(qk_loaded[b // LB], LOADS)
                    elif not whole and u % (NH * UC) == 0:
                        wait(qk_loaded[s], (b + 1) * LOADS)
                    ps = bank()
                    for i in range(NC):
                        last = pe.matmul(ps[0:TN, i * CH:(i + 1) * CH], query(b, slice(0, KB), s, h, j, t * TN, TN), key(b, slice(0, KB), s, j, i * CH, CH), start=True, stop=True)
                    last.then_inc(first_made, 1)

                def turn_maxima(of, c):
                    wait(rows_ready, of * CPB + c + 1)
                    ps = bank()[:].bitcast(BF16)
                    for part in range(3):
                        last = pe.transpose(ps[0:UC, part * TN:(part + 1) * TN], mparts[:, part, :], m.identb[0:TN, 0:TN])
                    last.then_inc(first_made, 1)

                def second_pass(of, place, heads):
                    c, t = place // T, place % T
                    if t == 0 and 0 in heads:
                        wait(row_loaded[of * CPB + c if whole else c], 48 * TQ if whole else (of + 1) * 48)
                    for j in heads:
                        i, back = score_bank(of, place, j)
                        wait(exped, 4 * (of * SLOTS + place) + j + 1 - back)
                        pe.matmul(t_ps[i][0:TN, 0:CH], key(of, slice(0, KM), c // NH, j, t * TN, TN), query(of, slice(0, KM), c // NH, c % NH, j, 0, CH), start=True, stop=True).then_inc(scored, 1)

                def mix(of, place):
                    c, t = place // T, place % T
                    s = c // NH
                    if place % (NH * T) == 0:
                        wait(v_loaded[of // LB if whole else s], 16 if whole else (of + 1) * 16)
                    if t == 0:
                        wait(kept, of * CPB + c)
                    wait(exped, 4 * (of * SLOTS + place + 1))
                    for j in range(4):
                        i = (4 * (of * SLOTS if whole else 0) + 4 * place + j) % 8
                        last = pe.matmul(o_ps[SLOT * j:SLOT * (j + 1), 0:CH], vs[:, of if whole else 0, t, (4 * s + j) * SLOT:(4 * s + j + 1) * SLOT], prob[i][:], start=(t == 0), stop=(t == T - 1))
                    last.then_inc(mixed, 1)

                for k in range(slots):
                    units = range(R * k, R * (k + 1)) if not over(b) else ()
                    of, place = behind(b, k, LAG)
                    for u in units[:R // 2]:
                        first_pass(u)
                    if of is not None:
                        second_pass(of, place, (0, 1))
                    for u in units[R // 2:]:
                        first_pass(u)
                    turned, at_ = behind(b, k, 1)
                    if at_ % T == T - 1 and turned is not None:
                        turn_maxima(turned, at_ // T)
                    if of is not None:
                        second_pass(of, place, (2, 3))
                    of, place = behind(b, k, LAG + 1)
                    if of is not None:
                        mix(of, place)

            over_batches(pe, emit)

        @block.gpsimd
        def _(pool):
            for rows in (qs, ks):
                pool.memset(rows[STACK:KM, :].bitcast(F32), TWO_ONES).then_inc(cleared, 1)
            if ahead is not None:
                pool.wait_ge(cleared, 2)
                ahead.clear(pool, zeroed)
            if not whole:
                def divide_half(b, s):
                    done = 2 * b + s + 1
                    half = out[:, s, bass.ds(b, 1), :].rearrange("p o n -> p (o n)")
                    hold(pool, kept, b * CPB + (s + 1) * NH, held)
                    pool.dma_start(sums_dram, out[HD:P:SLOT, s, bass.ds(b, 1), :].rearrange("p o n -> p (o n)")).then_inc(sums_out, 16)
                    hold(pool, sums_out, (rounds + done) * 16, held)
                    pool.dma_start(spread[:], sums_dram.rearrange("h (c q) -> (h c) q", q=SUMS)).then_inc(sums_in, 16)
                    hold(pool, inverted, done, held)
                    pool.dma_start(inverse_dram.rearrange("h (c q) -> (h c) q", q=SUMS), inverse[:]).then_inc(inverse_out, 16)
                    hold(pool, inverse_out, (rounds + done) * 16, held)
                    pool.dma_start(wide[s][:], inverse_dram.rearrange("h (o n) -> h o n", o=1).broadcast_to((4, SLOT, n))).then_inc(inverse_in, 16)
                    hold(pool, inverse_in, (rounds + done) * 16, held)
                    pool.tensor_tensor(half, half, wide[s][:], ALU.mult).then_inc(divided, 1)
                    hold(pool, divided, done, held)

                with pool.Fori(0, B - 1) as b:
                    for s in range(2):
                        divide_half(b, s)
                divide_half(B - 1, 0)

        @block.scalar
        def _(act):
            def emit(b, slots):
                for k in range(slots):
                    of, place = behind(b, k, LAG)
                    if of is None:
                        continue
                    group = of * SLOTS + place
                    if not isinstance(group, int) or group >= 2:
                        act.wait_ge(mixed, group - 1)
                    for j in range(4):
                        act.wait_ge(scored, 4 * group + j + 1)
                        to = prob[(4 * (group if whole else place) + j) % 8]
                        act.activation(to[:], t_ps[score_bank(of, place, j)[0]][0:TN, 0:CH], ACT.Exp, scale=scale).then_inc(exped, 1)

            over_batches(act, emit)

        @block.vector
        def _(dve):
            def emit(b, slots):
                step = Chain(dve, dve_step, b * CPB * 3)
                done = first_use(b)
                uses = [0]

                def bank():
                    dve.wait_ge(first_made, done[0] + uses[0] + 1)
                    uses[0] += 1
                    return n_ps[(done[1] + uses[0] - 1) % 2]

                def maximum(u):
                    dve.tensor_reduce(mx[:, u % UC:u % UC + 1], bank()[0:TN, 0:n], AX.X, ALU.max, negate=True).then_inc(first_used, 1)

                def rows_of(c):
                    dve.wait_ge(first_used, done[0] + uses[0])
                    split_in_three(dve, step, mparts[:], mx[:], mrest[:]).then_inc(rows_ready, 1)
                    dve.wait_ge(rows_ready, b * CPB + c + 1)

                def keep_rows(of, c):
                    ps = bank()[:].bitcast(BF16)
                    dve.tensor_copy(mrows[(of * CPB + c if whole else c) % NROW][:].rearrange("a b c -> a (b c)"), ps[0:UC, 0:3 * TN]).then_inc(first_used, 1)
                    dve.wait_ge(first_used, done[0] + uses[0])
                    dve.sem_inc(rows_made, 1)

                def keep_output(of, c):
                    s, h = c // NH, c % NH
                    dve.wait_ge(mixed, of * SLOTS + (c + 1) * T)
                    to = out[:, s, bass.ds(of, 1), h * CH:(h + 1) * CH].rearrange("p o n -> p (o n)")
                    dve.tensor_copy(to, o_ps[:, 0:CH]).then_inc(kept, 1)

                def divide(of):
                    hold(dve, kept, (of + 1) * CPB, held_dve)
                    batch = out[:, :, of, :]
                    sums = wide[0][:].rearrange("p (s n) -> p s n", s=2)
                    normed = Chain(dve, norm_step, 4 * of)
                    for s in range(2):
                        last = dve.stream_shuffle(sums[:, s], batch[:, s], [HD + r % HD for r in range(SLOT)])
                        if s == 0:
                            normed(last)
                    hold(dve, norm_step, 4 * of + 1, held_dve)
                    normed(last)
                    normed(dve.reciprocal(wide[0][:], wide[0][:]))
                    normed(dve.tensor_tensor(batch, batch, sums, ALU.mult))

                def divide_chunk(of, c):
                    s, h = c // NH, c % NH
                    hold(dve, kept, of * CPB + c + 1, held_dve)
                    part, sums = out[:, s, of, h * CH:(h + 1) * CH], wide[1][:, 0:CH]
                    normed = Chain(dve, norm_step, 3 * h)
                    normed(dve.stream_shuffle(sums, part, [HD + r % HD for r in range(SLOT)]))
                    normed(dve.reciprocal(sums, sums))
                    normed(dve.tensor_tensor(part, part, sums, ALU.mult))

                def invert(of, s):
                    dve.wait_ge(sums_in, (rounds + 2 * of + s + 1) * 16)
                    dve.reciprocal(inverse[:], spread[:]).then_inc(inverted, 1)

                for k in range(slots):
                    if not over(b):
                        for u in range(R * k, R * (k + 1)):
                            maximum(u)
                    turned, place = behind(b, k, 1)
                    if place % T == T - 1 and turned is not None:
                        keep_rows(turned, place // T)
                    if not over(b) and k % T == T - 1:
                        rows_of(k // T)
                    of, place = behind(b, k, LAG + 1)
                    if of is not None and place % T == T - 1:
                        keep_output(of, place // T)
                        if whole and place == SLOTS - 1:
                            divide(of)
                        if not whole and over(b) and place // T >= NH:
                            divide_chunk(of, place // T)
                    if not whole:
                        of, place = behind(b, k, LAG + 4)
                        last_half = over(b) and place == SLOTS - 1
                        if of is not None and place % (NH * T) == NH * T - 1 and not last_half:
                            invert(of, place // (NH * T))

            over_batches(dve, emit)


def head_inputs(m, name, n, scratch, wq, wk, wv, bq, bk, bv, k_scale=1.0, padded=None, taps=None):
    nc = m.nc
    TN, size = min(P, n), int(n ** 0.5)
    together = scratch.together
    rounds = 1 if together else B
    one, room = n, n
    if together:
        room = (size + 2) * size
        n = B * n
    CH = min(512, n)
    T, NC = n // TN, n // CH
    with Stage(nc) as ctx:
        sb = lambda nm, s, dt=F32: m.sb(f"{name}_{nm}", s, dt, ctx)
        src, pos, shared, sums = (sb(x, [P, n // one * room]) if taps is not None or x == "src" else None for x in ("src", "pos", "shared", "tap_sums"))
        wqk, wvp, bqk, bvp = sb("wqk", [P, 2, C]), sb("wvp", [P, 8, SLOT]), sb("bqk", [P, 2]), sb("bvp", [P, 8, SLOT])
        v = sb("values", [TN, 2, T * HEADS * SLOT])
        SHARED = 5
        OWN = 9 - SHARED
        product = [sb(f"product{i}", [P, n // one * room]) if taps is not None else None for i in range(2)]
        tapped, pos_made, shared_added, pos_added = (m.sem(f"{name}_{z}", ctx) for z in ("tapped", "pos_made", "shared_added", "pos_added"))
        x, rest, parts = [sb(f"x{i}", [P, n]) for i in range(2)], [sb(f"rest{i}", [P, n]) for i in range(2)], [sb(f"parts{i}", [P, 2, 3 * n], BF16) for i in range(2)]
        qk_ps = [m.psum(f"{name}_p{i}", [P, 1024], ctx) for i in range(2)]
        v_ps = m.psum(f"{name}_v", [P, 2048], ctx)
        zeroed, loaded, staged, qk_made, v_made, qk_kept, taken, cast, left, split, stored = (
            m.sem(f"{name}_{z}", ctx) for z in ("zeroed", "loaded", "staged", "qk_made", "v_made", "qk_kept", "taken", "cast", "left", "split", "stored"))
        held = m.sem(f"{name}_held", ctx)
        block = ctx.enter_context(nc.Block())
        column = lambda a: a.rearrange("(c o) -> c o", o=1)

        @block.sync
        def _(sp):
            sp.dma_start(wqk[:, 0, :], wq).then_inc(loaded, 16)
            sp.dma_start(wqk[:, 1, :], wk).then_inc(loaded, 16)
            sp.dma_start(bqk[:, 0:1], column(bq)).then_inc(loaded, 16)
            sp.dma_start(bqk[:, 1:2], column(bk)).then_inc(loaded, 16)
            sp.wait_ge(zeroed, 2)
            sp.dma_start(wvp[:, :, 0:HD], wv.rearrange("c (h d) -> c h d", d=HD)).then_inc(loaded, 16)
            sp.dma_start(bvp[:, :, 0:HD], bv.rearrange("(o h d) -> o h d", o=1, d=HD).broadcast_to((P, HEADS, HD))).then_inc(loaded, 16)
            for b in range(rounds):
                sp.wait_ge(stored, b * 48 + 96)
                for i, dram in enumerate((scratch.q, scratch.k)):
                    sp.wait_ge(split, 2 * b + i + 1)
                    sp.dma_start(scratch.batch(dram, b).rearrange("l p n -> p l n"), parts[i][:, b % 2, :].rearrange("p (l n) -> p l n", l=3)).then_inc(stored, 16)
                sp.wait_ge(taken, b + 2)
                to, values = (scratch.v.rearrange("b p t c -> p b (t c)"), v[:, 0, :].rearrange("p (b c) -> p b c", b=B)) if together else (
                    scratch.v[b], v[:, b % 2, :].rearrange("p (t c) -> p t c", t=T))
                sp.dma_start(to, values).then_inc(stored, 16)
            sp.wait_ge(stored, (rounds + 2) * 48)

        def part(b, i, level):
            return parts[i][:, bass.ds(b % 2, 1), level * n:(level + 1) * n].rearrange("p o n -> p (o n)")

        def window(b, i):
            if together:
                rows = B * (size + 2) - 2
                return padded[:].rearrange("p b y x -> p (b y) x")[:, i // 3:i // 3 + rows, i % 3:i % 3 + size]
            batch = padded[:, bass.ds(b, 1), :, :].rearrange("p o y x -> p (o y) x")
            return batch[:, i // 3:i // 3 + size, i % 3:i % 3 + size]

        def image(t):
            return t[:, 0:n // one * room - (2 * size if together else 0)].rearrange("p (y x) -> p y x", x=size)

        def tokens(t, gaps=False):
            return t.rearrange("p (b r) -> p b r", b=n // one)[:, :, 0:one] if gaps else t.rearrange("p (b r) -> p b r", b=n // one)

        def over_batches(eng, emit):
            if rounds > 1:
                with eng.Fori(0, rounds - 1) as b:
                    emit(b, True)
            emit(rounds - 1, False)

        @block.gpsimd
        def _(pool):
            pool.memset(wvp[:], 0.0).then_inc(zeroed, 1)
            pool.memset(bvp[:], 1.0).then_inc(zeroed, 1)
            if taps is not None:
                def add_products(b, further):
                    for i in range(1, SHARED):
                        hold(pool, pos_made, SHARED * b + i + 1, held)
                        if i >= 2:
                            hold(pool, shared_added, (SHARED - 1) * b + i - 1, held)
                        pool.tensor_tensor(image(shared), image(shared), image(product[i % 2]), ALU.add).then_inc(shared_added, 1)

                over_batches(pool, add_products)

        @block.scalar
        def _(act):
            def place(b):
                for i in range(SHARED):
                    if i == 0:
                        act.activation(image(shared), window(b, 0), ACT.Identity, bias=taps[:, 1, 9:10], scale=taps[:, 1, 0:1]).then_inc(pos_made, 1)
                    else:
                        if i >= 3:
                            act.wait_ge(shared_added, (SHARED - 1) * b + i - 2)
                        act.activation(image(product[i % 2]), window(b, i), ACT.Copy, scale=taps[:, 1, i:i + 1]).then_inc(pos_made, 1)

            def cast_batch(b, further):
                if taps is not None and further:
                    act.wait_ge(pos_added, OWN * b + 1)
                    place(b + 1)
                act.wait_ge(stored, b * 48 + 48)
                for i in range(2):
                    act.wait_ge(qk_kept, 2 * b + 3 + i)
                    act.activation(part(b, i, 0), x[i][:], ACT.Copy).then_inc(cast, 1)
                if taps is None and further:
                    act.wait_ge(v_made, b + 1)
                    act.activation(src[:], at(m.xnT, b + 1), ACT.Copy).then_inc(staged, 1)
                for i in range(2):
                    act.wait_ge(left, 2 * b + i + 1)
                    act.activation(part(b, i, 1), rest[i][:], ACT.Copy).then_inc(cast, 1)

            act.sem_inc(qk_kept, 2)
            if taps is not None:
                place(0)
            else:
                act.activation(src[:], m.xnT[:, 0, :], ACT.Copy).then_inc(staged, 1)
            over_batches(act, cast_batch)

        @block.tensor
        def _(pe):
            pe.wait_ge(loaded, 96)

            def chunk(c):
                if CH <= one:
                    return src[:, c * CH:(c + 1) * CH]
                return tokens(src[:], True)[:, c * CH // one:(c + 1) * CH // one, :]

            with pe.Fori(0, rounds) as b:
                pe.wait_ge(staged, b + 1)
                pe.wait_ge(qk_kept, 2 * b + 2)
                for i in range(2):
                    for c in range(NC):
                        pe.matmul(qk_ps[i][:, c * CH:(c + 1) * CH], wqk[:, i, :], chunk(c), start=True, stop=True).then_inc(qk_made, 1)
                pe.wait_ge(taken, b + 1)
                for t in range(T):
                    last = pe.matmul(v_ps[0:TN, t * 256:(t + 1) * 256], src[:, t * TN // one * room + t * TN % one:t * TN // one * room + t * TN % one + TN], wvp[:].rearrange("p h d -> p (h d)"), start=True, stop=True)
                last.then_inc(v_made, 1)

        @block.vector
        def _(dve):
            dve.sem_inc(taken, 1)
            dve.sem_inc(stored, 96)

            def convolve(b, i):
                weight = taps[:, 0, i:i + 1]
                if i == 0:
                    dve.tensor_scalar(image(sums), window(b, 0), weight, taps[:, 0, 9:10], ALU.mult, ALU.add).then_inc(tapped, 1)
                else:
                    dve.wait_ge(tapped, b * 8 + i)
                    dve.scalar_tensor_tensor(out=image(sums if i < 8 else src), in0=window(b, i), scalar=weight, in1=image(sums), op0=ALU.mult, op1=ALU.add).then_inc(tapped if i < 8 else staged, 1)

            def split_batch(b, further):
                def taps_of_next(*which):
                    if taps is not None and further:
                        for i in which:
                            if i == 8:
                                dve.wait_ge(v_made, b + 1)
                            convolve(b + 1, i)

                if taps is not None and further:
                    dve.wait_ge(staged, b + 1)
                if taps is not None:
                    for j, i in enumerate(range(SHARED, 9)):
                        taps_of_next(j)
                        if j == 0:
                            dve.wait_ge(shared_added, (SHARED - 1) * (b + 1))
                        else:
                            dve.wait_ge(pos_added, OWN * b + j)
                        dve.scalar_tensor_tensor(out=image(pos), in0=window(b, i), scalar=taps[:, 1, i:i + 1], in1=image(shared if i == SHARED else pos), op0=ALU.mult, op1=ALU.add).then_inc(pos_added, 1)
                    taps_of_next(9 - SHARED)
                    dve.wait_ge(pos_added, OWN * (b + 1))
                for i in range(2):
                    dve.wait_ge(qk_made, 2 * NC * b + NC * (i + 1))
                    if taps is not None:
                        dve.scalar_tensor_tensor(out=tokens(x[i][:]), in0=tokens(qk_ps[i][:, 0:n]), scalar=bqk[:, i:i + 1], in1=tokens(pos[:], True), op0=ALU.add, op1=ALU.add).then_inc(qk_kept, 1)
                    else:
                        dve.tensor_scalar(x[i][:], qk_ps[i][:, 0:n], bqk[:, i:i + 1], (1.0, k_scale)[i], ALU.add, ALU.mult).then_inc(qk_kept, 1)
                    taps_of_next(5 + i)
                dve.wait_ge(stored, b * 48 + 48)
                dve.wait_ge(v_made, b + 1)
                flat_bias = bvp[0:TN].rearrange("p h d -> p (h d)").rearrange("p (o c) -> p o c", o=1).broadcast_to((TN, T, 8 * SLOT))
                to = v[:, bass.ds(b % 2, 1), :].rearrange("p o (t c) -> p (o t) c", t=T)
                dve.tensor_tensor(to, v_ps[0:TN, 0:T * 256].rearrange("p (t c) -> p t c", c=256), flat_bias, ALU.add).then_inc(taken, 1)
                for i in range(2):
                    dve.wait_ge(cast, 4 * b + 1 + i)
                    dve.tensor_tensor(rest[i][:], x[i][:], part(b, i, 0), ALU.subtract).then_inc(left, 1)
                    taps_of_next(7 + i)
                for i in range(2):
                    dve.wait_ge(cast, 4 * b + 3 + i)
                    dve.tensor_tensor(part(b, i, 2), rest[i][:], part(b, i, 1), ALU.subtract).then_inc(split, 1)

            if taps is not None:
                for i in range(9):
                    convolve(0, i)
            dve.wait_ge(loaded, 96)
            over_batches(dve, split_batch)


class Picks:

    def __init__(self, m, ctx, name, n_experts):
        self.one_hot = [m.sb(f"{name}_pick{i}", [P, TILES, n_experts], F32, ctx) for i in range(2)]
        self.weight = m.sb(f"{name}_weight", [P, TILES, 2], F32, ctx)
        self.slots = [m.sb(f"{name}_slots{i}", [P, TILES], U32, ctx) for i in range(2)]


def route(m, name, n_experts, gate, gate_bias, picks, combine=None, combineT=None):
    nc = m.nc
    E = n_experts
    with Stage(nc) as ctx:
        sb = lambda nm, s, dt=F32: m.sb(f"{name}_{nm}", s, dt, ctx)
        gw, gb, logits, iota = sb("gw", [P, E]), sb("gb", [P, E]), sb("logits", [P, TILES, E]), sb("iota", [P, E])
        top, index, indexf = sb("top", [P, TILES, 8]), sb("index", [P, TILES, 8], U32), sb("indexf", [P, TILES, 2])
        gap, odds, weight = sb("gap", [P, TILES]), sb("odds", [P, TILES]), picks.weight
        ps = m.psum(f"{name}_ps", [P, TILES, E], ctx)
        dT_ps = [m.psum(f"{name}_d{i}", [P, 512], ctx) for i in range(2)] if combineT is not None else None
        loaded, made, counted, compared, exped, combined, turned, taken, dve_step = (
            m.sem(f"{name}_{x}", ctx) for x in ("loaded", "made", "counted", "compared", "exped", "combined", "turned", "taken", "dve"))
        block = ctx.enter_context(nc.Block())
        n_loads = 2 if gate_bias is not None else 1

        @block.sync
        def _(sp):
            sp.dma_start(gw[:], gate).then_inc(loaded, 16)
            if gate_bias is not None:
                sp.dma_start(gb[:], gate_bias.rearrange("(o e) -> o e", o=1).broadcast_to((P, E))).then_inc(loaded, 16)

        @block.gpsimd
        def _(pool):
            pool.iota(iota[:], pattern=[[1, E]], base=0, channel_multiplier=0, allow_small_or_imprecise_dtypes=True).then_inc(counted, 1)

        @block.tensor
        def _(pe):
            pe.wait_ge(loaded, 16 * n_loads)
            for t in range(TILES):
                last = pe.matmul(ps[:, t, :], m.xnT[:].rearrange("p b n -> p (b n)")[:, t * P:(t + 1) * P], gw[:], start=True, stop=True)
            last.then_inc(made, 1)
            if combineT is not None:
                pe.wait_ge(combined, 1)
                for g in range(TILES // 4):
                    if g >= 2:
                        pe.wait_ge(taken, g - 1)
                    for t in range(4):
                        last = pe.transpose(dT_ps[g % 2][0:E, t * P:(t + 1) * P], combine[:, 4 * g + t, :], m.ident[:])
                    last.then_inc(turned, 1)

        @block.scalar
        def _(act):
            act.wait_ge(compared, 1)
            act.activation(odds[:], gap[:], ACT.Exp).then_inc(exped, 1)

        @block.vector
        def _(dve):
            step = Chain(dve, dve_step)
            dve.wait_ge(made, 1)
            if gate_bias is not None:
                step(dve.tensor_tensor(logits[:], ps[:], gb[:].rearrange("p (o e) -> p o e", o=1).broadcast_to((P, TILES, E)), ALU.add))
            else:
                step(dve.tensor_copy(logits[:], ps[:]))
            for t in range(TILES):
                last = dve.max(top[:, t, :], logits[:, t, :])
            step(last)
            for t in range(TILES):
                last = dve.max_index(index[:, t, :], top[:, t, :], logits[:, t, :])
            dve.tensor_tensor(gap[:], top[:, :, 1], top[:, :, 0], ALU.subtract).then_inc(compared, 1)
            step(last)
            step(dve.tensor_copy(indexf[:], index[:, :, 0:2]))
            dve.wait_ge(exped, 1)
            step(dve.tensor_scalar(weight[:, :, 1], odds[:], 1.0, None, ALU.add))
            step(dve.reciprocal(weight[:, :, 0], weight[:, :, 1]))
            step(dve.tensor_tensor(weight[:, :, 1], weight[:, :, 0], odds[:], ALU.mult))
            dve.wait_ge(counted, 1)
            numbers = iota[:].rearrange("p (o e) -> p o e", o=1).broadcast_to((P, TILES, E))
            for i, to in enumerate(picks.one_hot):
                step(dve.tensor_tensor(to[:], numbers, indexf[:, :, i:i + 1].broadcast_to((P, TILES, E)), ALU.is_equal))
            if combine is not None:
                for i, to in enumerate(picks.one_hot):
                    step(dve.tensor_tensor(to[:], to[:], weight[:, :, i:i + 1].broadcast_to((P, TILES, E)), ALU.mult))
                dve.tensor_tensor(combine[:], picks.one_hot[0][:], picks.one_hot[1][:], ALU.add).then_inc(combined, 1)
            if combineT is not None:
                for g in range(TILES // 4):
                    dve.wait_ge(turned, g + 1)
                    dve.tensor_copy(combineT[:, g, :], dT_ps[g % 2][0:E, :]).then_inc(taken, 1)
                dve.wait_ge(taken, TILES // 4)


ROUTED_TILES = 2 * TILES + 16
STEP_TILES = 40


class Routed:

    def __init__(self, m, ctx):
        rows = (ROUTED_TILES + STEP_TILES) * P
        self.x = m.nc.dram_tensor("routed_x", [rows, C], F32, kind="Internal").ap()
        self.y = m.nc.dram_tensor("routed_y", [ROUTED_TILES * P, C], F32, kind="Internal").ap()
        self.tile_expert = m.sb("tile_expert", [1, ROUTED_TILES], I32, ctx)


def clear_routed(sp, pool, routed, zeros, zeroed, cleared):
    if pool is not None:
        pool.memset(zeros[:], 0.0).then_inc(zeroed, 1)
    if sp is not None:
        sp.wait_ge(zeroed, 1)
        rows = routed.x.rearrange("(k p r) c -> k p (r c)", p=P, r=STEP_TILES)
        for k in range(rows.shape[0]):
            sp.dma_start(rows[k], zeros[:]).then_inc(cleared, 16)
        sp.wait_ge(cleared, 16 * rows.shape[0])


def edge_bias(m, name, ctx, targets, attributes, we, be, bias_parts):
    nc = m.nc
    EDGES = targets.shape[0]
    CHUNK, KEYS = 8192, N // P
    CHUNKS = EDGES // CHUNK
    sb = lambda nm, s, dt=F32: m.sb(f"{name}_{nm}", s, dt, ctx)
    raw, a, c_, short = sb("raw", [P, EDGES // P], I32), sb("a", [P, EDGES // P]), sb("c", [P, EDGES // P]), sb("short", [P, EDGES // P], U16)
    text = [sb(f"text{i}", [P, CHUNK + KEYS], U16) for i in range(2)]
    keys, where = sb("keys", [P, KEYS], I32), sb("where", [P, CHUNKS, KEYS], U32)
    place, miss, best, found, index = sb("place", [P, CHUNKS, KEYS]), sb("miss", [P, CHUNKS, KEYS]), sb("best", [P, KEYS]), sb("found", [P, KEYS]), sb("index", [P, KEYS], U32)
    rows, rowsT, wb = sb("rows", [P, KEYS, 4]), sb("rowsT", [4, N]), sb("wb", [4, HEADS])
    bias, rest, parts = sb("bias", [HEADS, N]), sb("rest", [HEADS, N]), sb("parts", [HEADS, 3, N], BF16)
    ps, b_ps = m.psum(f"{name}_ps", [P, N], ctx), m.psum(f"{name}_b", [P, N], ctx)
    dram = nc.dram_tensor(f"{name}_targets", [EDGES], U16, kind="Internal").ap()
    loaded, packed, sent, keyed, keys_set, chunk_in, searched, indexed, ones, masked, turned, kept, summed, split, stored, dve_step = (
        m.sem(f"{name}_{x}", ctx) for x in ("loaded", "packed", "sent", "keyed", "keys_set", "chunk_in", "searched", "indexed",
                                            "ones", "masked", "turned", "kept_", "summed", "split", "stored", "dve"))
    def sync(sp):
        sp.dma_start(raw[:], targets.rearrange("(p e) -> p e", p=P)).then_inc(loaded, 16)
        sp.dma_start(wb[0:3, :], we).then_inc(loaded, 16)
        sp.dma_start(wb[3:4, :], be.rearrange("(o h) -> o h", o=1)).then_inc(loaded, 16)
        sp.wait_ge(packed, 1)
        sp.dma_start(dram.rearrange("(p e) -> p e", p=P), short[:]).then_inc(sent, 16)
        sp.wait_ge(sent, 16)
        for i in range(CHUNKS):
            if i >= 2:
                sp.wait_ge(searched, i - 1)
            sp.dma_start(text[i % 2][:, 0:CHUNK], dram[i * CHUNK:(i + 1) * CHUNK].rearrange("(o e) -> o e", o=1).broadcast_to((P, CHUNK))).then_inc(chunk_in, 16)
            sp.wait_ge(chunk_in, 16 * (i + 1))
        sp.wait_ge(split, 1)
        sp.dma_start(bias_parts.rearrange("l h n -> h l n"), parts[:]).then_inc(stored, 16)
        sp.wait_ge(stored, 16)

    def prepare(pool):
        pool.memset(rows[:, :, 3:4], 1.0).then_inc(ones, 1)
        pool.iota(keys[:], pattern=[[P, KEYS]], base=0, channel_multiplier=1).then_inc(keyed, 1)

    def gpsimd(pool):
        pool.wait_ge(indexed, 1)
        for r in range(KEYS):
            pool.indirect_dma_start(out=rows[:, r, 0:3], out_offset=None, in_=attributes,
                                    in_offset=bass.IndirectOffsetOnAxis(ap=index[:, r:r + 1], axis=0)).then_inc(m.gathered, 16)
        pool.wait_ge(m.gathered, 16 * KEYS)

    def vector(dve):
        step = Chain(dve, dve_step)
        dve.wait_ge(loaded, 48)
        step(dve.tensor_copy(a[:], raw[:]))
        step(dve.tensor_scalar(c_[:], a[:], 0.0, float(N), ALU.is_lt, ALU.mult))
        step(dve.tensor_tensor(a[:], a[:], c_[:], ALU.add))
        step(dve.tensor_scalar(c_[:], a[:], 0.0, float(2 * N), ALU.is_lt, ALU.mult))
        step(dve.tensor_scalar(a[:], a[:], 0.0, float(N), ALU.max, ALU.min))
        step(dve.tensor_tensor(a[:], a[:], c_[:], ALU.max))
        dve.tensor_copy(short[:], a[:]).then_inc(packed, 1)
        dve.wait_ge(keyed, 1)
        for i in range(2):
            dve.tensor_copy(text[i][:, CHUNK:CHUNK + KEYS], keys[:]).then_inc(keys_set, 1)
        dve.wait_ge(keys_set, 2)
        for i in range(CHUNKS):
            dve.wait_ge(chunk_in, 16 * (i + 1))
            dve.max_index(where[:, i, :], text[i % 2][:, CHUNK:CHUNK + KEYS], text[i % 2][:]).then_inc(searched, 1)
        dve.wait_ge(searched, CHUNKS)
        step(dve.tensor_copy(place[:], where[:]))
        step(dve.tensor_scalar(miss[:], place[:], float(CHUNK), float(2 * EDGES), ALU.is_ge, ALU.mult))
        for i in range(CHUNKS):
            last = dve.scalar_tensor_tensor(out=place[:, i, :], in0=place[:, i, :], scalar=float(i * CHUNK), in1=miss[:, i, :], op0=ALU.add, op1=ALU.add)
        step(last)
        step(dve.tensor_reduce(best[:], place[:].rearrange("p c k -> p k c"), AX.X, ALU.min))
        step(dve.tensor_scalar(found[:], best[:], float(EDGES), None, ALU.is_lt))
        step(dve.tensor_scalar(best[:], best[:], float(EDGES - 1), None, ALU.min))
        dve.tensor_copy(index[:], best[:]).then_inc(indexed, 1)
        dve.wait_ge(m.gathered, 16 * KEYS)
        dve.wait_ge(ones, 1)
        dve.tensor_tensor(rows[:], rows[:], found[:].rearrange("p (k o) -> p k o", o=1).broadcast_to((P, KEYS, 4)), ALU.mult).then_inc(masked, 1)
        dve.wait_ge(turned, 1)
        dve.tensor_copy(rowsT[:], ps[0:4, :]).then_inc(kept, 1)
        dve.wait_ge(summed, 1)
        step(dve.tensor_copy(bias[:], b_ps[0:HEADS, :]))
        split_in_three(dve, step, parts[:], bias[:], rest[:]).then_inc(split, 1)

    def tensor(pe):
        pe.wait_ge(masked, 1)
        for r in range(KEYS):
            last = pe.transpose(ps[0:4, r * P:(r + 1) * P], rows[:, r, :], m.ident[:])
        last.then_inc(turned, 1)
        pe.wait_ge(kept, 1)
        for h in range(2):
            last = pe.matmul(b_ps[0:HEADS, h * 512:(h + 1) * 512], wb[:], rowsT[:, h * 512:(h + 1) * 512], start=True, stop=True)
        last.then_inc(summed, 1)

    return sync, prepare, gpsimd, vector, tensor


class ExpertWeights:

    def __init__(self, m, ctx, n_experts, hidden, w1, w2, w3):
        self.hidden, self.chunks = hidden, hidden // P
        self.w12, self.w3 = m.sb("expert_w12", [P, n_experts, 2 * hidden], F32, ctx), m.sb("expert_w3", [P, n_experts, self.chunks, C], F32, ctx)
        self.dram = w1, w2, w3

    def load(self, sp, loaded):
        w1, w2, w3 = self.dram
        sp.dma_start(self.w12[:, :, 0:self.hidden], w1.rearrange("e c h -> c e h")).then_inc(loaded, 16)
        sp.dma_start(self.w12[:, :, self.hidden:], w2.rearrange("e c h -> c e h")).then_inc(loaded, 16)
        sp.dma_start(self.w3[:], w3.rearrange("e (k h) c -> h e k c", k=self.chunks)).then_inc(loaded, 16)


def dispatch_tokens(m, name, picks, routed, xn, weights, beside):
    nc = m.nc
    E = picks.one_hot[0].shape[2]
    with Stage(nc) as ctx:
        beside_sync, beside_prepare, beside_gpsimd, beside_vector, beside_tensor = beside(ctx)
        weights_loaded = m.sem(f"{name}_weights_loaded", ctx)
        sb = lambda nm, s, dt=F32: m.sb(f"{name}_{nm}", s, dt, ctx)
        before, ones = sb("before", [P, P]), sb("ones", [P, P])
        both, total, scan = sb("both", [P, TILES, E]), sb("total", [P, TILES, E]), [sb(f"scan{i}", [P, TILES, E]) for i in range(2)]
        count, tiles_i, tiles, ends = sb("count", [P, E]), sb("tiles_i", [P, E], I32), sb("tiles", [P, E]), [sb(f"ends{i}", [P, E]) for i in range(2)]
        slotf = sb("slotf", [P, 2, TILES])
        numbers, past, expert = sb("numbers", [1, ROUTED_TILES]), sb("past", [1, ROUTED_TILES, E]), sb("expert", [1, ROUTED_TILES])
        within_ps, total_ps = m.psum(f"{name}_within", [P, TILES, E], ctx), m.psum(f"{name}_total", [P, TILES, E], ctx)
        loaded, ready, counted, numbered, placed, dve_step = (m.sem(f"{name}_{x}", ctx) for x in ("loaded", "ready", "counted", "numbered", "placed", "dve"))
        block = ctx.enter_context(nc.Block())

        @block.sync
        def _(sp):
            sp.dma_start(before[:], m.ins["c_before"]).then_inc(loaded, 16)
            beside_sync(sp)
            sp.wait_ge(weights_loaded, 48)

        @block.scalar
        def _(act):
            weights.load(act, weights_loaded)

        @block.tensor
        def _(pe):
            pe.wait_ge(loaded, 16)
            pe.wait_ge(ready, 2)
            pe.matmul(within_ps[:].rearrange("p t e -> p (t e)"), before[:], both[:].rearrange("p t e -> p (t e)"), start=True, stop=True)
            pe.matmul(total_ps[:].rearrange("p t e -> p (t e)"), ones[:], both[:].rearrange("p t e -> p (t e)"), start=True, stop=True).then_inc(counted, 1)
            beside_tensor(pe)

        @block.gpsimd
        def _(pool):
            pool.iota(numbers[:], pattern=[[1, ROUTED_TILES]], base=0, channel_multiplier=0, allow_small_or_imprecise_dtypes=True).then_inc(numbered, 1)
            beside_prepare(pool)
            pool.wait_ge(placed, 2)
            for t in range(TILES):
                if t == 3 * TILES // 4:
                    beside_gpsimd(pool)
                for slots in picks.slots:
                    pool.indirect_dma_start(out=routed.x, out_offset=bass.IndirectOffsetOnAxis(ap=slots[:, t:t + 1], axis=0),
                                            in_=xn[:, t, :], in_offset=None).then_inc(m.scattered, 16)
            pool.wait_ge(m.scattered, 16 * 2 * TILES)

        @block.vector
        def _(dve):
            step = Chain(dve, dve_step)
            dve.tensor_tensor(both[:], picks.one_hot[0][:], picks.one_hot[1][:], ALU.add).then_inc(ready, 1)
            dve.memset(ones[:], 1.0).then_inc(ready, 1)
            dve.wait_ge(counted, 1)
            step(dve.tensor_copy(total[:], total_ps[:]))
            dve.memset(scan[0][:, 0:1, :], 0.0)
            step(dve.tensor_copy(scan[0][:, 1:TILES, :], total[:, 0:TILES - 1, :]))
            now, d = 0, 1
            while d < TILES:
                a, b = scan[now], scan[1 - now]
                dve.tensor_copy(b[:, 0:d, :], a[:, 0:d, :])
                step(dve.tensor_tensor(b[:, d:TILES, :], a[:, d:TILES, :], a[:, 0:TILES - d, :], ALU.add))
                now, d = 1 - now, 2 * d
            base, slot = scan[now], scan[1 - now]
            step(dve.tensor_tensor(count[:], base[:, TILES - 1, :], total[:, TILES - 1, :], ALU.add))
            step(dve.tensor_scalar(tiles_i[:], count[:], float(P - 1), None, ALU.add))
            step(dve.tensor_single_scalar(tiles_i[:], tiles_i[:], 7, ALU.arith_shift_right))
            step(dve.tensor_copy(tiles[:], tiles_i[:]))
            step(dve.tensor_copy(ends[0][:], tiles[:]))
            now, d = 0, 1
            while d < E:
                a, b = ends[now], ends[1 - now]
                dve.tensor_copy(b[:, 0:d], a[:, 0:d])
                step(dve.tensor_tensor(b[:, d:E], a[:, d:E], a[:, 0:E - d], ALU.add))
                now, d = 1 - now, 2 * d
            end, start = ends[now], ends[1 - now]
            step(dve.tensor_tensor(start[:], end[:], tiles[:], ALU.subtract))
            step(dve.tensor_scalar(start[:], start[:], float(P), None, ALU.mult))
            step(dve.tensor_tensor(slot[:], base[:], within_ps[:], ALU.add))
            step(dve.tensor_tensor(slot[:], slot[:], start[:].rearrange("p (o e) -> p o e", o=1).broadcast_to((P, TILES, E)), ALU.add))
            for i in range(2):
                step(dve.tensor_tensor(both[:], slot[:], picks.one_hot[i][:], ALU.mult))
                step(dve.tensor_reduce(slotf[:, i, :], both[:], AX.X, ALU.add))
                dve.tensor_copy(picks.slots[i][:], slotf[:, i, :]).then_inc(placed, 1)
            dve.wait_ge(numbered, 1)
            step(dve.tensor_tensor(past[:], end[0:1, :].rearrange("p (o e) -> p o e", o=1).broadcast_to((1, ROUTED_TILES, E)),
                                   numbers[:].rearrange("p (t o) -> p t o", o=1).broadcast_to((1, ROUTED_TILES, E)), ALU.is_le))
            step(dve.tensor_reduce(expert[:], past[:], AX.X, ALU.add))
            step(dve.tensor_scalar(expert[:], expert[:], float(E - 1), None, ALU.min))
            step(dve.tensor_copy(routed.tile_expert[:], expert[:]))
            beside_vector(dve)


def routed_experts(m, name, n_experts, weights, routed):
    nc = m.nc
    E, hidden, HC, ST, CHUNK = n_experts, weights.hidden, weights.chunks, STEP_TILES, 5
    w12, w3s = weights.w12, weights.w3
    CHUNKS, STEPS = ST // CHUNK, ROUTED_TILES // ST
    with Stage(nc) as ctx:
        sb = lambda nm, s, dt=F32: m.sb(f"{name}_{nm}", s, dt, ctx)
        xs, ys = sb("xs", [P, ST, C]), sb("ys", [P, ST, C])
        pairs = lambda nm, s: [sb(f"{nm}{i}", s) for i in range(2)]
        xT, gate, hid, hidT = pairs("xT", [P, P]), pairs("gate", [P, hidden]), pairs("hid", [P, hidden]), pairs("hidT", [P, HC, P])
        x_ps, h_ps, t_ps, y_ps = ([m.psum(f"{name}_{x}{i}", [P, 512], ctx) for i in range(2)] for x in ("xp", "hp", "tp", "yp"))
        x_in, y_out = [m.sem(f"{name}_x_in{q}", ctx) for q in range(CHUNKS)], [m.sem(f"{name}_y_out{q}", ctx) for q in range(CHUNKS)]
        x_turned, x_kept, opened, gated, made, turned, kept, mixed, y_kept = (
            m.sem(f"{name}_{x}", ctx) for x in ("x_turned", "x_kept", "opened", "gated", "made", "turned", "kept_", "mixed", "y_kept"))
        block = ctx.enter_context(nc.Block())
        x_tiles = routed.x.rearrange("(t p) c -> p t c", p=P)
        y_tiles = routed.y.rearrange("(t p) c -> p t c", p=P)

        @block.sync
        def _(sp):
            for q in range(CHUNKS):
                sp.dma_start(xs[:, q * CHUNK:(q + 1) * CHUNK, :], x_tiles[:, q * CHUNK:(q + 1) * CHUNK, :]).then_inc(x_in[q], 16)
            with sp.Fori(0, STEPS) as i:
                for q in range(CHUNKS):
                    sp.wait_ge(x_turned, i * ST + (q + 1) * CHUNK)
                    sp.dma_start(xs[:, q * CHUNK:(q + 1) * CHUNK, :], x_tiles[:, bass.ds((i + 1) * ST + q * CHUNK, CHUNK), :]).then_inc(x_in[q], 16)
                    sp.wait_ge(y_kept, 2 + i * ST + (q + 1) * CHUNK)
                    sp.dma_start(y_tiles[:, bass.ds(i * ST + q * CHUNK, CHUNK), :], ys[:, q * CHUNK:(q + 1) * CHUNK, :]).then_inc(y_out[q], 16)
            for q in range(CHUNKS):
                sp.wait_ge(y_out[q], 16 * (STEPS + 1))
                sp.wait_ge(x_in[q], 16 * (STEPS + 1))

        @block.tensor
        def _(pe):
            pe.sem_inc(opened, 2)
            pe.sem_inc(turned, 2)
            pe.sem_inc(mixed, 2)
            with pe.Fori(0, STEPS) as i:

                def turn_x(j):
                    if j % CHUNK == 0:
                        pe.wait_ge(x_in[j // CHUNK], 16 * i + 16)
                    pe.wait_ge(x_kept, i * ST + j + 1)
                    pe.transpose(x_ps[j % 2][:, 0:P], xs[:, j, :], m.ident[:]).then_inc(x_turned, 1)

                def opening(j):
                    expert = pe.value_load(routed.tile_expert[0:1, bass.ds(i * ST + j, 1)], min_val=0, max_val=E - 1)
                    pe.wait_ge(x_kept, i * ST + j + 3)
                    pe.wait_ge(made, i * ST + j + 1)
                    pe.matmul(h_ps[j % 2][:], xT[j % 2][:], w12[:, bass.ds(expert, 1), :].rearrange("p o h -> p (o h)"), start=True, stop=True).then_inc(opened, 1)
                    return expert

                def turn_hidden(j):
                    pe.wait_ge(made, i * ST + j + 3)
                    pe.wait_ge(kept, i * ST + j + 1)
                    for k in range(HC):
                        last = pe.transpose(t_ps[j % 2][:, k * P:(k + 1) * P], hid[j % 2][:, k * P:(k + 1) * P], m.ident[:])
                    last.then_inc(turned, 1)

                def closing(j, expert):
                    pe.wait_ge(kept, i * ST + j + 3)
                    pe.wait_ge(y_kept, i * ST + j + 1)
                    for k in range(HC):
                        last = pe.matmul(y_ps[j % 2][:, 0:C], hidT[j % 2][:, k, :], w3s[:, bass.ds(expert, 1), k, :].rearrange("p o c -> p (o c)"), start=(k == 0), stop=(k == HC - 1))
                    last.then_inc(mixed, 1)

                experts = {}
                for slot in range(ST + 3):
                    if slot < ST:
                        turn_x(slot)
                    if 0 <= slot - 1 < ST:
                        experts[slot - 1] = opening(slot - 1)
                    if 0 <= slot - 2 < ST:
                        turn_hidden(slot - 2)
                    if 0 <= slot - 3 < ST:
                        closing(slot - 3, experts.pop(slot - 3))

        @block.scalar
        def _(act):
            act.sem_inc(x_kept, 2)
            with act.Fori(0, STEPS) as i:

                def keep_x(j):
                    act.wait_ge(x_turned, i * ST + j + 1)
                    act.wait_ge(opened, i * ST + j + 1)
                    act.activation(xT[j % 2][:], x_ps[j % 2][:, 0:P], ACT.Copy).then_inc(x_kept, 1)

                def open_gate(j):
                    act.wait_ge(opened, i * ST + j + 3)
                    act.wait_ge(made, i * ST + j + 1)
                    act.activation(gate[j % 2][:], h_ps[j % 2][:, 0:hidden], ACT.Silu).then_inc(gated, 1)

                for slot in range(ST + 1):
                    if slot < ST:
                        keep_x(slot)
                    if slot >= 1:
                        open_gate(slot - 1)

        @block.vector
        def _(dve):
            dve.sem_inc(made, 2)
            dve.sem_inc(kept, 2)
            dve.sem_inc(y_kept, 2)
            for q in range(CHUNKS):
                dve.sem_inc(y_out[q], 16)
            with dve.Fori(0, STEPS) as i:

                def make(j):
                    dve.wait_ge(gated, i * ST + j + 1)
                    dve.wait_ge(turned, i * ST + j + 1)
                    dve.tensor_tensor(hid[j % 2][:], gate[j % 2][:], h_ps[j % 2][:, hidden:2 * hidden], ALU.mult).then_inc(made, 1)

                def keep_hidden(j):
                    dve.wait_ge(turned, i * ST + j + 3)
                    dve.wait_ge(mixed, i * ST + j + 1)
                    dve.tensor_copy(hidT[j % 2][:].rearrange("p k t -> p (k t)"), t_ps[j % 2][:, 0:HC * P]).then_inc(kept, 1)

                def keep_y(j):
                    if j % CHUNK == 0:
                        dve.wait_ge(y_out[j // CHUNK], 16 * i + 16)
                    dve.wait_ge(mixed, i * ST + j + 3)
                    dve.tensor_copy(ys[:, j, :], y_ps[j % 2][:, 0:C]).then_inc(y_kept, 1)

                for slot in range(ST + 2):
                    if slot < ST:
                        make(slot)
                    if 0 <= slot - 1 < ST:
                        keep_hidden(slot - 1)
                    if 0 <= slot - 2 < ST:
                        keep_y(slot - 2)


def gelu_experts(m, name, n_experts, w1, b1, w2, b2, combine, combineT, xn):
    nc = m.nc
    E, TG = n_experts, 4
    GROUPS = TILES // TG
    with Stage(nc) as ctx:
        sb = lambda nm, s, dt=F32: m.sb(f"{name}_{nm}", s, dt, ctx)
        w1s, w2s, b1s, b2s = sb("w1", [P, E, C]), sb("w2", [P, E, C]), sb("b1", [P, E]), sb("b2", [E, C])
        share, hid = sb("share", [E, 512]), [sb(f"hid{i}", [P, 512]) for i in range(2)]
        h_ps = [m.psum(f"{name}_h{i}", [P, 512], ctx) for i in range(2)]
        o_ps = [m.psum(f"{name}_o{i}", [P, 512], ctx) for i in range(2)]
        b_ps = m.psum(f"{name}_b", [P, 512], ctx)
        loaded, staged, opened, made, mixed, biased, bias_added, added = (
            m.sem(f"{name}_{x}", ctx) for x in ("loaded", "staged", "opened", "made", "mixed", "biased", "bias_added", "added"))
        block = ctx.enter_context(nc.Block())

        @block.sync
        def _(sp):
            sp.dma_start(w1s[:], w1.rearrange("e c h -> c e h")).then_inc(loaded, 16)
            sp.dma_start(w2s[:], w2.rearrange("e h c -> h e c")).then_inc(loaded, 16)
            sp.dma_start(b1s[:], b1).then_inc(loaded, 16)
            sp.dma_start(b2s[:], b2).then_inc(loaded, 16)

        @block.tensor
        def _(pe):
            pe.wait_ge(loaded, 64)
            with pe.Fori(0, GROUPS) as g:
                x = m.xnT[:].rearrange("p b n -> p (b n)")[:, bass.ds(g * 512, 512)]
                pe.wait_ge(staged, g + 1)
                pe.wait_ge(bias_added, 2 * g + 2)
                for t in range(TG):
                    last = pe.matmul(b_ps[:, t * P:(t + 1) * P], share[:, t * P:(t + 1) * P], b2s[:], start=True, stop=True)
                last.then_inc(biased, 1)

                def closing(e):
                    pe.wait_ge(made, g * E + e + 1)
                    pe.wait_ge(added, 2 + g * E + e - 1)
                    for t in range(TG):
                        last = pe.matmul(o_ps[e % 2][:, t * P:(t + 1) * P], hid[e % 2][:, t * P:(t + 1) * P], w2s[:, e, :], start=True, stop=True)
                    last.then_inc(mixed, 1)

                for e in range(E):
                    if e >= 2:
                        pe.wait_ge(made, g * E + e - 1)
                    pe.matmul(h_ps[e % 2][:], w1s[:, e, :], x, start=True, stop=True).then_inc(opened, 1)
                    if e >= 1:
                        closing(e - 1)
                closing(E - 1)

        @block.scalar
        def _(act):
            act.wait_ge(loaded, 64)
            with act.Fori(0, GROUPS) as g:
                for e in range(E):
                    act.wait_ge(opened, g * E + e + 1)
                    if e >= 2:
                        act.wait_ge(mixed, g * E + e - 1)
                    act.activation(hid[e % 2][:], h_ps[e % 2][:], ACT.Gelu, bias=b1s[:, e:e + 1]).then_inc(made, 1)

        @block.vector
        def _(dve):
            dve.sem_inc(added, 2)
            dve.sem_inc(bias_added, 2)

            def stage_share(g):
                dve.tensor_copy(share[:], combineT[:, bass.ds(g, 1), :].rearrange("p o n -> p (o n)")).then_inc(staged, 1)

            def add_group(g, further):
                group = m.tt[:, bass.ds(g * TG, TG), :]
                dve.wait_ge(biased, g + 1)
                dve.tensor_tensor(group, group, b_ps[:].rearrange("p (t c) -> p t c", c=C), ALU.add).then_inc(bias_added, 1)
                dve.wait_ge(bias_added, 2 * g + 3)
                dve.tensor_tensor(group, group, xn[:, bass.ds(g * TG, TG), :], ALU.add).then_inc(bias_added, 1)
                if further:
                    stage_share(g + 1)
                dve.wait_ge(bias_added, 2 * g + 4)
                for e in range(E):
                    dve.wait_ge(mixed, g * E + e + 1)
                    dve.wait_ge(added, 2 + g * E + e)
                    for t in range(TG):
                        tile = m.tt[:, bass.ds(g * TG + t, 1), :].rearrange("p o c -> p (o c)")
                        weight = combine[:, bass.ds(g * TG + t, 1), e:e + 1].rearrange("p o e -> p (o e)")
                        last = dve.scalar_tensor_tensor(out=tile, in0=o_ps[e % 2][:, t * P:(t + 1) * P], scalar=weight, in1=tile, op0=ALU.mult, op1=ALU.add)
                    last.then_inc(added, 1)

            stage_share(0)
            with dve.Fori(0, GROUPS - 1) as g:
                add_group(g, True)
            add_group(GROUPS - 1, False)


class Ahead:

    def __init__(self, plain, padded):
        self.plain, self.padded = plain, padded
        self.loads = len(plain) + 8 * len(padded)

    def clear(self, pool, zeroed):
        for to, _ in self.padded:
            pool.memset(to[:], 0.0).then_inc(zeroed, 1)

    def load(self, sp, zeroed, loaded):
        for to, dram in self.plain:
            sp.dma_start(to, dram).then_inc(loaded, 16)
        sp.wait_ge(zeroed, len(self.padded))
        for to, rows in self.padded:
            for half in range(2):
                for j in range(4):
                    first = half * 64 + j * HD
                    sp.dma_start(to[j * SLOT:j * SLOT + HD, half, :], rows[first:first + HD, :]).then_inc(loaded, 16)
        sp.wait_ge(loaded, self.loads * 16)


def output_projection(m, name, heads_out, wp, bob):
    nc = m.nc
    T = N // P
    with Stage(nc) as ctx:
        sb = lambda nm, s, dt=F32: m.sb(f"{name}_{nm}", s, dt, ctx)
        src, total = [sb(f"src{i}", [P, 2, N]) for i in range(2)], [sb(f"total{i}", [P, T, C]) for i in range(2)]
        ps = [m.psum(f"{name}_ps{i}", [P, T, C], ctx) for i in range(2)]
        staged, made, taken, added = (m.sem(f"{name}_{x}", ctx) for x in ("staged", "made", "taken", "added"))
        block = ctx.enter_context(nc.Block())

        @block.scalar
        def _(act):
            act.sem_inc(made, 2)
            with act.Fori(0, B // 2) as i:
                for p in range(2):
                    b = 2 * i + p
                    act.wait_ge(made, b + 1)
                    act.activation(src[p][:], heads_out[:, :, bass.ds(b, 1), :].rearrange("p h o n -> p (h o) n"), ACT.Copy).then_inc(staged, 1)

        @block.tensor
        def _(pe):
            with pe.Fori(0, B // 2) as i:
                for p in range(2):
                    b = 2 * i + p
                    pe.wait_ge(staged, b + 1)
                    pe.wait_ge(taken, b + 1)
                    for t in range(T):
                        for half in range(2):
                            last = pe.matmul(ps[p][:, t, :], src[p][:, half, t * P:(t + 1) * P], wp[:, half, :], start=(half == 0), stop=(half == 1))
                    last.then_inc(made, 1)

        @block.vector
        def _(dve):
            dve.sem_inc(taken, 2)
            dve.sem_inc(added, 2)
            with dve.Fori(0, B // 2) as i:
                for p in range(2):
                    b = 2 * i + p
                    dve.wait_ge(made, b + 3)
                    dve.wait_ge(added, b + 1)
                    dve.tensor_tensor(total[p][:], ps[p][:], bob[:].rearrange("p (o c) -> p o c", o=1).broadcast_to((P, T, C)), ALU.add).then_inc(taken, 1)
                    dve.wait_ge(taken, b + 3)
                    tokens = at(m.xc, b)
                    dve.tensor_tensor(tokens, tokens, total[p][:].rearrange("p t c -> p (t c)"), ALU.add).then_inc(added, 1)


def pool_by_two(m, name, src, size, dst):
    nc = m.nc
    half = size // 2
    with Stage(nc) as ctx:
        pair = m.sb(f"{name}_pair", [P, B, size, half], F32, ctx)
        four = m.sb(f"{name}_four", [P, B, half, half], F32, ctx)
        step_sem = m.sem(f"{name}_step", ctx)
        block = ctx.enter_context(nc.Block())

        @block.vector
        def _(dve):
            step = Chain(dve, step_sem)
            step(dve.memset(dst[:], 0.0))
            for b in range(B):
                last = dve.tensor_tensor(pair[:, b], src[:, b, 1:size + 1, 1:size + 1:2], src[:, b, 1:size + 1, 2:size + 2:2], ALU.add)
            step(last)
            for b in range(B):
                last = dve.tensor_tensor(four[:, b], pair[:, b, 0:size:2, :], pair[:, b, 1:size:2, :], ALU.add)
            step(last)
            for b in range(B):
                last = dve.tensor_scalar(dst[:, b, 1:half + 1, 1:half + 1], four[:, b], 0.25, None, ALU.mult)
            step(last)


def fuse_scales(m, name, outs, wp, up2, up4, fb):
    nc = m.nc
    with Stage(nc) as ctx:
        sb = lambda nm, s, dt=F32: m.sb(f"{name}_{nm}", s, dt, ctx)
        s2, s4, f = sb("s2", [P, 2, 256]), sb("s4", [P, 2, 64]), sb("f", [P, 3, C])
        f_ps, ps = m.psum(f"{name}_f", [P, 4, C], ctx), m.psum(f"{name}_ps", [P, N], ctx)
        staged, projected, kept, fused, added = (m.sem(f"{name}_{x}", ctx) for x in ("staged", "projected", "kept_", "fused", "added"))
        block = ctx.enter_context(nc.Block())

        @block.tensor
        def _(pe):
            with pe.Fori(0, B) as b:
                pe.wait_ge(staged, 2 * b + 2)
                for k in range(2):
                    for half in range(2):
                        pe.matmul(f_ps[:, k, :], s2[:, half, k * P:(k + 1) * P], wp[1][:, half, :], start=(half == 0), stop=(half == 1))
                for half in range(2):
                    last = pe.matmul(f_ps[0:64, 2, :], s4[:, half, :], wp[2][:, half, :], start=(half == 0), stop=(half == 1))
                last.then_inc(projected, 1)
                pe.wait_ge(added, b + 1)
                for c in range(2):
                    for half in range(2):
                        pe.matmul(ps[:, c * 512:(c + 1) * 512], wp[0][:, half, :], outs[0][:, half, bass.ds(b, 1), c * 512:(c + 1) * 512].rearrange("p o n -> p (o n)"), start=(half == 0), stop=False)
                pe.wait_ge(kept, 2 * b + 2)
                for c in range(2):
                    to, cols = ps[:, c * 512:(c + 1) * 512], slice(c * 512, (c + 1) * 512)
                    for k in range(2):
                        pe.matmul(to, f[:, k, :], up2[:, k, cols], start=False, stop=False)
                    last = pe.matmul(to, f[0:64, 2, :], up4[:, cols], start=False, stop=True)
                last.then_inc(fused, 1)

        @block.vector
        def _(dve):
            dve.sem_inc(added, 1)

            def fuse_batch(b, further):
                dve.wait_ge(projected, b + 1)
                dve.tensor_copy(f[:, 0:2, :], f_ps[:, 0:2, :]).then_inc(kept, 1)
                dve.tensor_copy(f[0:64, 2, :], f_ps[0:64, 2, :]).then_inc(kept, 1)
                if further:
                    stage_coarse(b + 1)
                dve.wait_ge(fused, b + 1)
                batch = at(m.xc, b)
                dve.scalar_tensor_tensor(out=batch, in0=ps[:], scalar=fb[:, 0:1], in1=batch, op0=ALU.add, op1=ALU.add).then_inc(added, 1)

            def stage_coarse(b):
                for to, src in ((s2, outs[1]), (s4, outs[2])):
                    dve.tensor_copy(to[:], src[:, :, bass.ds(b, 1), :].rearrange("p h o n -> p (h o) n")).then_inc(staged, 1)

            stage_coarse(0)
            with dve.Fori(0, B - 1) as b:
                fuse_batch(b, True)
            fuse_batch(B - 1, False)


def scaled_attention_block(m, ins):
    nc = m.nc
    sizes = (H, H // 2, H // 4)
    with ExitStack() as outer:
        outs = [m.sb(f"scale{i}_out", [P, 2, B, s * s], F32, outer) for i, s in enumerate(sizes)]
        scratch = [HeadScratch(nc, f"scale{i}", s * s) for i, s in enumerate(sizes)]
        with Stage(nc) as ctx:
            padded = [m.sb(f"padded{i}", [P, B, s + 2, s + 2], F32, ctx) for i, s in enumerate(sizes)]
            taps = [m.sb(f"taps{i}", [P, 2, 10], F32, ctx) for i in range(3)]
            tap_loaded = m.sem("tap_loaded", ctx)
            bordered = m.sem("bordered", ctx)
            with nc.Block() as block:
                @block.sync
                def _(sp):
                    for i in range(3):
                        for j, kind in enumerate(("dw", "pos")):
                            sp.dma_start(taps[i][:, j, 0:9], ins[f"L1_conv_{kind}_w"][i].rearrange("c o y x -> c (o y x)")).then_inc(tap_loaded, 16)
                            sp.dma_start(taps[i][:, j, 9:10], ins[f"L1_conv_{kind}_b"][i].rearrange("(c o) -> c o", o=1)).then_inc(tap_loaded, 16)
                    sp.wait_ge(tap_loaded, 12 * 16)

                @block.gpsimd
                def _(pool):
                    pool.memset(padded[0][:], 0.0).then_inc(bordered, 1)
                    pool.wait_ge(bordered, 1)

            inside = lambda b: padded[0][:, b, 1:H + 1, 1:W + 1]
            group_norm(m, "gn1", lambda b: (m.xc[:, b, :].rearrange("p (y x) -> p y x", x=W), inside(b)))
            pool_by_two(m, "pool2", padded[0], H, padded[1])
            pool_by_two(m, "pool4", padded[1], H // 2, padded[2])
            for i, s in enumerate(sizes):
                pw, pb = ins["L1_conv_pw_w"], ins["L1_conv_pw_b"]
                head_inputs(m, f"in{i}", s * s, scratch[i], *(pw[i, :, j * C:(j + 1) * C] for j in range(3)),
                            *(pb[i, j * C:(j + 1) * C] for j in range(3)), padded=padded[i], taps=taps[i])
        for i, s in enumerate(sizes):
            if i == 2:
                wp = [m.sb(f"fuse_w{i}", [P, 2, C], F32, outer) for i in range(3)]
                up2, up4, fb = m.sb("up2", [P, 2, N], F32, outer), m.sb("up4", [64, N], F32, outer), m.sb("fb", [P, 1], F32, outer)
                fusion_w = ins["L1_conv_fusion_w"]
                ahead = Ahead([(up2[:], ins["c_up2"].rearrange("(k p) n -> p k n", p=P)), (up4[:], ins["c_up4"]),
                               (fb[:], ins["L1_conv_fusion_b"].rearrange("(c o) -> c o", o=1))],
                              [(wp[j], fusion_w[j * C:(j + 1) * C, :]) for j in range(3)])
            many_heads_attention(m, f"heads{i}", s * s, scratch[i], outs[i], HD ** -0.5, ahead=ahead if i == 2 else None)
        fuse_scales(m, "fuse", outs, wp, up2, up4, fb)


def hybrid_kernel(nc, ins, out):
    with ExitStack() as ctx:
        m = Machine(nc, ctx, ins)
        make_identities(m)
        group_norm(m, "gn0", lambda b: (m.xc[:, b, :], m.xnT[:, b, :]))
        one_head_attention(m, "attn0", *(ins[f"L0_conv_{x}"] for x in ("Wq", "Wk", "Wv", "bq", "bk", "bv")), 1.0, False)
        scaled_attention_block(m, ins)
        turn_activations(m, "to_tokens")
        token_norm(m, "ln2")
        with ExitStack() as layer:
            routed = Routed(m, layer)
            one_head_attention(m, "attn2", ins["L2_attn_WQ"], ins["L2_attn_WK"], ins["L2_attn_WV"], None, None, None, C ** -0.5, True, routed)
            picks = Picks(m, layer, "pick", 16)
            weights = ExpertWeights(m, layer, 16, 2 * C, ins["L2_ffn_w1"], ins["L2_ffn_w2"], ins["L2_ffn_w3"])
            bias_parts = nc.dram_tensor("bias_parts", [3, HEADS, N], BF16, kind="Internal").ap()
            beside = lambda ctx: edge_bias(m, "edges", ctx, ins["targets"], ins["attributes"], ins["L3_attn_We"], ins["L3_attn_be"], bias_parts)
            with ExitStack() as inputs:
                xn = m.sb("xn3", [P, TILES, C], F32, inputs)
                token_norm(m, "ln3", keep=xn)
                route(m, "route2", 16, ins["L2_ffn_gate_w"], ins["L2_ffn_gate_b"], picks)
                dispatch_tokens(m, "dispatch", picks, routed, xn, weights, beside)
            routed_experts(m, "experts2", 16, weights, routed)
            token_norm(m, "ln4", collected=(picks, routed))
        with ExitStack() as layer:
            heads_out = m.sb("heads_out", [P, 2, B, N], F32, layer)
            scratch = HeadScratch(nc, "edge", N)
            head_inputs(m, "in3", N, scratch, *(ins[f"L3_attn_{x}"] for x in ("Wq", "Wk", "Wv", "bq", "bk", "bv")), k_scale=HD ** -0.5)
            wo, bo = m.sb("wo", [P, 2, C], F32, layer), m.sb("bo", [P, C], F32, layer)
            ahead = Ahead([(bo[:], ins["L3_attn_bo"].rearrange("(o c) -> o c", o=1).broadcast_to((P, C)))], [(wo, ins["L3_attn_Wo"])])
            many_heads_attention(m, "heads3", N, scratch, heads_out, 1.0, bias_parts, ahead)
            output_projection(m, "project", heads_out, wo, bo)
        with ExitStack() as layer:
            combine, combineT = m.sb("combine3", [P, TILES, 8], F32, layer), m.sb("combineT3", [8, TILES // 4, 512], F32, layer)
            xn = m.sb("xn5", [P, TILES, C], F32, layer)
            token_norm(m, "ln5", keep=xn)
            route(m, "route3", 8, ins["L3_ffn_router_w"], None, Picks(m, layer, "pick3", 8), combine, combineT)
            gelu_experts(m, "experts3", 8, ins["L3_ffn_w1"], ins["L3_ffn_b1"], ins["L3_ffn_w2"], ins["L3_ffn_b2"], combine, combineT, xn)
        turn_activations(m, "to_channels", out)


def spreading_matrix(factor):
    import numpy as np

    def line(fine):
        at_ = (np.arange(fine) + 0.5) / factor - 0.5
        weight = np.maximum(0.0, 1.0 - np.abs(at_[None, :] - np.arange(fine // factor)[:, None]))
        return weight / weight.sum(0, keepdims=True)
    return np.kron(line(H), line(W)).astype(np.float32)


def kernel(**inputs):
    import numpy as np
    from concourse import bacc
    from concourse.bass_utils import run_bass_kernel_spmd

    arrays = {name: np.asarray(a) for name, a in inputs.items()}
    for name in ("L0_conv_Wq", "L0_conv_Wk", "L0_conv_Wv", "L2_attn_WQ", "L2_attn_WK", "L2_attn_WV", "L1_conv_fusion_w", "L3_ffn_router_w", "L3_ffn_b1"):
        arrays[name] = arrays[name].T
    arrays["L1_conv_pw_w"] = arrays["L1_conv_pw_w"].transpose(0, 2, 1)
    arrays["targets"] = arrays.pop("L3_attn_edge_index")[1, ::-1]
    arrays["attributes"] = arrays.pop("L3_attn_edge_attr")[::-1]
    arrays["c_group"] = np.kron(np.eye(C // 4), np.full((4, 4), 0.25)).astype(np.float32)
    arrays["c_before"] = np.triu(np.ones((P, P), np.float32), 1)
    arrays["c_tril"] = np.tril(np.ones((P, P), np.float32))
    arrays["c_up2"], arrays["c_up4"] = spreading_matrix(2), spreading_matrix(4)

    nc = bacc.Bacc("TRN2", target_bir_lowering=False, num_devices=1)
    ins = {}
    for name in arrays:
        arrays[name] = np.ascontiguousarray(arrays[name])
        ins[name] = nc.dram_tensor(name, arrays[name].shape, mybir.dt.from_np(arrays[name].dtype), kind="ExternalInput").ap()
    out = nc.dram_tensor("out", (B, C, H, W), F32, kind="ExternalOutput").ap()
    hybrid_kernel(nc, ins, out)
    return run_bass_kernel_spmd(nc, [arrays], core_ids=[0]).results[0]["out"]
```
